# Optimizing a Trainium2 kernel written in Bass

```python
import numpy as np
import jax
import jax.numpy as jnp

def _softmax(x, axis=-1):
    return jax.nn.softmax(x, axis=axis)

def _gelu(x):
    return jax.nn.gelu(x, approximate=True)

def _silu(x):
    return jax.nn.silu(x)

def _sigmoid(x):
    return jax.nn.sigmoid(x)

def _layernorm(x, axis=-1, eps=1e-05):
    m = jnp.mean(x, axis=axis, keepdims=True)
    v = jnp.var(x, axis=axis, keepdims=True)
    return (x - m) / jnp.sqrt(v + eps)

def _scatter_add(tgt, idx, src, axis=0):
    return tgt.at[idx].add(src)

def _segment_sum(src, seg, n):
    return jax.ops.segment_sum(src, seg, n)
kernel_name = 'mk_decoder_postln_d1_seqx_r4_4184de'

def setup_inputs(seed: int=0):
    np.random.seed(seed)
    _w = jnp.asarray

    def _rec_inputs():
        import jax
        import jax.numpy as jnp
        _rk = jax.random.key(seed)
        x = -0.0005207 + 1.001 * jax.random.normal(jax.random.fold_in(_rk, 1), (16, 256, 256), jnp.float32)
        _lenS = 256 - jax.random.randint(jax.random.fold_in(_rk, 7), (16,), 0, max(1, 256 // 4) + 1, jnp.int32)
        _lenS2 = 77 - jax.random.randint(jax.random.fold_in(_rk, 8), (16,), 0, max(1, 77 // 4) + 1, jnp.int32)
        _ctx_1024P = jax.random.normal(jax.random.fold_in(_rk, 11), (16, 16, 256), jnp.float32)
        _ctx_1024c = jax.random.dirichlet(jax.random.fold_in(_rk, 511), 0.3 * jnp.ones((16,), jnp.float32), (16, 77))
        _ctx_1024t = jnp.einsum('bsk,bkd->bsd', _ctx_1024c, _ctx_1024P)
        _ctx_1024t = _ctx_1024t * jax.lax.rsqrt(jnp.mean(jnp.square(_ctx_1024t)) + 1e-12) * 0.953939
        ctx_1024 = -0.000514642 + 1.00011 * (_ctx_1024t + 0.3 * jax.random.normal(jax.random.fold_in(_rk, 611), (16, 77, 256), jnp.float32))
        return (x, ctx_1024)
    x, ctx_1024 = _rec_inputs()

    def _L0_attn_setup():
        import jax, jax.numpy as jnp
        import numpy as np
        B, T, D = (2, 512, 256)
        HEAD_DIM, N_HEADS, N_HH, HEAD_V_DIM, CONV_SIZE = (128, 8, 3, 128, 4)

        def _short_conv(x, w):
            cs = w.shape[-1]
            t = x.shape[1]
            xp = jnp.pad(x, ((0, 0), (cs - 1, 0), (0, 0)))
            y = sum((xp[:, i:i + t, :] * w[:, i] for i in range(cs)))
            return jax.nn.silu(y)

        def _l2norm(x, eps=1e-06):
            return x * jax.lax.rsqrt(jnp.sum(x * x, -1, keepdims=True) + eps)

        def _forward(x, Wq, Wk, Wv, Wb, Wa, A_log, dt_bias, conv_q, conv_k, conv_v, Wg, rms_weight, Wo):
            b, t, _ = x.shape
            h, d, dv, nh = (N_HEADS, HEAD_DIM, HEAD_V_DIM, N_HH)
            q = _short_conv(x @ Wq, conv_q).reshape(b, t, h, d)
            k = _short_conv(x @ Wk, conv_k).reshape(b, t, nh, h, d).transpose(0, 1, 3, 2, 4)
            v = _short_conv(x @ Wv, conv_v).reshape(b, t, nh, h, dv).transpose(0, 1, 3, 2, 4)
            beta = 2.0 * jax.nn.sigmoid(x @ Wb).reshape(b, t, nh, h).transpose(0, 1, 3, 2)
            g = -jnp.exp(A_log) * jax.nn.softplus(x @ Wa + dt_bias)
            q = _l2norm(q) * d ** (-0.5)
            k = _l2norm(k)

            def step(S, inp):
                qt, kt, vt, bt, gt = inp
                S = S * jnp.exp(gt)[..., None, None]
                for i in range(nh):
                    ki, vi, bi = (kt[:, :, i], vt[:, :, i], bt[:, :, i])
                    kS = jnp.einsum('bhd,bhde->bhe', ki, S)
                    S = S + bi[..., None, None] * (ki[..., None] * (vi - kS)[:, :, None, :])
                o = jnp.einsum('bhd,bhde->bhe', qt, S)
                return (S, o)
            xs = tuple((jnp.moveaxis(a, 1, 0) for a in (q, k, v, beta, g)))
            S0 = jnp.zeros((b, h, d, dv), x.dtype)
            _, o = jax.lax.scan(step, S0, xs)
            o = jnp.moveaxis(o, 0, 1)
            gate = (x @ Wg).reshape(b, t, h, dv)
            o = o * jax.lax.rsqrt(jnp.mean(o * o, -1, keepdims=True) + 1e-05) * rms_weight
            o = o * jax.nn.silu(gate)
            return o.reshape(b, t, h * dv) @ Wo
        key = jax.random.key(seed)
        ks = jax.random.split(key, 16)
        h, d, dv, nh, cs = (N_HEADS, HEAD_DIM, HEAD_V_DIM, N_HH, CONV_SIZE)
        f = lambda k, shape, s=0.02: jax.random.normal(k, shape, jnp.float32) * s
        return {'x': f(ks[0], (B, T, D), 1.0), 'cos': f(ks[1], (T, d), 1.0), 'sin': f(ks[2], (T, d), 1.0), 'Wq': f(ks[3], (D, h * d)), 'Wk': f(ks[4], (D, h * d * nh)), 'Wv': f(ks[5], (D, h * dv * nh)), 'Wb': f(ks[6], (D, h * nh)), 'Wa': f(ks[7], (D, h)), 'A_log': jnp.log(jax.random.uniform(ks[8], (h,), jnp.float32, 0.5, 8.0)), 'dt_bias': f(ks[9], (h,), 0.1), 'conv_q': f(ks[10], (h * d, cs), 0.5), 'conv_k': f(ks[11], (h * d * nh, cs), 0.5), 'conv_v': f(ks[12], (h * dv * nh, cs), 0.5), 'Wg': f(ks[13], (D, h * dv)), 'rms_weight': jnp.ones((dv,), jnp.float32), 'Wo': f(ks[14], (h * dv, D))}
    _L0_attn_all = _L0_attn_setup()
    _L0_attn_in = {k: v for k, v in _L0_attn_all.items() if k in ('cos', 'sin', 'Wq', 'Wk', 'Wv', 'Wb', 'Wa', 'A_log', 'dt_bias', 'conv_q', 'conv_k', 'conv_v', 'Wg', 'rms_weight', 'Wo')}
    del _L0_attn_all

    def _L0_xattn_setup():
        import jax, jax.numpy as jnp
        import numpy as np
        import math
        B, S, D, H = (1, 512, 256, 16)
        DK = D // H
        DH = 64
        LOG_T_MIN = math.log(0.1)
        LOG_T_MAX = math.log(10.0)

        def _linear(x, W, b):
            return x @ W.T + b
        key = jax.random.key(seed)
        ks = jax.random.split(key, 20)
        p = 0.02
        return {'query': jax.random.normal(ks[0], (B, S, D), jnp.float32), 'key': jax.random.normal(ks[1], (B, S, D), jnp.float32), 'value': jax.random.normal(ks[2], (B, S, D), jnp.float32), 'Wq': jax.random.normal(ks[3], (D, D), jnp.float32) * p, 'bq': jax.random.normal(ks[4], (D,), jnp.float32) * p, 'Wk': jax.random.normal(ks[5], (D, D), jnp.float32) * p, 'bk': jax.random.normal(ks[6], (D,), jnp.float32) * p, 'Wv': jax.random.normal(ks[7], (D, D), jnp.float32) * p, 'bv': jax.random.normal(ks[8], (D,), jnp.float32) * p, 'Wo': jax.random.normal(ks[9], (D, D), jnp.float32) * p, 'bo': jax.random.normal(ks[10], (D,), jnp.float32) * p, 'w1': jax.random.normal(ks[11], (DH, 3), jnp.float32) * 0.3, 'b1': jax.random.normal(ks[12], (DH,), jnp.float32) * 0.1, 'w2': jax.random.normal(ks[13], (DH, DH), jnp.float32) * 0.1, 'b2': jax.random.normal(ks[14], (DH,), jnp.float32) * 0.1, 'w3': jax.random.normal(ks[15], (1, DH), jnp.float32) * 0.1, 'b3': jnp.full((1,), (LOG_T_MIN + LOG_T_MAX) / 2, jnp.float32)}
    _L0_xattn_all = _L0_xattn_setup()
    _L0_xattn_in = {k: v for k, v in _L0_xattn_all.items() if k in ('Wq', 'bq', 'Wk', 'bk', 'Wv', 'bv', 'Wo', 'bo', 'w1', 'b1', 'w2', 'b2', 'w3', 'b3')}
    del _L0_xattn_all

    def _L0_ffn_setup():
        import jax, jax.numpy as jnp
        import numpy as np
        B, S, D_MODEL, D_FF = (4, 512, 256, 1024)

        def _quantum_transform(hidden, theta, w_real, w_imag):
            imag = w_imag * jnp.sin(theta + hidden * 0.1)
            quantum_phase = jnp.cos(theta) * w_real + jnp.sin(theta) * w_imag
            return hidden + quantum_phase * imag * 0.1
        key = jax.random.key(seed)
        ks = jax.random.split(key, 8)
        return {'x': jax.random.normal(ks[0], (B, S, D_MODEL), dtype=jnp.float32), 'W1': jax.random.normal(ks[1], (D_MODEL, D_FF), dtype=jnp.float32) * (1.0 / np.sqrt(D_MODEL)), 'b1': jnp.zeros((D_FF,), dtype=jnp.float32), 'quantum_phases': jax.random.normal(ks[2], (D_FF,), dtype=jnp.float32) * (2.0 * np.pi), 'quantum_weights_real': jax.random.normal(ks[3], (D_FF,), dtype=jnp.float32) * 0.1, 'quantum_weights_imag': jax.random.normal(ks[4], (D_FF,), dtype=jnp.float32) * 0.1, 'W2': jax.random.normal(ks[5], (D_FF, D_MODEL), dtype=jnp.float32) * (1.0 / np.sqrt(D_FF)), 'b2': jnp.zeros((D_MODEL,), dtype=jnp.float32)}
    _L0_ffn_all = _L0_ffn_setup()
    _L0_ffn_in = {k: v for k, v in _L0_ffn_all.items() if k in ('W1', 'b1', 'quantum_phases', 'quantum_weights_real', 'quantum_weights_imag', 'W2', 'b2')}
    del _L0_ffn_all
    return {'x': x, 'ctx_1024': ctx_1024, 'L0_attn_cos': _L0_attn_in['cos'], 'L0_attn_sin': _L0_attn_in['sin'], 'L0_attn_Wq': _L0_attn_in['Wq'], 'L0_attn_Wk': _L0_attn_in['Wk'], 'L0_attn_Wv': _L0_attn_in['Wv'], 'L0_attn_Wb': _L0_attn_in['Wb'], 'L0_attn_Wa': _L0_attn_in['Wa'], 'L0_attn_A_log': _L0_attn_in['A_log'], 'L0_attn_dt_bias': _L0_attn_in['dt_bias'], 'L0_attn_conv_q': _L0_attn_in['conv_q'], 'L0_attn_conv_k': _L0_attn_in['conv_k'], 'L0_attn_conv_v': _L0_attn_in['conv_v'], 'L0_attn_Wg': _L0_attn_in['Wg'], 'L0_attn_rms_weight': _L0_attn_in['rms_weight'], 'L0_attn_Wo': _L0_attn_in['Wo'], 'L0_xattn_Wq': _L0_xattn_in['Wq'], 'L0_xattn_bq': _L0_xattn_in['bq'], 'L0_xattn_Wk': _L0_xattn_in['Wk'], 'L0_xattn_bk': _L0_xattn_in['bk'], 'L0_xattn_Wv': _L0_xattn_in['Wv'], 'L0_xattn_bv': _L0_xattn_in['bv'], 'L0_xattn_Wo': _L0_xattn_in['Wo'], 'L0_xattn_bo': _L0_xattn_in['bo'], 'L0_xattn_w1': _L0_xattn_in['w1'], 'L0_xattn_b1': _L0_xattn_in['b1'], 'L0_xattn_w2': _L0_xattn_in['w2'], 'L0_xattn_b2': _L0_xattn_in['b2'], 'L0_xattn_w3': _L0_xattn_in['w3'], 'L0_xattn_b3': _L0_xattn_in['b3'], 'L0_ffn_W1': _L0_ffn_in['W1'], 'L0_ffn_b1': _L0_ffn_in['b1'], 'L0_ffn_quantum_phases': _L0_ffn_in['quantum_phases'], 'L0_ffn_quantum_weights_real': _L0_ffn_in['quantum_weights_real'], 'L0_ffn_quantum_weights_imag': _L0_ffn_in['quantum_weights_imag'], 'L0_ffn_W2': _L0_ffn_in['W2'], 'L0_ffn_b2': _L0_ffn_in['b2']}

def reference(x, ctx_1024, L0_attn_cos, L0_attn_sin, L0_attn_Wq, L0_attn_Wk, L0_attn_Wv, L0_attn_Wb, L0_attn_Wa, L0_attn_A_log, L0_attn_dt_bias, L0_attn_conv_q, L0_attn_conv_k, L0_attn_conv_v, L0_attn_Wg, L0_attn_rms_weight, L0_attn_Wo, L0_xattn_Wq, L0_xattn_bq, L0_xattn_Wk, L0_xattn_bk, L0_xattn_Wv, L0_xattn_bv, L0_xattn_Wo, L0_xattn_bo, L0_xattn_w1, L0_xattn_b1, L0_xattn_w2, L0_xattn_b2, L0_xattn_w3, L0_xattn_b3, L0_ffn_W1, L0_ffn_b1, L0_ffn_quantum_phases, L0_ffn_quantum_weights_real, L0_ffn_quantum_weights_imag, L0_ffn_W2, L0_ffn_b2):
    import jax
    import jax.numpy as jnp

    def _L0_attn_ref(x, cos, sin, Wq, Wk, Wv, Wb, Wa, A_log, dt_bias, conv_q, conv_k, conv_v, Wg, rms_weight, Wo):
        import jax, jax.numpy as jnp
        import numpy as np
        B, T, D = (2, 512, 256)
        HEAD_DIM, N_HEADS, N_HH, HEAD_V_DIM, CONV_SIZE = (128, 8, 3, 128, 4)

        def _short_conv(x, w):
            cs = w.shape[-1]
            t = x.shape[1]
            xp = jnp.pad(x, ((0, 0), (cs - 1, 0), (0, 0)))
            y = sum((xp[:, i:i + t, :] * w[:, i] for i in range(cs)))
            return jax.nn.silu(y)

        def _l2norm(x, eps=1e-06):
            return x * jax.lax.rsqrt(jnp.sum(x * x, -1, keepdims=True) + eps)

        def _forward(x, Wq, Wk, Wv, Wb, Wa, A_log, dt_bias, conv_q, conv_k, conv_v, Wg, rms_weight, Wo):
            b, t, _ = x.shape
            h, d, dv, nh = (N_HEADS, HEAD_DIM, HEAD_V_DIM, N_HH)
            q = _short_conv(x @ Wq, conv_q).reshape(b, t, h, d)
            k = _short_conv(x @ Wk, conv_k).reshape(b, t, nh, h, d).transpose(0, 1, 3, 2, 4)
            v = _short_conv(x @ Wv, conv_v).reshape(b, t, nh, h, dv).transpose(0, 1, 3, 2, 4)
            beta = 2.0 * jax.nn.sigmoid(x @ Wb).reshape(b, t, nh, h).transpose(0, 1, 3, 2)
            g = -jnp.exp(A_log) * jax.nn.softplus(x @ Wa + dt_bias)
            q = _l2norm(q) * d ** (-0.5)
            k = _l2norm(k)

            def step(S, inp):
                qt, kt, vt, bt, gt = inp
                S = S * jnp.exp(gt)[..., None, None]
                for i in range(nh):
                    ki, vi, bi = (kt[:, :, i], vt[:, :, i], bt[:, :, i])
                    kS = jnp.einsum('bhd,bhde->bhe', ki, S)
                    S = S + bi[..., None, None] * (ki[..., None] * (vi - kS)[:, :, None, :])
                o = jnp.einsum('bhd,bhde->bhe', qt, S)
                return (S, o)
            xs = tuple((jnp.moveaxis(a, 1, 0) for a in (q, k, v, beta, g)))
            S0 = jnp.zeros((b, h, d, dv), x.dtype)
            _, o = jax.lax.scan(step, S0, xs)
            o = jnp.moveaxis(o, 0, 1)
            gate = (x @ Wg).reshape(b, t, h, dv)
            o = o * jax.lax.rsqrt(jnp.mean(o * o, -1, keepdims=True) + 1e-05) * rms_weight
            o = o * jax.nn.silu(gate)
            return o.reshape(b, t, h * dv) @ Wo
        return _forward(x, Wq, Wk, Wv, Wb, Wa, A_log, dt_bias, conv_q, conv_k, conv_v, Wg, rms_weight, Wo)

    def _L0_xattn_ref(query, key, value, Wq, bq, Wk, bk, Wv, bv, Wo, bo, w1, b1, w2, b2, w3, b3):
        import jax, jax.numpy as jnp
        import numpy as np
        import math
        B, S, D, H = (1, 512, 256, 16)
        DK = D // H
        DH = 64
        LOG_T_MIN = math.log(0.1)
        LOG_T_MAX = math.log(10.0)

        def _linear(x, W, b):
            return x @ W.T + b
        b, sq, d = query.shape
        sk = key.shape[1]
        h, dk = (H, DK)
        Q = _linear(query, Wq, bq).reshape(b, sq, h, dk).transpose(0, 2, 1, 3)
        K = _linear(key, Wk, bk).reshape(b, sk, h, dk).transpose(0, 2, 1, 3)
        V = _linear(value, Wv, bv).reshape(b, sk, h, dk).transpose(0, 2, 1, 3)
        qk = jnp.einsum('bhqd,bhkd->bhqk', Q, K)
        scores = qk / math.sqrt(dk)
        mean_sim = scores.mean(axis=(-2, -1))
        max_sim = scores.max(axis=-1).mean(axis=-1)
        probs = jax.nn.softmax(scores, axis=-1)
        entropy_proxy = jnp.var(probs, axis=-1, ddof=1).mean(axis=-1)
        feats = jnp.stack([mean_sim, max_sim, entropy_proxy], axis=-1)
        hidden = jax.nn.gelu(_linear(feats, w1, b1), approximate=False)
        hidden = jax.nn.gelu(_linear(hidden, w2, b2), approximate=False)
        log_t = jnp.clip(_linear(hidden, w3, b3), LOG_T_MIN, LOG_T_MAX)
        t = jnp.exp(log_t)[..., None]
        attn_scores = qk / (2.0 * t)
        attn = jax.nn.softmax(attn_scores, axis=-1)
        attn = jnp.nan_to_num(attn, nan=0.0)
        out = jnp.einsum('bhqk,bhkd->bhqd', attn, V)
        out = out.transpose(0, 2, 1, 3).reshape(b, sq, d)
        return _linear(out, Wo, bo)

    def _L0_ffn_ref(x, W1, b1, quantum_phases, quantum_weights_real, quantum_weights_imag, W2, b2):
        import jax, jax.numpy as jnp
        import numpy as np
        B, S, D_MODEL, D_FF = (4, 512, 256, 1024)

        def _quantum_transform(hidden, theta, w_real, w_imag):
            imag = w_imag * jnp.sin(theta + hidden * 0.1)
            quantum_phase = jnp.cos(theta) * w_real + jnp.sin(theta) * w_imag
            return hidden + quantum_phase * imag * 0.1
        hidden = jnp.einsum('bsd,df->bsf', x, W1) + b1
        q = _quantum_transform(hidden, quantum_phases, quantum_weights_real, quantum_weights_imag)
        act = jax.nn.relu(q)
        return jnp.einsum('bsf,fd->bsd', act, W2) + b2
    x = _layernorm(x + _L0_attn_ref(x, L0_attn_cos, L0_attn_sin, L0_attn_Wq, L0_attn_Wk, L0_attn_Wv, L0_attn_Wb, L0_attn_Wa, L0_attn_A_log, L0_attn_dt_bias, L0_attn_conv_q, L0_attn_conv_k, L0_attn_conv_v, L0_attn_Wg, L0_attn_rms_weight, L0_attn_Wo), axis=-1)
    x = _layernorm(x + _L0_xattn_ref(x, ctx_1024, ctx_1024, L0_xattn_Wq, L0_xattn_bq, L0_xattn_Wk, L0_xattn_bk, L0_xattn_Wv, L0_xattn_bv, L0_xattn_Wo, L0_xattn_bo, L0_xattn_w1, L0_xattn_b1, L0_xattn_w2, L0_xattn_b2, L0_xattn_w3, L0_xattn_b3), axis=-1)
    x = _layernorm(x + _L0_ffn_ref(x, L0_ffn_W1, L0_ffn_b1, L0_ffn_quantum_phases, L0_ffn_quantum_weights_real, L0_ffn_quantum_weights_imag, L0_ffn_W2, L0_ffn_b2), axis=-1)
    return x

_drawn_inputs = setup_inputs


def setup_inputs(seed=0):
    import zlib

    import numpy as np

    out = dict(_drawn_inputs(seed))
    spreads = {'L0_attn_rms_weight': (1.0, 0.6), 'L0_ffn_b1': (0.0, 0.1), 'L0_ffn_b2': (0.0, 0.1)}
    factors = {'L0_attn_Wb': 6.987,
     'L0_attn_Wa': 8.0,
     'L0_attn_A_log': 2.87,
     'L0_attn_dt_bias': 35.015,
     'L0_xattn_Wq': 8.0,
     'L0_xattn_bq': 8.0,
     'L0_xattn_Wk': 8.0,
     'L0_xattn_bk': 64.0,
     'L0_xattn_bv': 8.0,
     'L0_xattn_bo': 2.728,
     'L0_xattn_w1': 8.0,
     'L0_xattn_b1': 8.0,
     'L0_xattn_w2': 8.0,
     'L0_xattn_b2': 8.0,
     'L0_xattn_w3': 8.0,
     'L0_ffn_quantum_phases': 8.0,
     'L0_ffn_quantum_weights_real': 35.685,
     'L0_ffn_quantum_weights_imag': 8.0}
    for name, (base, spread) in spreads.items():
        noise = np.random.default_rng([zlib.crc32(name.encode()), seed]).standard_normal(out[name].shape)
        drawn = base * np.exp(spread * noise) if base else spread * noise
        out[name] = jnp.asarray(drawn.astype(out[name].dtype))
    for name, factor in factors.items():
        out[name] = (out[name] * factor).astype(out[name].dtype)
    return out
```

```python
from contextlib import ExitStack

import numpy as np
import concourse.bass as bass
from concourse import mybir

F32, F16 = mybir.dt.float32, mybir.dt.float16
ALU, ACT, AX = mybir.AluOpType, mybir.ActivationFunctionType, mybir.AxisListType

P = 128
BATCHES, T, D = 16, 256, 256
TT, KC = T // P, D // P
H, DH, NHH = 8, 128, 3
TOK = 32
CH = T // TOK
L = TOK * NHH
G = H // 2
PARTS = 1 + 1 + 2 * NHH
STREAM = PARTS + 2
CONV = 4
LEVELS = 6
XH, DK, SK = 16, 16, 77
XG = 4
FF = 1024
FT = FF // P
LN_EPS = 1e-5
MAGIC = float(1.5 * 2 ** 23)
RS = 11
TWO_PI = 2 * float(np.pi)
PI_BELOW = 3.1415925
LOG_T_MIN, LOG_T_MAX = float(np.log(0.1)), float(np.log(10.0))


def shape_constants():
    s, m, t = np.arange(L), np.arange(TOK)[:, None], np.arange(TOK)
    tok = s // NHH
    out = {
        "ident": np.eye(P),
        "after": m > tok[None],
        "upto": np.concatenate([m <= tok[None], m <= t[None]], 1),
        "strict": s[:, None] < s[None],
        "causal": tok[:, None] <= t[None],
        "spread": np.concatenate([s[None] == NHH * m + i for i in range(NHH)], 1),
        "ones": np.ones((P, P)),
    }
    return {k: v.astype(np.float32) for k, v in out.items()}


def build(nc, a, out):
    const = shape_constants()
    ctx = ExitStack()
    with ctx:
        def sb(name, shape, dt=F32):
            return ctx.enter_context(nc.sbuf_tensor(name, shape, dt))

        def sem(name):
            return ctx.enter_context(nc.semaphore(name))

        bank = [ctx.enter_context(nc.psum_tensor(f"bank{i}", [P, 512], F32)) for i in range(8)]

        cst = {k: sb(f"c_{k}", list(v.shape)) for k, v in const.items()}
        ident, ones = cst["ident"], cst["ones"]
        ident_h = sb("ident_h", [P, P], F16)
        w_ab = sb("w_ab", [P, KC, 4 * H])
        conv_w = sb("conv_w", [P, (PARTS - 1) * H, CONV])
        w_o = sb("w_o", [P, H, D])
        rms_w = sb("rms_w", [P, 1])
        neg_a = sb("neg_a", [TOK, H])
        dt_b = sb("dt_b", [TOK, H])
        xwq = sb("xwq", [P, KC, XG * P])
        xwk = sb("xwk", [P, KC, XG * P])
        xbq, xbk = sb("xbq", [P, XG]), sb("xbk", [P, XG])
        xwv, xwo = sb("xwv", [P, KC, D]), sb("xwo", [P, KC, D])
        xbv, xbo, fb2 = sb("xbv", [P, D]), sb("xbo", [P, D]), sb("fb2", [P, D])
        tw1, tb1 = sb("tw1", [P, 3, 64]), sb("tb1", [64, 1])
        tw2, tb2 = sb("tw2", [64, P]), sb("tb2", [64, 1])
        tw3, tw3b, tb3 = sb("tw3", [64, 1]), sb("tw3b", [64, P]), sb("tb3", [P, 1])
        fb1 = sb("fb1", [P, FT])
        theta, w_re, w_im = sb("theta", [P, FT]), sb("w_re", [P, FT]), sb("w_im", [P, FT])
        coef, trig, turn = sb("coef", [P, FT]), sb("trig", [P, 2 * FT]), sb("turn", [P, 2 * FT])

        w_part = [sb(f"w_part{i}", [P, KC, H * DH]) for i in range(2)]
        x_tok, xT = sb("x_tok", [P, TT, D]), sb("xT", [P, KC, T])
        fw1, fw2 = w_part[0], w_part[1][:].rearrange("p k (g n) -> p (k g) n", n=D)
        raw_all = sb("raw_all", [P, 2, H, CONV - 1 + T])
        raw = [raw_all[:, i] for i in range(2)]
        co = sb("co", [P, (PARTS - 1) * H, T])
        gate, oT = sb("gate", [P, H, T]), sb("oT", [P, H, T])
        zdec, zabs, gdec = sb("zdec", [TOK, CH, H]), sb("zabs", [TOK, CH, H]), sb("gdec", [TOK, CH, H])
        beta = sb("beta", [TOK, CH, NHH, H])
        e_seg = sb("e_seg", [L, CH * H, TOK])
        e_in = sb("e_in", [P, 2, CH * H])
        e_out = sb("e_out", [L, CH * H])
        beta_s = sb("beta_s", [L, CH * H])

        space = sb("space", [P, 3 * H * P + 4 * H * L])

        def lay(parts, at, rows=P):
            got = []
            for shape in parts:
                n = int(np.prod(shape))
                u = at[0][0:rows, at[1]:at[1] + n]
                at[1] += n
                got.append(u if len(shape) == 1 else u.rearrange("p (a b) -> p a b", b=shape[1]))
            return got

        at = [space, 0]
        KQ, SQ = lay([(H, P)] * 2, at)
        VT, = lay([(H, L)], at)
        DD, = lay([(H, P)], at, L)
        M32, R0, Z = lay([(H, L)] * 3, at, L)
        gtab, = lay([(CH * H, TOK)], [space, 0], TOK)
        X = sb("X", [P, H, P])
        Nh = [sb(f"Nh{i}", [L, H, L], F16) for i in range(2)]
        Mh = [sb(f"Mh{i}", [L, H, L], F16) for i in range(2)]
        Rh = [sb(f"Rh{i}", [L, H, L], F16) for i in range(2)]
        R0h, R0T, Er = sb("R0h", [L, H, L], F16), sb("R0T", [L, H, L], F16), sb("Er", [L, H, L], F16)
        R = sb("R", [P, H, P])
        Vn = sb("Vn", [P, H, P])
        at = [raw_all[:].rearrange("p a h t -> p (a h t)"), 0]
        Wn, Y, S = lay([(H, P)] * 3, at)
        Ks, = lay([(H, P)], at, L)
        ssb, inv, bneg = sb("ssb", [L, H]), sb("inv", [L, H]), sb("bneg", [L, H])
        kend, vnorm = sb("kend", [L, H]), sb("vnorm", [L, H])
        epsq, so, ms = sb("epsq", [P, 2]), sb("so", [P, 2]), sb("ms", [P, 2])
        rs_t, rs_y = sb("rs_t", [P, H]), sb("rs_y", [P, H])
        rstd, On = sb("rstd", [P, 2]), sb("On", [P, 2, P])

        at = [space, 0]
        x1, x1b, x2, x2b, yln, ao = lay([(TT, D)] * 6, at)
        x1T, x2T, aoT = lay([(KC, T)] * 3, at)
        qTx, kTx = lay([(XG, T), (XG, SK)], at)
        x3 = sb("x3", [P, TT, D])
        bst, mv, lnr = sb("bst", [P, TT, 6]), sb("mv", [P, TT, 2]), sb("lnr", [P, TT])
        ctx_sb, ctxT = sb("ctx_sb", [SK, D]), sb("ctxT", [P, KC, SK])
        vx = sb("vx", [SK, D])
        ROWS = TT * XH
        co_flat = co[:].rearrange("p a t -> p (a t)")
        qk = co_flat[:, 0:ROWS * SK].rearrange("p (r k) -> p r k", k=SK)
        ex = co_flat[:, 2560:2560 + ROWS * SK].rearrange("p (r k) -> p r k", k=SK)
        exT = co_flat[0:SK, 5120:5120 + ROWS * P].rearrange("p (r q) -> p r q", q=P)
        e_sq = co_flat[:, 9216:9216 + ROWS * SK].rearrange("p (r k) -> p r k", k=SK)
        hid = co_flat[:, 0:FT * T].rearrange("p (f t) -> p f t", t=T)
        arg = co_flat[:, 2560:2560 + FT * T].rearrange("p (f t) -> p f t", t=T)
        rnd = co_flat[:, 5120:5120 + FT * T].rearrange("p (f t) -> p f t", t=T)
        stat = sb("stat", [P, 3, ROWS])
        s_1, r_1, s_2 = sb("s_1", [P, ROWS]), sb("r_1", [P, ROWS]), sb("s_2", [P, ROWS])
        h1, h2 = sb("h1", [64, XH]), sb("h2", [64, XH])
        lt, inv_t = sb("lt", [P, XH]), sb("inv_t", [P, XH])

        names = """const pad_v x_in ctx_in w_in0 w_in1 setup_p setup_a setup_v
            xT_ps xT ab_ps zdec_v eb_a ab_used gate_v beta_v gtab_p gsum_ps eseg_ps gsum_a beta_s_v eseg_a
            proj_ps raw_a tap_v conv_v
            silu_a sq_a norm_ps norm_v vnorm_v p1_ps kt_ps vt_ps dd_p x_v nh_p xt_ps mh_a m32_a vn_a ks_a
            n2_ps m2_ps rr_ps n_a m_a r_v z_p ar_ps rt_ps rt_a er_v re_ps rf_v
            S_v st_ps wn_v y_ps y_a su_ps o_ps so_a ms_v rstd_v on_a ot_ps oT_v
            ao_ps yln_v bst_v mv_v ve_v lnr_v rs_n_v rs_o_v rs_l_v x1_v x1b_p x1T_ps x1T_a ctxT_ps ctxT_a kx_ps kx_a vx_ps vx_v
            qx_ps qx_a sc_ps qk_a stat_v d_v e1_a esq_p s1_v s2_v r1_v var_v h1_ps h1_a h2_ps h2_a h3_ps
            lt_v it_a it_v d2_v e2_a se_v rinv_v eT_ps eT_v av_ps ao_v aoT_ps aoT_a x2_ps x2_v x2b_p
            x2T_ps x2T_a hid_ps hid_a arg_v rnd_v sin_a q_v act_v x3_ps x3_v stored""".split()
        s = {n: sem(n) for n in names}

        block = ctx.enter_context(nc.Block())

        def ld(eng, dst, src):
            eng.dma_start(dst, src).then_inc(s["const"], 16)

        loads = [(cst[k][:], a["c_" + k]) for k in const] + [
            (w_ab[:], a["w_ab"]), (conv_w[:], a["conv_w"]), (w_o[:], a["w_o"]), (rms_w[:], a["rms_w"]),
            (neg_a[:], a["A_log"].partition_broadcast(TOK)), (dt_b[:], a["dt_bias"].partition_broadcast(TOK)),
            (xwq[:], a["xwq"]), (xwk[:], a["xwk"]), (xbq[:], a["xbq"]), (xbk[:], a["xbk"]),
            (xwv[:], a["xwv"]), (xwo[:], a["xwo"]),
            (xbv[:], a["xbv"].partition_broadcast(P)), (xbo[:], a["xbo"].partition_broadcast(P)),
            (fb2[:], a["fb2"].partition_broadcast(P)), (tw1[:], a["tw1"].partition_broadcast(P)),
            (tb1[:], a["tb1"]), (tw2[:], a["tw2"]), (tb2[:], a["tb2"]), (tw3[:], a["tw3"]),
            (tb3[:], a["tb3"].partition_broadcast(P)), (fb1[:], a["fb1"]),
            (theta[:], a["theta"]), (w_re[:], a["w_re"]), (w_im[:], a["w_im"]),
        ]
        ALL_CONST = 16 * len(loads)
        BANKS = H // 2
        NL = 2 * LEVELS

        @block.sync
        def _(sp):
            for dst, src in loads:
                ld(sp, dst, src)
            with sp.Fori(0, BATCHES) as b:
                sp.wait_ge(s["x1_v"], 2 * b + 2)
                sp.dma_start(x_tok[:], a["x"][bass.ds(b, 1)].rearrange("b (t p) d -> (b p) t d", p=P)).then_inc(s["x_in"], 16)
                sp.wait_ge(s["ctxT_a"], b + 1)
                sp.dma_start(ctx_sb[:], a["ctx"][bass.ds(b, 1)].rearrange("b k d -> (b k) d")).then_inc(s["ctx_in"], 16)
                for n in range(STREAM):
                    if n == 0:
                        sp.wait_ge(s["hid_ps"], 4 * b + 4)
                    elif n == 1:
                        sp.wait_ge(s["x3_ps"], 2 * b + 2)
                    else:
                        sp.wait_ge(s["proj_ps"], PARTS * BANKS * b + BANKS * (n - 2) + BANKS)
                    sp.dma_start(w_part[n % 2][:], a["w_parts"][n]).then_inc(s[f"w_in{n % 2}"], 16)

        @block.gpsimd
        def _(pool):
            pool.memset(Vn[:], 0.0)
            pool.memset(X[:], 0.0)
            pool.memset(R[:], 0.0).then_inc(s["setup_p"], 1)
            pool.wait_ge(s["const"], ALL_CONST)
            pool.wait_ge(s["setup_p"], 1)
            pool.tensor_copy(ident_h[:], ident[:]).then_inc(s["setup_p"], 1)

            eye = ident[0:L, 0:L].unsqueeze(1).to_broadcast([L, G, L])
            with pool.Fori(0, BATCHES) as b:
                pool.wait_ge(s["gate_v"], b + 1)
                pool.tensor_tensor(gtab, gdec[:].rearrange("m c h -> m (c h)").unsqueeze(2).to_broadcast([TOK, CH * H, TOK]),
                                   cst["upto"][:, L:P].unsqueeze(1).to_broadcast([TOK, CH * H, TOK]), ALU.mult).then_inc(s["gtab_p"], 1)
                with pool.Fori(0, CH) as c:
                    it = b * CH + c
                    pool.wait_ge(s["eseg_a"], 4 * b + 4)
                    es = e_seg[:, bass.ds(c * H, H), :]
                    pool.tensor_tensor(DD[:, :, 0:L].rearrange("s h (t i) -> s h t i", i=NHH),
                                       es.unsqueeze(3).to_broadcast([L, H, TOK, NHH]),
                                       cst["strict"][:].rearrange("s (t i) -> s t i", i=NHH).unsqueeze(1).to_broadcast([L, H, TOK, NHH]),
                                       ALU.mult).then_inc(s["dd_p"], 1)
                    pool.tensor_tensor(DD[:, :, L:P], es, cst["causal"][:].unsqueeze(1).to_broadcast([L, H, TOK]),
                                       ALU.mult).then_inc(s["dd_p"], 1)
                    for g in range(2):
                        hs = slice(G * g, G * g + G)
                        pool.wait_ge(s["x_v"], 2 * it + g + 1)
                        pool.tensor_tensor(Rh[0][:, hs, :], X[0:L, hs, 0:L], eye, ALU.add).then_inc(s["nh_p"], 1)
                        pool.tensor_copy(Nh[0][:, hs, :], X[0:L, hs, 0:L]).then_inc(s["nh_p"], 1)
                    for g in range(2):
                        hs = slice(G * g, G * g + G)
                        pool.wait_ge(s["r_v"], NL * it + NL - 2 + g + 1)
                        pool.tensor_tensor(Z[:, hs, :], R0[:, hs, :], eye, ALU.subtract).then_inc(s["z_p"], 1)
                        pool.tensor_copy(R0h[:, hs, :], R0[:, hs, :]).then_inc(s["z_p"], 1)
                for t in range(TT):
                    pool.wait_ge(s["x1_v"], 2 * b + t + 3)
                    pool.tensor_tensor(x1b[:, t, :], x1[:, t, :], xbo[:], ALU.add).then_inc(s["x1b_p"], 1)
                pool.wait_ge(s["e1_a"], b + 1)
                pool.tensor_tensor(e_sq, ex, ex, ALU.mult).then_inc(s["esq_p"], 1)
                for t in range(TT):
                    pool.wait_ge(s["x2_v"], 2 * b + t + 1)
                    pool.tensor_tensor(x2b[:, t, :], x2[:, t, :], fb2[:], ALU.add).then_inc(s["x2b_p"], 1)

        @block.scalar
        def _(act):
            A = act.activation
            act.wait_ge(s["const"], ALL_CONST)
            A(neg_a[:], neg_a[:], ACT.Exp).then_inc(s["setup_a"], 1)
            act.wait_ge(s["setup_v"], 5)
            A(trig[:], turn[:], ACT.Sin).then_inc(s["setup_a"], 1)
            act.copy(ctxT[:, 0, :], ident[:, 0:SK]).then_inc(s["ctxT_a"], 1)
            with act.Fori(0, BATCHES) as b:
                act.wait_ge(s["xT_ps"], b + 1)
                A(xT[:].rearrange("p k t -> p (k t)"), bank[0][:], ACT.Copy).then_inc(s["xT"], 1)
                act.wait_ge(s["ab_ps"], b + 1)
                ab = bank[7][0:TOK, 0:CH * 4 * H].rearrange("m (c k) -> m c k", k=4 * H)
                A(beta[:].rearrange("m c i h -> m c (i h)"), ab[:, :, H:4 * H], ACT.Exp, scale=-1.0).then_inc(s["eb_a"], 1)
                act.wait_ge(s["zdec_v"], 2 * b + 2)
                A(zabs[:], zabs[:], ACT.Exp, scale=-1.0).then_inc(s["eb_a"], 1)
                act.wait_ge(s["eb_a"], 3 * b + 2)
                A(zabs[:], zabs[:], ACT.Ln, bias=1.0).then_inc(s["eb_a"], 1)

                def evacuate(n, e):
                    for q in range(BANKS):
                        act.wait_ge(s["proj_ps"], PARTS * BANKS * b + BANKS * n + q + 1)
                        src = bank[BANKS * e + q][:].rearrange("p (j t) -> p j t", t=T)
                        A(raw[e][:, 2 * q:2 * q + 2, CONV - 1:], src, ACT.Copy).then_inc(s["raw_a"], 1)

                for q in range(BANKS):
                    act.wait_ge(s["proj_ps"], PARTS * BANKS * b + q + 1)
                    A(gate[:, 2 * q:2 * q + 2, :], bank[q][:].rearrange("p (j t) -> p j t", t=T), ACT.Silu).then_inc(s["raw_a"], 1)
                evacuate(1, 1)
                with act.Fori(0, (PARTS - 2) // 2) as pp:
                    for e in range(2):
                        act.wait_ge(s["conv_v"], (PARTS - 1) * b + 2 * pp + e + 1)
                        evacuate(2 * pp + 2 + e, e)

                act.wait_ge(s["gsum_ps"], b + 1)
                A(e_in[:].rearrange("p a c -> p (a c)"), bank[0][:, 0:2 * CH * H], ACT.Exp).then_inc(s["gsum_a"], 1)
                A(e_out[:], bank[0][0:L, 2 * CH * H:3 * CH * H], ACT.Exp).then_inc(s["gsum_a"], 1)
                for q in range(4):
                    act.wait_ge(s["eseg_ps"], 4 * b + q + 1)
                    A(e_seg[:, 16 * q:16 * q + 16, :].rearrange("s c t -> s (c t)"), bank[1 + q][0:L, :], ACT.Exp).then_inc(s["eseg_a"], 1)
                act.wait_ge(s["conv_v"], (PARTS - 1) * b + PARTS)

                with act.Fori(0, CH) as c:
                    it = b * CH + c
                    tk = bass.ds(c * TOK, TOK)
                    A(KQ[:, :, L:P], co[:, 0:H, tk], ACT.Silu).then_inc(s["silu_a"], 1)
                    for i in range(NHH):
                        A(KQ[:, :, 0:L].rearrange("p h (t i) -> p h t i", i=NHH)[:, :, :, i], co[:, H + H * i:2 * H + H * i, tk],
                          ACT.Silu).then_inc(s["silu_a"], 1)
                    act.wait_ge(s["silu_a"], 7 * it + 4)
                    A(SQ, KQ, ACT.Square).then_inc(s["sq_a"], 1)
                    for i in range(NHH):
                        A(VT.rearrange("p h (t i) -> p h t i", i=NHH)[:, :, :, i], co[:, H * (4 + i):H * (5 + i), tk],
                          ACT.Silu).then_inc(s["silu_a"], 1)
                    act.wait_ge(s["norm_v"], 5 * it + 5)
                    act.wait_ge(s["vnorm_v"], it + 1)
                    for g in range(2):
                        act.wait_ge(s["vt_ps"], 2 * it + g + 1)
                        for j in range(G):
                            h = G * g + j
                            ins = A(Vn[0:L, h, :], bank[2 + 3 * g][0:L, P * j:P * j + P], ACT.Copy, scale=vnorm[:, h:h + 1])
                        ins.then_inc(s["vn_a"], 1)
                        act.wait_ge(s["kt_ps"], 2 * it + g + 1)
                        for j in range(G):
                            h = G * g + j
                            ins = A(Ks[:, h, :], bank[1 + 3 * g][0:L, P * j:P * j + P], ACT.Copy, scale=kend[:, h:h + 1])
                        ins.then_inc(s["ks_a"], 1)
                    for g in range(2):
                        hs = slice(G * g, G * g + G)
                        act.wait_ge(s["xt_ps"], 2 * it + g + 1)
                        src = bank[6 + g][0:L, 0:G * L].rearrange("r (h s) -> r h s", s=L)
                        A(Mh[0][:, hs, :], src, ACT.Copy).then_inc(s["mh_a"], 1)
                        A(M32[:, hs, :], src, ACT.Copy).then_inc(s["m32_a"], 1)
                    for lv in range(LEVELS):
                        for g in range(2):
                            hs = slice(G * g, G * g + G)
                            if lv < LEVELS - 1:
                                act.wait_ge(s["n2_ps"], (NL - 2) * it + 2 * lv + g + 1)
                                A(Nh[(lv + 1) % 2][:, hs, :], bank[3 * g][0:L, 0:G * L].rearrange("r (h s) -> r h s", s=L),
                                  ACT.Copy).then_inc(s["n_a"], 1)
                            act.wait_ge(s["m2_ps"], NL * it + 2 * lv + g + 1)
                            A(Mh[(lv + 1) % 2][:, hs, :], bank[3 * g + 2][0:L, 0:G * L].rearrange("r (h s) -> r h s", s=L),
                              ACT.Copy).then_inc(s["m_a"], 1)
                    for g in range(2):
                        act.wait_ge(s["rt_ps"], 2 * it + g + 1)
                        A(R0T[:, G * g:G * g + G, :], bank[3 * g + 2].bitcast(F16)[0:L, 0:G * L].rearrange("r (h s) -> r h s", s=L),
                          ACT.Copy).then_inc(s["rt_a"], 1)
                    for g in range(2):
                        act.wait_ge(s["y_ps"], 2 * it + g + 1)
                        A(Y[:, G * g:G * g + G, :].rearrange("p h d -> p (h d)"), bank[3 * g][:], ACT.Copy).then_inc(s["y_a"], 1)
                    act.wait_ge(s["o_ps"], it + 1)
                    for j in range(2):
                        A(On[:, j, :], bank[1][:, P * j:P * j + P], ACT.Square, accum_out=so[:, j:j + 1]).then_inc(s["so_a"], 1)
                    act.wait_ge(s["rstd_v"], it + 1)
                    act.wait_ge(s["so_a"], 2 * it + 2)
                    for j in range(2):
                        A(On[:, j, :], bank[1][:, P * j:P * j + P], ACT.Copy, scale=rstd[:, j:j + 1]).then_inc(s["on_a"], 1)

                act.wait_ge(s["ctxT_ps"], b + 1)
                A(ctxT[:].rearrange("p k c -> p (k c)"), bank[2][:, 0:KC * SK], ACT.Copy).then_inc(s["ctxT_a"], 1)
                act.wait_ge(s["kx_ps"], b + 1)
                for g in range(XG):
                    ins = A(kTx[:, g, :], bank[3][:, SK * g:SK * g + SK], ACT.Identity, bias=xbk[:, g:g + 1])
                ins.then_inc(s["kx_a"], 1)
                act.wait_ge(s["x1T_ps"], b + 1)
                A(x1T.rearrange("p k t -> p (k t)"), bank[0][:], ACT.Copy).then_inc(s["x1T_a"], 1)
                for q in range(2):
                    act.wait_ge(s["qx_ps"], 2 * b + q + 1)
                    for j in range(2):
                        ins = A(qTx[:, 2 * q + j, :], bank[6 + q][:, T * j:T * j + T], ACT.Identity, bias=xbq[:, 2 * q + j:2 * q + j + 1])
                    ins.then_inc(s["qx_a"], 1)
                for q in range(8):
                    act.wait_ge(s["sc_ps"], 8 * b + q + 1)
                    A(qk[:, XG * q:XG * q + XG, :].rearrange("p r k -> p (r k)"), bank[q][:, 0:XG * SK], ACT.Copy).then_inc(s["qk_a"], 1)
                act.wait_ge(s["d_v"], b + 1)
                A(ex, qk, ACT.Exp, scale=DK ** -0.5).then_inc(s["e1_a"], 1)
                act.wait_ge(s["h1_ps"], b + 1)
                A(h1[:], bank[0][0:64, 0:XH], ACT.Gelu, bias=tb1[:]).then_inc(s["h1_a"], 1)
                act.wait_ge(s["h2_ps"], b + 1)
                A(h2[:], bank[1][0:64, 0:XH], ACT.Gelu, bias=tb2[:]).then_inc(s["h2_a"], 1)
                act.wait_ge(s["lt_v"], 2 * b + 2)
                A(inv_t[:], lt[:], ACT.Exp, scale=-1.0).then_inc(s["it_a"], 1)
                act.wait_ge(s["d2_v"], b + 1)
                A(ex, qk, ACT.Exp).then_inc(s["e2_a"], 1)
                act.wait_ge(s["aoT_ps"], b + 1)
                A(aoT.rearrange("p k t -> p (k t)"), bank[1][:], ACT.Copy).then_inc(s["aoT_a"], 1)

                act.wait_ge(s["x2T_ps"], b + 1)
                A(x2T.rearrange("p k t -> p (k t)"), bank[4][:], ACT.Copy).then_inc(s["x2T_a"], 1)
                for q, bk in enumerate((0, 1, 6, 7)):
                    act.wait_ge(s["hid_ps"], 4 * b + q + 5)
                    for j in range(2):
                        f = 2 * q + j
                        ins = A(hid[:, f, :], bank[bk][:, T * j:T * j + T], ACT.Identity, bias=fb1[:, f:f + 1])
                    ins.then_inc(s["hid_a"], 1)
                act.wait_ge(s["rnd_v"], 4 * b + 4)
                A(rnd, arg, ACT.Sin).then_inc(s["sin_a"], 1)
                act.wait_ge(s["x3_v"], 2 * b + 4)
                act.dma_start(out[bass.ds(b, 1)].rearrange("b (t p) d -> (b p) t d", p=P), x3[:]).then_inc(s["stored"], 16)
                act.wait_ge(s["stored"], 16 * b + 16)

        @block.tensor
        def _(pe):
            MM = pe.matmul
            pe.wait_ge(s["const"], ALL_CONST)
            pe.wait_ge(s["setup_p"], 2)
            for q in range(4):
                MM(bank[0][:, 0:P], ident[:], ident[:], start=True, stop=True).then_inc(s["hid_ps"], 1)
            for q in range(2):
                MM(bank[0][:, 0:P], ident[:], ident[:], start=True, stop=True).then_inc(s["x3_ps"], 1)
            with pe.Fori(0, BATCHES) as b:
                pe.wait_ge(s["x3_v"], 2 * b + 2)
                pe.wait_ge(s["x_in"], 16 * b + 16)
                for k in range(KC):
                    for t in range(TT):
                        ins = pe.transpose(bank[0][:, T * k + P * t:T * k + P * t + P], x_tok[:, t, P * k:P * k + P], ident[:])
                ins.then_inc(s["xT_ps"], 1)
                pe.wait_ge(s["xT"], b + 1)
                for c in range(CH):
                    for k in range(KC):
                        ins = MM(bank[7][0:TOK, 4 * H * c:4 * H * (c + 1)], xT[:, k, TOK * c:TOK * c + TOK], w_ab[:, k, :],
                                 start=(k == 0), stop=(k == KC - 1))
                ins.then_inc(s["ab_ps"], 1)

                def project(n, e, wsem_value):
                    pe.wait_ge(s[f"w_in{e}"], wsem_value)
                    for q in range(BANKS):
                        if not isinstance(n, int) or n >= 2:
                            pe.wait_ge(s["raw_a"], PARTS * BANKS * b + BANKS * (n - 2) + q + 1)
                        for j in range(2):
                            o = DH * (2 * q + j)
                            for k in range(KC):
                                ins = MM(bank[BANKS * e + q][:, T * j:T * j + T], w_part[e][:, k, o:o + DH], xT[:, k, :],
                                         start=(k == 0), stop=(k == KC - 1))
                        ins.then_inc(s["proj_ps"], 1)

                project(0, 0, 16 * (STREAM // 2) * b + 16)
                pe.wait_ge(s["ab_used"], b + 1)
                pe.wait_ge(s["eb_a"], 3 * b + 1)
                project(1, 1, 16 * (STREAM // 2) * b + 16)
                with pe.Fori(0, (PARTS - 2) // 2) as pp:
                    for e in range(2):
                        project(2 * pp + 2 + e, e, 16 * (STREAM // 2) * b + 16 * pp + 32)

                pe.wait_ge(s["raw_a"], PARTS * BANKS * b + PARTS * BANKS)
                pe.wait_ge(s["gate_v"], b + 1)
                pe.wait_ge(s["beta_v"], 2 * b + 2)
                gflat = gdec[:].rearrange("m c h -> m (c h)")
                NCH = CH * H
                MM(bank[0][:, 0:NCH], cst["upto"][:], gflat, start=True, stop=True)
                MM(bank[0][:, NCH:2 * NCH], ones[0:TOK, :], gflat, start=True, stop=True)
                MM(bank[0][0:L, 2 * NCH:3 * NCH], cst["after"][:], gflat, start=True, stop=True).then_inc(s["gsum_ps"], 1)
                for i in range(NHH):
                    ins = MM(bank[5][0:L, 0:NCH], cst["spread"][:, L * i:L * i + L], beta[:, :, i, :], start=(i == 0), stop=(i == NHH - 1))
                ins.then_inc(s["norm_ps"], 1)
                pe.wait_ge(s["gtab_p"], b + 1)
                for q in range(4):
                    MM(bank[1 + q][0:L, :], cst["after"][:], gtab[:, 16 * q:16 * q + 16, :], start=True, stop=True).then_inc(s["eseg_ps"], 1)
                with pe.Fori(0, CH) as c:
                    it = b * CH + c
                    pe.wait_ge(s["beta_s_v"], b + 1)
                    pe.wait_ge(s["sq_a"], it + 1)
                    for h in range(H):
                        MM(bank[0][:, h:h + 1], SQ[:, h, :], ones[:, 0:1], start=True, stop=True)
                    for h in range(H):
                        o = TOK * (h % G)
                        ins = MM(bank[0][o:o + TOK, H + h // G:H + h // G + 1], SQ[:, h, L:P], ones[:, 0:1], start=True, stop=True)
                    ins.then_inc(s["norm_ps"], 1)
                    for g in range(2):
                        for j in range(G):
                            h = G * g + j
                            ins = MM(bank[6 + g][0:L, P * j:P * j + P], KQ[:, h, 0:L], KQ[:, h, :], start=True, stop=True)
                        ins.then_inc(s["p1_ps"], 1)
                    pe.wait_ge(s["silu_a"], 7 * it + 7)
                    pe.wait_ge(s["oT_v"], it + 1)
                    for g in range(2):
                        for j in range(G):
                            ins = pe.transpose(bank[2 + 3 * g][0:L, P * j:P * j + P], VT[:, G * g + j, :], ident[:])
                        ins.then_inc(s["vt_ps"], 1)
                        for j in range(G):
                            ins = pe.transpose(bank[1 + 3 * g][0:L, P * j:P * j + P], KQ[:, G * g + j, 0:L], ident[:])
                        ins.then_inc(s["kt_ps"], 1)
                    for g in range(2):
                        pe.wait_ge(s["x_v"], 2 * it + g + 1)
                        for j in range(G):
                            ins = pe.transpose(bank[6 + g][0:L, L * j:L * j + L], X[0:L, G * g + j, 0:L], ident[0:L, 0:L])
                        ins.then_inc(s["xt_ps"], 1)
                    for lv in range(LEVELS + 1):
                        cur = lv % 2
                        for g in range(2):
                            if lv == 0:
                                pe.wait_ge(s["mh_a"], 2 * it + g + 1)
                                pe.wait_ge(s["nh_p"], 4 * it + 2 * g + 2)
                                pe.wait_ge(s["vn_a"], 2 * it + g + 1)
                            else:
                                pe.wait_ge(s["m_a"], NL * it + 2 * (lv - 1) + g + 1)
                            if 1 <= lv < LEVELS:
                                pe.wait_ge(s["n_a"], (NL - 2) * it + 2 * (lv - 1) + g + 1)
                            if lv < LEVELS:
                                if lv < LEVELS - 1:
                                    for j in range(G):
                                        ins = MM(bank[3 * g][0:L, L * j:L * j + L], Mh[cur][:, G * g + j, :], Nh[cur][:, G * g + j, :], start=True, stop=True)
                                    ins.then_inc(s["n2_ps"], 1)
                                for j in range(G):
                                    ins = MM(bank[3 * g + 2][0:L, L * j:L * j + L], Nh[cur][:, G * g + j, :], Mh[cur][:, G * g + j, :], start=True, stop=True)
                                ins.then_inc(s["m2_ps"], 1)
                            if lv >= 1:
                                if lv == 1:
                                    pe.wait_ge(s["ks_a"], 2 * it + g + 1)
                                else:
                                    pe.wait_ge(s["r_v"], NL * it + 2 * (lv - 2) + g + 1)
                                for j in range(G):
                                    ins = MM(bank[3 * g + 1][0:L, L * j:L * j + L], Mh[cur][:, G * g + j, :], Rh[1 - cur][:, G * g + j, :], start=True, stop=True)
                                ins.then_inc(s["rr_ps"], 1)
                    for g in range(2):
                        pe.wait_ge(s["r_v"], NL * it + NL - 2 + g + 1)
                        pe.wait_ge(s["m32_a"], 2 * it + g + 1)
                        for j in range(G):
                            ins = MM(bank[3 * g][0:L, L * j:L * j + L], M32[:, G * g + j, :], R0[:, G * g + j, :], start=True, stop=True)
                        ins.then_inc(s["ar_ps"], 1)
                    for g in range(2):
                        pe.wait_ge(s["z_p"], 4 * it + 2 * g + 2)
                        for j in range(G):
                            ins = pe.transpose(bank[3 * g + 2].bitcast(F16)[0:L, L * j:L * j + L], R0h[:, G * g + j, :], ident_h[0:L, 0:L])
                        ins.then_inc(s["rt_ps"], 1)
                    for g in range(2):
                        pe.wait_ge(s["er_v"], 2 * it + g + 1)
                        pe.wait_ge(s["rt_a"], 2 * it + g + 1)
                        for j in range(G):
                            ins = MM(bank[3 * g + 1][0:L, L * j:L * j + L], R0T[:, G * g + j, :], Er[:, G * g + j, :], start=True, stop=True)
                        ins.then_inc(s["re_ps"], 1)
                    for g in range(2):
                        pe.wait_ge(s["S_v"], (2 * CH + 2) * b + 2 * c + g + 1)
                        for j in range(G):
                            h = G * g + j
                            ins = MM(bank[6 + g][:, P * j:P * j + P], KQ[:, h, :], S[:, h, :], start=True, stop=True)
                        ins.then_inc(s["st_ps"], 1)
                    for g in range(2):
                        pe.wait_ge(s["wn_v"], 2 * it + g + 1)
                        pe.wait_ge(s["rf_v"], 2 * it + g + 1)
                        for j in range(G):
                            h = G * g + j
                            ins = MM(bank[3 * g][:, P * j:P * j + P], R[:, h, :], Wn[:, h, :], start=True, stop=True)
                        ins.then_inc(s["y_ps"], 1)
                    for g in range(2):
                        pe.wait_ge(s["y_a"], 2 * it + g + 1)
                        for j in range(G):
                            h = G * g + j
                            ins = MM(bank[3 * g + 2][:, P * j:P * j + P], Ks[:, h, :], Y[0:L, h, :], start=True, stop=True)
                        ins.then_inc(s["su_ps"], 1)
                    for h in range(H):
                        o = TOK * (h % G)
                        ins = MM(bank[1][o:o + TOK, P * (h // G):P * (h // G) + P], X[:, h, L:P], Y[:, h, :], start=True, stop=True)
                    ins.then_inc(s["o_ps"], 1)
                    pe.wait_ge(s["on_a"], 2 * it + 2)
                    for j in range(2):
                        ins = pe.transpose(bank[4][:, P * j:P * j + P], On[:, j, :], ident[:])
                    ins.then_inc(s["ot_ps"], 1)

                pe.wait_ge(s["oT_v"], CH * b + CH + 1)
                for t in range(TT):
                    for h in range(H):
                        ins = MM(bank[6 + t][:, 0:D], oT[:, h, P * t:P * t + P], w_o[:, h, :], start=(h == 0), stop=(h == H - 1))
                    ins.then_inc(s["ao_ps"], 1)

                pe.wait_ge(s["ctx_in"], 16 * b + 16)
                for k in range(KC):
                    ins = pe.transpose(bank[2][:, SK * k:SK * k + SK], ctx_sb[:, P * k:P * k + P], ident[0:SK, 0:SK])
                ins.then_inc(s["ctxT_ps"], 1)
                pe.wait_ge(s["ctxT_a"], b + 2)
                for g in range(XG):
                    for k in range(KC):
                        ins = MM(bank[3][:, SK * g:SK * g + SK], xwk[:, k, P * g:P * g + P], ctxT[:, k, :], start=(k == 0), stop=(k == KC - 1))
                ins.then_inc(s["kx_ps"], 1)
                for k in range(KC):
                    ins = MM(bank[5][0:SK, 0:D], ctxT[:, k, :], xwv[:, k, :], start=(k == 0), stop=(k == KC - 1))
                ins.then_inc(s["vx_ps"], 1)
                pe.wait_ge(s["x1_v"], 2 * b + 4)
                for k in range(KC):
                    for t in range(TT):
                        ins = pe.transpose(bank[0][:, T * k + P * t:T * k + P * t + P], x1[:, t, P * k:P * k + P], ident[:])
                ins.then_inc(s["x1T_ps"], 1)
                pe.wait_ge(s["x1T_a"], b + 1)
                for q in range(2):
                    for j in range(2):
                        g = 2 * q + j
                        for k in range(KC):
                            ins = MM(bank[6 + q][:, T * j:T * j + T], xwq[:, k, P * g:P * g + P], x1T[:, k, :], start=(k == 0), stop=(k == KC - 1))
                    ins.then_inc(s["qx_ps"], 1)
                pe.wait_ge(s["kx_a"], b + 1)
                pe.wait_ge(s["vx_v"], b + 1)
                pe.wait_ge(s["qx_a"], 2 * b + 2)
                for t in range(TT):
                    for g in range(XG):
                        for j in range(XG):
                            r = slice(32 * j, 32 * j + 32)
                            ins = MM(bank[XG * t + j][:, SK * g:SK * g + SK], qTx[r, g, P * t:P * t + P], kTx[r, g, :], start=True, stop=True)
                            if g == XG - 1:
                                ins.then_inc(s["sc_ps"], 1)
                pe.wait_ge(s["qk_a"], 8 * b + 8)
                pe.wait_ge(s["var_v"], 3 * b + 3)
                for f in range(3):
                    for t in range(TT):
                        ins = MM(bank[0][0:64, 0:XH], tw1[:, f, :], stat[:, f, XH * t:XH * t + XH], start=(f + t == 0), stop=(f == 2 and t == TT - 1))
                ins.then_inc(s["h1_ps"], 1)
                pe.wait_ge(s["h1_a"], b + 1)
                MM(bank[1][:, 0:XH], tw2[:], h1[:], start=True, stop=True).then_inc(s["h2_ps"], 1)
                pe.wait_ge(s["h2_a"], b + 1)
                MM(bank[2][:, 0:XH], tw3b[:], h2[:], start=True, stop=True).then_inc(s["h3_ps"], 1)
                pe.wait_ge(s["e2_a"], b + 1)
                for q in range(8):
                    for j in range(XG):
                        ins = pe.transpose(bank[q][0:SK, P * j:P * j + P], ex[:, XG * q + j, :], ident[:])
                    ins.then_inc(s["eT_ps"], 1)
                for t in range(TT):
                    pe.wait_ge(s["eT_v"], 8 * b + XG * t + XG)
                    for h in range(XH):
                        ins = MM(bank[XG * t][:, DK * h:DK * h + DK], exT[:, XH * t + h, :], vx[:, DK * h:DK * h + DK], start=True, stop=True)
                    ins.then_inc(s["av_ps"], 1)
                pe.wait_ge(s["ao_v"], 2 * b + 2)
                for k in range(KC):
                    for t in range(TT):
                        ins = pe.transpose(bank[1][:, T * k + P * t:T * k + P * t + P], ao[:, t, P * k:P * k + P], ident[:])
                ins.then_inc(s["aoT_ps"], 1)
                pe.wait_ge(s["aoT_a"], b + 1)
                for t in range(TT):
                    for k in range(KC):
                        ins = MM(bank[2 + t][:, 0:D], aoT[:, k, P * t:P * t + P], xwo[:, k, :], start=(k == 0), stop=(k == KC - 1))
                    ins.then_inc(s["x2_ps"], 1)

                pe.wait_ge(s["x2_v"], 2 * b + 2)
                for k in range(KC):
                    for t in range(TT):
                        ins = pe.transpose(bank[4][:, T * k + P * t:T * k + P * t + P], x2[:, t, P * k:P * k + P], ident[:])
                ins.then_inc(s["x2T_ps"], 1)
                pe.wait_ge(s["x2T_a"], b + 1)
                pe.wait_ge(s["w_in0"], 16 * (STREAM // 2) * (b + 1))
                for q, bk in enumerate((0, 1, 6, 7)):
                    for j in range(2):
                        f = 2 * q + j
                        for k in range(KC):
                            ins = MM(bank[bk][:, T * j:T * j + T], fw1[:, k, P * f:P * f + P], x2T[:, k, :], start=(k == 0), stop=(k == KC - 1))
                    ins.then_inc(s["hid_ps"], 1)
                pe.wait_ge(s["act_v"], b + 1)
                pe.wait_ge(s["w_in1"], 16 * (STREAM // 2) * (b + 1))
                for t in range(TT):
                    for f in range(FT):
                        ins = MM(bank[2 + t][:, 0:D], arg[:, f, P * t:P * t + P], fw2[:, f, :], start=(f == 0), stop=(f == FT - 1))
                    ins.then_inc(s["x3_ps"], 1)

        @block.vector
        def _(v):
            v.memset(x1[:, 0, :], 0.0).then_inc(s["x1_v"], 1)
            v.memset(x1[:, 1, :], 0.0).then_inc(s["x1_v"], 1)
            v.memset(x3[:, 0, :], 0.0).then_inc(s["x3_v"], 1)
            v.memset(x3[:, 1, :], 0.0).then_inc(s["x3_v"], 1)
            v.memset(oT[:, 0, :], 0.0).then_inc(s["oT_v"], 1)
            v.memset(co[:, 0, :], 0.0).then_inc(s["conv_v"], 1)
            v.wait_ge(s["const"], ALL_CONST)

            def turns_off(x, y, sem_, at, add=0.0):
                v.tensor_scalar(y, x, 1 / TWO_PI, MAGIC, ALU.mult, ALU.add).then_inc(sem_, 1)
                v.wait_ge(sem_, at + 1)
                v.tensor_scalar(y, y, MAGIC, -TWO_PI, ALU.subtract, ALU.mult).then_inc(sem_, 1)
                v.wait_ge(sem_, at + 2)
                v.tensor_tensor(x, x, y, ALU.add).then_inc(sem_, 1)
                v.wait_ge(sem_, at + 3)
                v.tensor_scalar(x, x, PI_BELOW, -PI_BELOW, ALU.min, ALU.max).then_inc(sem_, 1)

            def rsqrt(x, y, tmp, sem_, at):
                I32 = mybir.dt.int32
                steps = [lambda: v.tensor_scalar(y.bitcast(I32), x.bitcast(I32), 1, None, ALU.logical_shift_right),
                         lambda: v.tensor_scalar(y.bitcast(I32), y.bitcast(I32), -1.0, float(0x5F3759DF), ALU.mult, ALU.add)]
                steps += [lambda: v.tensor_tensor(tmp, y, y, ALU.mult),
                          lambda: v.scalar_tensor_tensor(tmp, tmp, -0.5, x, ALU.mult, ALU.mult),
                          lambda: v.scalar_tensor_tensor(y, tmp, 1.5, y, ALU.add, ALU.mult)] * 3
                assert len(steps) == RS
                for k, one in enumerate(steps):
                    if k:
                        v.wait_ge(sem_, at + k)
                    one().then_inc(sem_, 1)
                v.wait_ge(sem_, at + RS)

            v.tensor_copy(turn[:, 0:FT], theta[:])
            v.tensor_scalar(turn[:, FT:2 * FT], theta[:], float(np.pi / 2), None, ALU.add).then_inc(s["setup_v"], 1)
            v.wait_ge(s["setup_v"], 1)
            turns_off(turn[:], trig[:], s["setup_v"], 1)
            for f, m in enumerate((DK ** -0.5 / (T * SK), DK ** -0.5 / T, 1.0 / T)):
                v.tensor_scalar(tw1[:, f, :], tw1[:, f, :], m, None, ALU.mult)
            v.tensor_copy(tw3b[:], tw3[:].to_broadcast([64, P]))
            v.wait_ge(s["setup_a"], 2)
            v.tensor_scalar(neg_a[:], neg_a[:], -1.0, None, ALU.mult).then_inc(s["setup_v"], 1)
            v.tensor_tensor(turn[:, 0:FT], trig[:, FT:2 * FT], w_re[:], ALU.mult).then_inc(s["setup_v"], 1)
            v.tensor_tensor(turn[:, FT:2 * FT], trig[:, 0:FT], w_im[:], ALU.mult).then_inc(s["setup_v"], 1)
            v.wait_ge(s["setup_v"], 8)
            v.tensor_tensor(turn[:, 0:FT], turn[:, 0:FT], turn[:, FT:2 * FT], ALU.add).then_inc(s["setup_v"], 1)
            v.wait_ge(s["setup_v"], 9)
            v.scalar_tensor_tensor(coef[:], turn[:, 0:FT], 0.1, w_im[:], ALU.mult, ALU.mult).then_inc(s["setup_v"], 1)
            v.wait_ge(s["setup_v"], 10)
            v.wait_ge(s["setup_p"], 2)
            v.tensor_copy(X[L:P, :, L:P], ident[L:P, L:P].unsqueeze(1).to_broadcast([TOK, H, TOK]))
            v.tensor_copy(R[L:P, :, L:P], ident[L:P, L:P].unsqueeze(1).to_broadcast([TOK, H, TOK]))

            with v.Fori(0, BATCHES) as b:
                v.wait_ge(s["ab_ps"], b + 1)
                v.wait_ge(s["eb_a"], 3 * b + 1)
                ab = bank[7][0:TOK, 0:CH * 4 * H].rearrange("m (c k) -> m c k", k=4 * H)
                v.tensor_tensor(zdec[:], ab[:, :, 0:H], dt_b[:].unsqueeze(1).to_broadcast([TOK, CH, H]), ALU.add).then_inc(s["zdec_v"], 1)
                v.wait_ge(s["zdec_v"], 2 * b + 1)
                v.scalar_tensor_tensor(zabs[:], zdec[:], -1.0, zdec[:], ALU.mult, ALU.max).then_inc(s["zdec_v"], 1)
                v.tensor_scalar(beta[:], beta[:], 1.0, 0.5, ALU.add, ALU.mult).then_inc(s["ab_used"], 1)
                v.wait_ge(s["ab_used"], b + 1)
                v.reciprocal(beta[:], beta[:]).then_inc(s["beta_v"], 1)
                v.wait_ge(s["eb_a"], 3 * b + 3)
                v.scalar_tensor_tensor(gdec[:], zdec[:], 0.0, zabs[:], ALU.max, ALU.add).then_inc(s["beta_v"], 1)
                v.wait_ge(s["beta_v"], 2 * b + 2)
                v.tensor_tensor(gdec[:], gdec[:], neg_a[:].unsqueeze(1).to_broadcast([TOK, CH, H]), ALU.mult).then_inc(s["gate_v"], 1)

                def conv(n, e):
                    v.wait_ge(s["raw_a"], PARTS * BANKS * b + BANKS * n + BANKS)
                    for i in range(CONV):
                        for j in range(H):
                            tile = (n - 1) * H + j
                            o = co[:, tile, :] if isinstance(tile, int) else co[:, bass.ds(tile, 1), :].rearrange("p o t -> p (o t)")
                            w = conv_w[:, tile, i:i + 1] if isinstance(tile, int) else conv_w[:, bass.ds(tile, 1), i:i + 1].rearrange("p o t -> p (o t)")
                            src = raw[e][:, j, i:i + T]
                            if i == 0:
                                ins = v.tensor_scalar(o, src, w, None, ALU.mult)
                            else:
                                v.wait_ge(s["tap_v"], CONV * H * (PARTS - 1) * b + CONV * H * (n - 1) + H * (i - 1) + j + 1)
                                ins = v.scalar_tensor_tensor(o, src, w, o, ALU.mult, ALU.add)
                            ins.then_inc(s["tap_v"], 1)
                    v.wait_ge(s["tap_v"], CONV * H * (PARTS - 1) * b + CONV * H * n)
                    v.tensor_copy(ms[:, 0:1], ones[:, 0:1]).then_inc(s["conv_v"], 1)

                v.memset(raw_all[:, :, :, 0:CONV - 1].rearrange("p a h t -> p (a h) t"), 0.0).then_inc(s["pad_v"], 1)
                v.wait_ge(s["pad_v"], b + 1)
                conv(1, 1)
                with v.Fori(0, (PARTS - 2) // 2) as pp:
                    for e in range(2):
                        conv(2 * pp + 2 + e, e)
                v.wait_ge(s["norm_ps"], (CH + 1) * b + 1)
                v.tensor_copy(beta_s[:], bank[5][0:L, 0:CH * H]).then_inc(s["beta_s_v"], 1)
                for g in range(2):
                    v.memset(S[:, G * g:G * g + G, :], 0.0).then_inc(s["S_v"], 1)
                with v.Fori(0, CH) as c:
                    it = b * CH + c
                    cs = bass.ds(c * H, H)
                    v.wait_ge(s["beta_s_v"], b + 1)
                    v.wait_ge(s["gsum_a"], 2 * b + 2)
                    v.wait_ge(s["norm_ps"], (CH + 1) * b + c + 2)
                    v.tensor_scalar(ssb[:], bank[0][0:L, 0:H], 1e-6, None, ALU.add).then_inc(s["norm_v"], 1)
                    v.tensor_scalar(epsq[:], bank[0][:, H:H + 2], DH * LN_EPS, DH * LN_EPS * 1e-6, ALU.mult, ALU.add).then_inc(s["norm_v"], 1)
                    v.wait_ge(s["norm_v"], 5 * it + 1)
                    v.reciprocal(inv[:], ssb[:]).then_inc(s["norm_v"], 1)
                    v.wait_ge(s["norm_v"], 5 * it + 3)
                    v.scalar_tensor_tensor(bneg[:], inv[:], -1.0, beta_s[:, cs], ALU.mult, ALU.mult).then_inc(s["norm_v"], 1)
                    v.wait_ge(s["norm_v"], 5 * it + 4)
                    v.tensor_tensor(kend[:], bneg[:], e_out[:, cs], ALU.mult).then_inc(s["norm_v"], 1)
                    rsqrt(ssb[:], rs_y[0:L, :], rs_t[0:L, :], s["rs_n_v"], RS * it)
                    v.tensor_tensor(vnorm[:], ssb[:], rs_y[0:L, :], ALU.mult).then_inc(s["vnorm_v"], 1)
                    v.wait_ge(s["dd_p"], 2 * it + 2)
                    for g in range(2):
                        v.wait_ge(s["p1_ps"], 2 * it + g + 1)
                        for j in range(G):
                            h = G * g + j
                            ins = v.scalar_tensor_tensor(X[0:L, h, :], bank[6 + g][0:L, P * j:P * j + P], bneg[:, h:h + 1], DD[:, h, :], ALU.mult, ALU.mult)
                        ins.then_inc(s["x_v"], 1)
                    for lv in range(1, LEVELS + 1):
                        for g in range(2):
                            hs = slice(G * g, G * g + G)
                            if lv == 1:
                                v.wait_ge(s["nh_p"], 4 * it + 2 * g + 2)
                            else:
                                v.wait_ge(s["r_v"], NL * it + 2 * (lv - 2) + g + 1)
                            v.wait_ge(s["rr_ps"], NL * it + 2 * (lv - 1) + g + 1)
                            dst = Rh[lv % 2] if lv < LEVELS else R0
                            v.tensor_tensor(dst[:, hs, :], bank[3 * g + 1][0:L, 0:G * L].rearrange("r (h s) -> r h s", s=L),
                                            Rh[(lv - 1) % 2][:, hs, :], ALU.add).then_inc(s["r_v"], 1)
                    for g in range(2):
                        hs = slice(G * g, G * g + G)
                        v.wait_ge(s["ar_ps"], 2 * it + g + 1)
                        v.wait_ge(s["z_p"], 4 * it + 2 * g + 2)
                        v.tensor_tensor(Er[:, hs, :], bank[3 * g][0:L, 0:G * L].rearrange("r (h s) -> r h s", s=L), Z[:, hs, :],
                                        ALU.subtract).then_inc(s["er_v"], 1)
                    for g in range(2):
                        hs = slice(G * g, G * g + G)
                        v.wait_ge(s["re_ps"], 2 * it + g + 1)
                        v.tensor_tensor(R[0:L, hs, 0:L], bank[3 * g + 1][0:L, 0:G * L].rearrange("r (h s) -> r h s", s=L), R0[:, hs, :],
                                        ALU.add).then_inc(s["rf_v"], 1)
                    for g in range(2):
                        v.wait_ge(s["st_ps"], 2 * it + g + 1)
                        v.wait_ge(s["vn_a"], 2 * it + g + 1)
                        for j in range(G):
                            h = G * g + j
                            ins = v.scalar_tensor_tensor(Wn[:, h, :], bank[6 + g][:, P * j:P * j + P], e_in[:, 0, bass.ds(c * H + h, 1)], Vn[:, h, :],
                                                         ALU.mult, ALU.subtract)
                        ins.then_inc(s["wn_v"], 1)
                    for g in range(2):
                        v.wait_ge(s["su_ps"], 2 * it + g + 1)
                        for j in range(G):
                            h = G * g + j
                            ins = v.scalar_tensor_tensor(S[:, h, :], S[:, h, :], e_in[:, 1, bass.ds(c * H + h, 1)], bank[3 * g + 2][:, P * j:P * j + P],
                                                         ALU.mult, ALU.add)
                        ins.then_inc(s["S_v"], 1)
                    v.wait_ge(s["so_a"], 2 * it + 2)
                    v.scalar_tensor_tensor(ms[:], so[:], 1.0 / DH, epsq[:], ALU.mult, ALU.add).then_inc(s["ms_v"], 1)
                    v.wait_ge(s["ms_v"], it + 1)
                    rsqrt(ms[:], rs_y[:, 0:2], rs_t[:, 0:2], s["rs_o_v"], RS * it)
                    v.tensor_copy(rstd[:], rs_y[:, 0:2]).then_inc(s["rstd_v"], 1)
                    v.wait_ge(s["ot_ps"], it + 1)
                    tk = bass.ds(c * TOK, TOK)
                    v.scalar_tensor_tensor(oT[:, :, tk], bank[4][:, 0:2 * P].rearrange("p (h t) -> p h t", t=TOK), rms_w[:], gate[:, :, tk],
                                           ALU.mult, ALU.mult).then_inc(s["oT_v"], 1)

                def layer_norm(k, psum, skip, dst, done, ready, skip_ready=None):
                    n = 3 * b + k
                    for t in range(TT):
                        if skip_ready:
                            v.wait_ge(skip_ready, TT * b + t + 1)
                        v.wait_ge(ready[0], ready[1] + t)
                        v.tensor_tensor(yln[:, t, :], psum[t], skip[:, t, :], ALU.add).then_inc(s["yln_v"], 1)
                    for t in range(TT):
                        v.wait_ge(s["yln_v"], TT * n + t + 1)
                        v.bn_stats(bst[:, t, :], yln[:, t, :]).then_inc(s["bst_v"], 1)
                    v.wait_ge(s["bst_v"], TT * n + TT)
                    v.tensor_copy(ms[:], ones[:, 0:2])
                    for t in range(TT):
                        v.bn_aggr(mv[:, t, :], bst[:, t, :]).then_inc(s["mv_v"], 1)
                    v.wait_ge(s["mv_v"], TT * n + TT)
                    v.tensor_scalar(lnr[:], mv[:, :, 1], LN_EPS, None, ALU.add).then_inc(s["ve_v"], 1)
                    v.wait_ge(s["ve_v"], n + 1)
                    rsqrt(lnr[:], rs_y[:, 0:TT], rs_t[:, 0:TT], s["rs_l_v"], RS * n)
                    for t in range(TT):
                        v.tensor_scalar(dst[:, t, :], yln[:, t, :], mv[:, t, 0:1], rs_y[:, t:t + 1], ALU.subtract, ALU.mult).then_inc(done, 1)

                layer_norm(0, [bank[6 + t][:, 0:D] for t in range(TT)], x_tok, x1, s["x1_v"], (s["ao_ps"], 2 * b + 1))

                v.wait_ge(s["vx_ps"], b + 1)
                v.tensor_tensor(vx[:], bank[5][0:SK, 0:D], xbv[0:SK, :], ALU.add).then_inc(s["vx_v"], 1)
                v.wait_ge(s["qk_a"], 8 * b + 8)
                v.tensor_reduce(stat[:, 0, :], qk, AX.X, ALU.add).then_inc(s["stat_v"], 1)
                v.tensor_reduce(stat[:, 1, :], qk, AX.X, ALU.max).then_inc(s["stat_v"], 1)
                v.wait_ge(s["stat_v"], 2 * b + 2)
                v.tensor_tensor(qk, qk, stat[:, 1, :].unsqueeze(2).to_broadcast([P, ROWS, SK]), ALU.subtract).then_inc(s["d_v"], 1)
                v.wait_ge(s["e1_a"], b + 1)
                v.tensor_reduce(s_1[:], ex, AX.X, ALU.add).then_inc(s["s1_v"], 1)
                v.wait_ge(s["s1_v"], b + 1)
                v.reciprocal(r_1[:], s_1[:]).then_inc(s["r1_v"], 1)
                v.wait_ge(s["esq_p"], b + 1)
                v.tensor_reduce(s_2[:], e_sq, AX.X, ALU.add).then_inc(s["s2_v"], 1)
                v.wait_ge(s["s2_v"], b + 1)
                v.wait_ge(s["r1_v"], b + 1)
                v.tensor_tensor(s_2[:], s_2[:], r_1[:], ALU.mult).then_inc(s["var_v"], 1)
                v.wait_ge(s["var_v"], 3 * b + 1)
                v.tensor_tensor(s_2[:], s_2[:], r_1[:], ALU.mult).then_inc(s["var_v"], 1)
                v.wait_ge(s["var_v"], 3 * b + 2)
                v.tensor_scalar(stat[:, 2, :], s_2[:], 1.0 / SK, 1.0 / (SK - 1), ALU.subtract, ALU.mult).then_inc(s["var_v"], 1)
                v.wait_ge(s["h3_ps"], b + 1)
                v.tensor_scalar(lt[:], bank[2][:, 0:XH], tb3[:], LOG_T_MAX, ALU.add, ALU.min).then_inc(s["lt_v"], 1)
                v.wait_ge(s["lt_v"], 2 * b + 1)
                v.tensor_scalar(lt[:], lt[:], LOG_T_MIN, None, ALU.max).then_inc(s["lt_v"], 1)
                v.wait_ge(s["it_a"], b + 1)
                v.tensor_scalar(inv_t[:], inv_t[:], 0.5, None, ALU.mult).then_inc(s["it_v"], 1)
                v.wait_ge(s["it_v"], b + 1)
                for t in range(TT):
                    rs = slice(XH * t, XH * t + XH)
                    ins = v.tensor_tensor(qk[:, rs, :], qk[:, rs, :], inv_t[:].unsqueeze(2).to_broadcast([P, XH, SK]), ALU.mult)
                ins.then_inc(s["d2_v"], 1)
                v.wait_ge(s["e2_a"], b + 1)
                v.tensor_reduce(s_1[:], ex, AX.X, ALU.add).then_inc(s["se_v"], 1)
                v.wait_ge(s["se_v"], b + 1)
                v.reciprocal(r_1[:], s_1[:]).then_inc(s["rinv_v"], 1)
                v.wait_ge(s["rinv_v"], 2 * b + 1)
                v.tensor_scalar(r_1[:], r_1[:], 0.0, None, ALU.max).then_inc(s["rinv_v"], 1)
                for q in range(8):
                    v.wait_ge(s["eT_ps"], 8 * b + q + 1)
                    v.tensor_scalar(exT[:, XG * q:XG * q + XG, :].rearrange("k r q -> k (r q)"), bank[q][0:SK, :], 0.0, None, ALU.max).then_inc(s["eT_v"], 1)
                v.wait_ge(s["rinv_v"], 2 * b + 2)
                for t in range(TT):
                    v.wait_ge(s["av_ps"], 2 * b + t + 1)
                    v.tensor_tensor(ao[:, t, :].rearrange("p (h d) -> p h d", d=DK), bank[XG * t][:, 0:D].rearrange("p (h d) -> p h d", d=DK),
                                    r_1[:, XH * t:XH * t + XH].unsqueeze(2).to_broadcast([P, XH, DK]), ALU.mult).then_inc(s["ao_v"], 1)
                layer_norm(1, [bank[2 + t][:, 0:D] for t in range(TT)], x1b, x2, s["x2_v"], (s["x2_ps"], 2 * b + 1), s["x1b_p"])

                for q in range(4):
                    v.wait_ge(s["hid_a"], 4 * b + q + 1)
                    for f in (2 * q, 2 * q + 1):
                        v.tensor_scalar(arg[:, f, :], hid[:, f, :], 0.1, theta[:, f:f + 1], ALU.mult, ALU.add).then_inc(s["arg_v"], 1)
                v.wait_ge(s["arg_v"], FT * b + FT)
                turns_off(arg, rnd, s["rnd_v"], 4 * b)
                v.wait_ge(s["sin_a"], b + 1)
                for f in range(FT):
                    v.scalar_tensor_tensor(hid[:, f, :], rnd[:, f, :], coef[:, f:f + 1], hid[:, f, :], ALU.mult, ALU.add).then_inc(s["q_v"], 1)
                v.wait_ge(s["q_v"], FT * b + FT)
                v.tensor_scalar(arg, hid, 0.0, None, ALU.max).then_inc(s["act_v"], 1)
                layer_norm(2, [bank[2 + t][:, 0:D] for t in range(TT)], x2b, x3, s["x3_v"], (s["x3_ps"], 2 * b + 3), s["x2b_p"])


def rows_to_tiles(w):
    return w.reshape(w.shape[0] // P, P, w.shape[1]).transpose(1, 0, 2)


def padded_heads(w):
    o = np.zeros((w.shape[0], XG, XG, 32), np.float32)
    o[..., :DK] = w.reshape(w.shape[0], XG, XG, DK).transpose(0, 2, 1, 3)
    return o.reshape(w.shape[0], XH * 32)


def lay_out(i):
    f = {k: np.asarray(v, np.float32) if np.asarray(v).dtype == np.float32 else np.asarray(v) for k, v in i.items()}
    d, x, n = "L0_attn_", "L0_xattn_", "L0_ffn_"
    k, v = f[d + "Wk"], f[d + "Wv"]
    parts = [f[d + "Wg"], f[d + "Wq"]] + [w[:, H * DH * j:H * DH * (j + 1)] for w in (k, v) for j in range(NHH)]
    taps = np.concatenate([f[d + "conv_q"], f[d + "conv_k"], f[d + "conv_v"]])
    cols = lambda u: u.reshape(-1, P).T
    a = {
        "x": f["x"], "ctx": f["ctx_1024"],
        "w_parts": np.stack([rows_to_tiles(w) for w in parts] + [
            rows_to_tiles(f[n + "W1"]), rows_to_tiles(f[n + "W2"]).reshape(P, KC, H * DH)]),
        "conv_w": taps.reshape(-1, P, CONV).transpose(1, 0, 2),
        "w_ab": rows_to_tiles(np.concatenate([f[d + "Wa"], f[d + "Wb"]], 1)),
        "w_o": rows_to_tiles(f[d + "Wo"]), "rms_w": f[d + "rms_weight"][:, None],
        "A_log": f[d + "A_log"], "dt_bias": f[d + "dt_bias"],
        "xwq": rows_to_tiles(padded_heads(f[x + "Wq"].T)), "xwk": rows_to_tiles(padded_heads(f[x + "Wk"].T)),
        "xbq": cols(padded_heads(f[x + "bq"][None])[0]), "xbk": cols(padded_heads(f[x + "bk"][None])[0]),
        "xwv": rows_to_tiles(f[x + "Wv"].T), "xwo": rows_to_tiles(f[x + "Wo"].T),
        "xbv": f[x + "bv"], "xbo": f[x + "bo"], "fb2": f[n + "b2"],
        "tw1": f[x + "w1"].T, "tb1": f[x + "b1"][:, None], "tw2": np.pad(f[x + "w2"].T, ((0, 0), (0, P - 64))), "tb2": f[x + "b2"][:, None],
        "tw3": f[x + "w3"].T, "tb3": f[x + "b3"],
        "fb1": cols(f[n + "b1"]),
        "theta": cols(f[n + "quantum_phases"]), "w_re": cols(f[n + "quantum_weights_real"]),
        "w_im": cols(f[n + "quantum_weights_imag"]),
    }
    a |= {"c_" + key: w for key, w in shape_constants().items()}
    return {key: np.ascontiguousarray(w) for key, w in a.items()}


def kernel(**inputs):
    import concourse.bacc as bacc
    from concourse.bass_utils import run_bass_kernel_spmd

    nc = bacc.Bacc("TRN2", target_bir_lowering=False, num_devices=1)
    arrays = lay_out(inputs)
    aps = {k: nc.dram_tensor(f"in_{k}", w.shape, mybir.dt.from_np(w.dtype), kind="ExternalInput").ap() for k, w in arrays.items()}
    out = nc.dram_tensor("out_x", (BATCHES, T, D), F32, kind="ExternalOutput").ap()
    build(nc, aps, out)
    r = run_bass_kernel_spmd(nc, [{f"in_{k}": w for k, w in arrays.items()}], core_ids=[0])
    return r.results[0]["out_x"]
```

```python
from contextlib import ExitStack

import numpy as np
import concourse.bass as bass
from concourse import mybir

F32, F16 = mybir.dt.float32, mybir.dt.float16
ALU, ACT, AX = mybir.AluOpType, mybir.ActivationFunctionType, mybir.AxisListType

P = 128
BATCHES, T, D = 16, 256, 256
TT, KC = T // P, D // P
H, DH, NHH = 8, 128, 3
TOK = 32
CH = T // TOK
L = TOK * NHH
G = H // 2
PARTS = 1 + 1 + 2 * NHH
STREAM = PARTS + 2
CONV = 4
LEVELS = 6
XH, DK, SK = 16, 16, 77
XG = 4
FF = 1024
FT = FF // P
LN_EPS = 1e-5
MAGIC = float(1.5 * 2 ** 23)
RS = 11
TWO_PI = 2 * float(np.pi)
PI_BELOW = 3.1415925
LOG_T_MIN, LOG_T_MAX = float(np.log(0.1)), float(np.log(10.0))


def shape_constants():
    s, m, t = np.arange(L), np.arange(TOK)[:, None], np.arange(TOK)
    tok = s // NHH
    out = {
        "ident": np.eye(P),
        "after": m > tok[None],
        "upto": np.concatenate([m <= tok[None], m <= t[None]], 1),
        "strict": s[:, None] < s[None],
        "causal": tok[:, None] <= t[None],
        "spread": np.concatenate([s[None] == NHH * m + i for i in range(NHH)], 1),
        "ones": np.ones((P, P)),
    }
    return {k: v.astype(np.float32) for k, v in out.items()}


def build(nc, a, out):
    const = shape_constants()
    ctx = ExitStack()
    with ctx:
        def sb(name, shape, dt=F32):
            return ctx.enter_context(nc.sbuf_tensor(name, shape, dt))

        def sem(name):
            return ctx.enter_context(nc.semaphore(name))

        bank = [ctx.enter_context(nc.psum_tensor(f"bank{i}", [P, 512], F32)) for i in range(8)]

        cst = {k: sb(f"c_{k}", list(v.shape)) for k, v in const.items()}
        ident, ones = cst["ident"], cst["ones"]
        ident_h = sb("ident_h", [P, P], F16)
        w_ab = sb("w_ab", [P, KC, 4 * H])
        conv_w = sb("conv_w", [P, (PARTS - 1) * H, CONV])
        w_o = sb("w_o", [P, H, D])
        rms_w = sb("rms_w", [P, 1])
        neg_a = sb("neg_a", [TOK, H])
        dt_b = sb("dt_b", [TOK, H])
        xwq = sb("xwq", [P, KC, XG * P])
        xwk = sb("xwk", [P, KC, XG * P])
        xbq, xbk = sb("xbq", [P, XG]), sb("xbk", [P, XG])
        xwv, xwo = sb("xwv", [P, KC, D]), sb("xwo", [P, KC, D])
        xbv, xbo, fb2 = sb("xbv", [P, D]), sb("xbo", [P, D]), sb("fb2", [P, D])
        tw1, tb1 = sb("tw1", [P, 3, 64]), sb("tb1", [64, 1])
        tw2, tb2 = sb("tw2", [64, P]), sb("tb2", [64, 1])
        tw3, tw3b, tb3 = sb("tw3", [64, 1]), sb("tw3b", [64, P]), sb("tb3", [P, 1])
        fb1 = sb("fb1", [P, FT])
        theta, w_re, w_im = sb("theta", [P, FT]), sb("w_re", [P, FT]), sb("w_im", [P, FT])
        coef, trig, turn = sb("coef", [P, FT]), sb("trig", [P, 2 * FT]), sb("turn", [P, 2 * FT])

        w_part = [sb(f"w_part{i}", [P, KC, H * DH]) for i in range(2)]
        x_tok, xT = sb("x_tok", [P, TT, D]), sb("xT", [P, KC, T])
        fw1, fw2 = w_part[0], w_part[1][:].rearrange("p k (g n) -> p (k g) n", n=D)
        raw_all = sb("raw_all", [P, 2, H, CONV - 1 + T])
        raw = [raw_all[:, i] for i in range(2)]
        co = sb("co", [P, (PARTS - 1) * H, T])
        gate, oT = sb("gate", [P, H, T]), sb("oT", [P, H, T])
        zdec, zabs, gdec = sb("zdec", [TOK, CH, H]), sb("zabs", [TOK, CH, H]), sb("gdec", [TOK, CH, H])
        beta = sb("beta", [TOK, CH, NHH, H])
        e_seg = sb("e_seg", [L, CH * H, TOK])
        e_in = sb("e_in", [P, 2, CH * H])
        e_out = sb("e_out", [L, CH * H])
        beta_s = sb("beta_s", [L, CH * H])

        space = sb("space", [P, 4 * H * P + 3 * H * L])

        def lay(parts, at, rows=P):
            got = []
            for shape in parts:
                n = int(np.prod(shape))
                u = at[0][0:rows, at[1]:at[1] + n]
                at[1] += n
                got.append(u if len(shape) == 1 else u.rearrange("p (a b) -> p a b", b=shape[1]))
            return got

        at = [space, 0]
        KQ0, KQ1, SQ = lay([(H, P)] * 3, at)
        KQ = [KQ0, KQ1]
        VT, = lay([(H, L)], at)
        DD, = lay([(H, P)], at, L)
        M32, R0 = lay([(H, L)] * 2, at, L)
        gtab, = lay([(CH * H, TOK)], [space, 0], TOK)
        X = [sb(f"X{i}", [P, H, P]) for i in range(2)]
        Nh = [sb(f"Nh{i}", [L, H, L], F16) for i in range(2)]
        Mh = [sb(f"Mh{i}", [L, H, L], F16) for i in range(2)]
        Rh = [sb(f"Rh{i}", [L, H, L], F16) for i in range(2)]
        R0T, Er = sb("R0T", [L, H, L], F16), sb("Er", [L, H, L], F16)
        R = sb("R", [P, H, P])
        Vn = sb("Vn", [P, H, P])
        at = [raw_all[:].rearrange("p a h t -> p (a h t)"), 0]
        Wn, Y, S = lay([(H, P)] * 3, at)
        Ks, = lay([(H, P)], at, L)
        inv = sb("inv", [L, H])
        bneg, kend, vnorm = ([sb(f"{n}{i}", [L, H]) for i in range(2)] for n in ("bneg", "kend", "vnorm"))
        epsq, so = [sb(f"epsq{i}", [P, 2]) for i in range(2)], sb("so", [P, 2])
        rs_x, rs_t, rs_y = sb("rs_x", [P, H + 2]), sb("rs_t", [P, H + 2]), sb("rs_y", [P, H + 2])
        rstd, On = sb("rstd", [P, 2]), sb("On", [P, 2, P])
        ms = sb("ms", [P, 2])

        at = [space, 0]
        x1, x1b, x2, x2b, yln, ao = lay([(TT, D)] * 6, at)
        x1T, x2T, aoT = lay([(KC, T)] * 3, at)
        qTx, kTx = lay([(XG, T), (XG, SK)], at)
        vx, = lay([(D,)], at, SK)
        ctxT, = lay([(KC, SK)], at)
        x3 = sb("x3", [P, TT, D])
        bst, mv, lnr = sb("bst", [P, TT, 6]), sb("mv", [P, TT, 2]), sb("lnr", [P, TT])
        ctx_sb = sb("ctx_sb", [SK, D])
        ROWS = TT * XH
        co_flat = co[:].rearrange("p a t -> p (a t)")
        qk = co_flat[:, 0:ROWS * SK].rearrange("p (r k) -> p r k", k=SK)
        ex = co_flat[:, 2560:2560 + ROWS * SK].rearrange("p (r k) -> p r k", k=SK)
        exT = co_flat[0:SK, 5120:5120 + ROWS * P].rearrange("p (r q) -> p r q", q=P)
        e_sq = co_flat[:, 9216:9216 + ROWS * SK].rearrange("p (r k) -> p r k", k=SK)
        hid = co_flat[:, 0:FT * T].rearrange("p (f t) -> p f t", t=T)
        arg = co_flat[:, 2560:2560 + FT * T].rearrange("p (f t) -> p f t", t=T)
        rnd = co_flat[:, 5120:5120 + FT * T].rearrange("p (f t) -> p f t", t=T)
        stat = sb("stat", [P, 3, ROWS])
        s_1, r_1, s_2 = sb("s_1", [P, ROWS]), sb("r_1", [P, ROWS]), sb("s_2", [P, ROWS])
        h1, h2 = sb("h1", [64, XH]), sb("h2", [64, XH])
        lt, inv_t = sb("lt", [P, XH]), sb("inv_t", [P, XH])

        names = """const pad_v x_in ctx_in w_in0 w_in1 setup_p setup_a setup_v
            xT_ps xT ab_ps zdec_v eb_a ab_used gate_v beta_v gtab_p gsum_ps eseg_ps gsum_a beta_s_v eseg_a
            proj_ps raw_a tap_v conv_v
            silu_a vsilu_a sq_p norm_ps norm_v vnorm_v p1_ps kt_ps vt_ps dd_p x_v rh_p nh_v xt_ps mh_a m32_a vn_a ks_v
            n2_ps m2_ps rr_ps n_a m_a r_v ar_ps rt_ps rt_a er_v re_ps rf_v
            S_v st_ps wn_v y_ps y_a su_ps o_ps so_a rs_in_v rstd_v on_a ot_ps oT_v
            ao_ps yln_v bst_v mv_v ve_v lnr_v rs_c_v rs_l_v x1_v x1b_p x1T_ps x1T_a ctxT_ps ctxT_a kx_ps kx_a vx_ps vx_v
            qx_ps qx_a sc_ps qk_a stat_v d_v e1_a esq_p s1_v s2_v r1_v var_v h1_ps h1_a h2_ps h2_a h3_ps
            lt_v it_a it_v d2_v e2_a se_v rinv_v eT_ps eT_v av_ps ao_v aoT_ps aoT_a x2_ps x2_v x2b_p
            x2T_ps x2T_a hid_ps hid_a arg_v rnd_v sin_a q_v act_v x3_ps x3_v stored""".split()
        s = {n: sem(n) for n in names}

        block = ctx.enter_context(nc.Block())

        def ld(eng, dst, src):
            eng.dma_start(dst, src).then_inc(s["const"], 16)

        loads = [(cst[k][:], a["c_" + k]) for k in const] + [
            (w_ab[:], a["w_ab"]), (conv_w[:], a["conv_w"]), (w_o[:], a["w_o"]), (rms_w[:], a["rms_w"]),
            (neg_a[:], a["A_log"].partition_broadcast(TOK)), (dt_b[:], a["dt_bias"].partition_broadcast(TOK)),
            (xwq[:], a["xwq"]), (xwk[:], a["xwk"]), (xbq[:], a["xbq"]), (xbk[:], a["xbk"]),
            (xwv[:], a["xwv"]), (xwo[:], a["xwo"]),
            (xbv[:], a["xbv"].partition_broadcast(P)), (xbo[:], a["xbo"].partition_broadcast(P)),
            (fb2[:], a["fb2"].partition_broadcast(P)), (tw1[:], a["tw1"].partition_broadcast(P)),
            (tb1[:], a["tb1"]), (tw2[:], a["tw2"]), (tb2[:], a["tb2"]), (tw3[:], a["tw3"]),
            (tb3[:], a["tb3"].partition_broadcast(P)), (fb1[:], a["fb1"]),
            (theta[:], a["theta"]), (w_re[:], a["w_re"]), (w_im[:], a["w_im"]),
        ]
        ALL_CONST = 16 * len(loads)
        BANKS = H // 2
        NL = 2 * LEVELS

        @block.sync
        def _(sp):
            for dst, src in loads:
                ld(sp, dst, src)
            with sp.Fori(0, BATCHES) as b:
                sp.wait_ge(s["x1_v"], 2 * b + 2)
                sp.dma_start(x_tok[:], a["x"][bass.ds(b, 1)].rearrange("b (t p) d -> (b p) t d", p=P)).then_inc(s["x_in"], 16)
                sp.wait_ge(s["ctxT_a"], b + 1)
                sp.dma_start(ctx_sb[:], a["ctx"][bass.ds(b, 1)].rearrange("b k d -> (b k) d")).then_inc(s["ctx_in"], 16)
                for n in range(STREAM):
                    if n == 0:
                        sp.wait_ge(s["hid_ps"], 4 * b + 4)
                    elif n == 1:
                        sp.wait_ge(s["x3_ps"], 2 * b + 2)
                    else:
                        sp.wait_ge(s["proj_ps"], PARTS * BANKS * b + BANKS * (n - 2) + BANKS)
                    sp.dma_start(w_part[n % 2][:], a["w_parts"][n]).then_inc(s[f"w_in{n % 2}"], 16)

        @block.gpsimd
        def _(pool):
            pool.memset(Vn[:], 0.0)
            for x in X:
                pool.memset(x[:], 0.0)
            pool.memset(R[:], 0.0).then_inc(s["setup_p"], 1)
            pool.wait_ge(s["const"], ALL_CONST)
            pool.wait_ge(s["setup_p"], 1)
            pool.tensor_copy(ident_h[:], ident[:]).then_inc(s["setup_p"], 1)

            eye = ident[0:L, 0:L].unsqueeze(1).to_broadcast([L, G, L])
            with pool.Fori(0, BATCHES) as b:
                pool.wait_ge(s["gate_v"], b + 1)
                pool.tensor_tensor(gtab, gdec[:].rearrange("m c h -> m (c h)").unsqueeze(2).to_broadcast([TOK, CH * H, TOK]),
                                   cst["upto"][:, L:P].unsqueeze(1).to_broadcast([TOK, CH * H, TOK]), ALU.mult).then_inc(s["gtab_p"], 1)

                def squares(m, par):
                    pool.wait_ge(s["norm_ps"], (CH + 1) * b + m + 1)
                    pool.wait_ge(s["silu_a"], 4 * (CH * b + m) + 4)
                    pool.tensor_tensor(SQ, KQ[par], KQ[par], ALU.mult).then_inc(s["sq_p"], 1)

                def decays(m):
                    es = e_seg[:, bass.ds(m * H, H), :]
                    pool.tensor_tensor(DD[:, :, 0:L].rearrange("s h (t i) -> s h t i", i=NHH),
                                       es.unsqueeze(3).to_broadcast([L, H, TOK, NHH]),
                                       cst["strict"][:].rearrange("s (t i) -> s t i", i=NHH).unsqueeze(1).to_broadcast([L, H, TOK, NHH]),
                                       ALU.mult).then_inc(s["dd_p"], 1)
                    pool.tensor_tensor(DD[:, :, L:P], es, cst["causal"][:].unsqueeze(1).to_broadcast([L, H, TOK]),
                                       ALU.mult).then_inc(s["dd_p"], 1)

                def stage(m, par):
                    squares(m, par)
                    if not isinstance(m, int) or m > 0:
                        pool.wait_ge(s["x_v"], 2 * (CH * b + m))
                    decays(m)
                    for g in range(2):
                        hs = slice(G * g, G * g + G)
                        pool.wait_ge(s["x_v"], 2 * (CH * b + m) + g + 1)
                        pool.tensor_tensor(Rh[0][:, hs, :], X[par][0:L, hs, 0:L], eye, ALU.add).then_inc(s["rh_p"], 1)

                pool.wait_ge(s["eseg_a"], 4 * b + 4)
                stage(0, 0)
                stage(1, 1)
                with pool.Fori(0, CH // 2 - 1) as cc:
                    stage(2 * cc + 2, 0)
                    stage(2 * cc + 3, 1)
                for t in range(TT):
                    pool.wait_ge(s["x1_v"], 2 * b + t + 3)
                    pool.tensor_tensor(x1b[:, t, :], x1[:, t, :], xbo[:], ALU.add).then_inc(s["x1b_p"], 1)
                pool.wait_ge(s["e1_a"], b + 1)
                pool.tensor_tensor(e_sq, ex, ex, ALU.mult).then_inc(s["esq_p"], 1)
                for t in range(TT):
                    pool.wait_ge(s["x2_v"], 2 * b + t + 1)
                    pool.tensor_tensor(x2b[:, t, :], x2[:, t, :], fb2[:], ALU.add).then_inc(s["x2b_p"], 1)

        @block.scalar
        def _(act):
            A = act.activation
            act.wait_ge(s["const"], ALL_CONST)
            A(neg_a[:], neg_a[:], ACT.Exp).then_inc(s["setup_a"], 1)
            act.wait_ge(s["setup_v"], 5)
            A(trig[:], turn[:], ACT.Sin).then_inc(s["setup_a"], 1)
            act.copy(ms[:], ident[:, 0:2]).then_inc(s["ctxT_a"], 1)
            with act.Fori(0, BATCHES) as b:
                act.wait_ge(s["xT_ps"], b + 1)
                A(xT[:].rearrange("p k t -> p (k t)"), bank[0][:], ACT.Copy).then_inc(s["xT"], 1)
                act.wait_ge(s["ab_ps"], b + 1)
                ab = bank[7][0:TOK, 0:CH * 4 * H].rearrange("m (c k) -> m c k", k=4 * H)
                A(beta[:].rearrange("m c i h -> m c (i h)"), ab[:, :, H:4 * H], ACT.Exp, scale=-1.0).then_inc(s["eb_a"], 1)
                act.wait_ge(s["zdec_v"], 2 * b + 2)
                A(zabs[:], zabs[:], ACT.Exp, scale=-1.0).then_inc(s["eb_a"], 1)
                act.wait_ge(s["eb_a"], 3 * b + 2)
                A(zabs[:], zabs[:], ACT.Ln, bias=1.0).then_inc(s["eb_a"], 1)

                def evacuate(n, e):
                    for q in range(BANKS):
                        act.wait_ge(s["proj_ps"], PARTS * BANKS * b + BANKS * n + q + 1)
                        src = bank[BANKS * e + q][:].rearrange("p (j t) -> p j t", t=T)
                        A(raw[e][:, 2 * q:2 * q + 2, CONV - 1:], src, ACT.Copy).then_inc(s["raw_a"], 1)

                for q in range(BANKS):
                    act.wait_ge(s["proj_ps"], PARTS * BANKS * b + q + 1)
                    A(gate[:, 2 * q:2 * q + 2, :], bank[q][:].rearrange("p (j t) -> p j t", t=T), ACT.Silu).then_inc(s["raw_a"], 1)
                evacuate(1, 1)
                with act.Fori(0, (PARTS - 2) // 2) as pp:
                    for e in range(2):
                        act.wait_ge(s["conv_v"], (PARTS - 1) * b + 2 * pp + e + 1)
                        evacuate(2 * pp + 2 + e, e)

                act.wait_ge(s["gsum_ps"], b + 1)
                A(e_in[:].rearrange("p a c -> p (a c)"), bank[0][:, 0:2 * CH * H], ACT.Exp).then_inc(s["gsum_a"], 1)
                A(e_out[:], bank[0][0:L, 2 * CH * H:3 * CH * H], ACT.Exp).then_inc(s["gsum_a"], 1)
                for q in range(4):
                    act.wait_ge(s["eseg_ps"], 4 * b + q + 1)
                    A(e_seg[:, 16 * q:16 * q + 16, :].rearrange("s c t -> s (c t)"), bank[1 + q][0:L, :], ACT.Exp).then_inc(s["eseg_a"], 1)
                act.wait_ge(s["conv_v"], (PARTS - 1) * b + PARTS)

                def stage_kq(m, par):
                    tk = bass.ds(m * TOK, TOK)
                    A(KQ[par][:, :, L:P], co[:, 0:H, tk], ACT.Silu).then_inc(s["silu_a"], 1)
                    for i in range(NHH):
                        A(KQ[par][:, :, 0:L].rearrange("p h (t i) -> p h t i", i=NHH)[:, :, :, i], co[:, H + H * i:2 * H + H * i, tk],
                          ACT.Silu).then_inc(s["silu_a"], 1)

                def stage_v(m):
                    tk = bass.ds(m * TOK, TOK)
                    for i in range(NHH):
                        A(VT.rearrange("p h (t i) -> p h t i", i=NHH)[:, :, :, i], co[:, H * (4 + i):H * (5 + i), tk],
                          ACT.Silu).then_inc(s["vsilu_a"], 1)

                def step(c, par, state=True, inverse=True, stage=True):
                    n, m = c + 1, c + 2
                    it, itn = CH * b + c, CH * b + n

                    def level(lv, g):
                        hs = slice(G * g, G * g + G)
                        if lv < LEVELS - 1:
                            act.wait_ge(s["n2_ps"], (NL - 2) * itn + 2 * lv + g + 1)
                            A(Nh[(lv + 1) % 2][:, hs, :], bank[2 * g][0:L, 0:G * L].rearrange("r (h s) -> r h s", s=L),
                              ACT.Copy).then_inc(s["n_a"], 1)
                        act.wait_ge(s["m2_ps"], NL * itn + 2 * lv + g + 1)
                        A(Mh[(lv + 1) % 2][:, hs, :], bank[2 * g + 1][0:L, 0:G * L].rearrange("r (h s) -> r h s", s=L),
                          ACT.Copy).then_inc(s["m_a"], 1)

                    def y_out(g):
                        act.wait_ge(s["y_ps"], 2 * it + g + 1)
                        A(Y[:, G * g:G * g + G, :].rearrange("p h d -> p (h d)"), bank[6 + g][:], ACT.Copy).then_inc(s["y_a"], 1)

                    def vn_out(g):
                        act.wait_ge(s["vnorm_v"], itn + 1)
                        act.wait_ge(s["vt_ps"], 2 * itn + g + 1)
                        for j in range(G):
                            h = G * g + j
                            ins = A(Vn[0:L, h, :], bank[6 + g][0:L, P * j:P * j + P], ACT.Copy, scale=vnorm[1 - par][:, h:h + 1])
                        ins.then_inc(s["vn_a"], 1)

                    if stage:
                        if state:
                            act.wait_ge(s["st_ps"], 2 * it + 2)
                        stage_kq(m, par)
                    if inverse:
                        for g in range(2):
                            hs = slice(G * g, G * g + G)
                            act.wait_ge(s["xt_ps"], 2 * itn + g + 1)
                            src = bank[2 * g][0:L, 0:G * L].rearrange("r (h s) -> r h s", s=L)
                            A(Mh[0][:, hs, :], src, ACT.Copy).then_inc(s["mh_a"], 1)
                            A(M32[:, hs, :], src, ACT.Copy).then_inc(s["m32_a"], 1)
                    for g in range(2):
                        if state:
                            y_out(g)
                        if inverse:
                            level(0, g)
                    if inverse:
                        level(1, 0)
                        level(1, 1)
                    if state:
                        act.wait_ge(s["o_ps"], it + 1)
                        for j in range(2):
                            A(On[:, j, :], bank[5][:, P * j:P * j + P], ACT.Square, accum_out=so[:, j:j + 1]).then_inc(s["so_a"], 1)
                    if inverse:
                        level(2, 0)
                        level(2, 1)
                        for g in range(2):
                            vn_out(g)
                            level(3, g)
                        for g in range(2):
                            level(4, g)
                        if stage:
                            stage_v(m)
                        for g in range(2):
                            level(5, g)
                    if state:
                        act.wait_ge(s["rstd_v"], it + 1)
                        act.wait_ge(s["so_a"], 2 * it + 2)
                        for j in range(2):
                            A(On[:, j, :], bank[5][:, P * j:P * j + P], ACT.Copy, scale=rstd[:, j:j + 1]).then_inc(s["on_a"], 1)
                    if inverse:
                        for g in range(2):
                            act.wait_ge(s["rt_ps"], 2 * itn + g + 1)
                            A(R0T[:, G * g:G * g + G, :], bank[4][0:L, 0:G * L].rearrange("r (h s) -> r h s", s=L),
                              ACT.Copy).then_inc(s["rt_a"], 1)

                stage_kq(0, 0)
                stage_v(0)
                step(-1, 1, state=False)
                with act.Fori(0, CH // 2 - 1) as cc:
                    step(2 * cc, 0)
                    step(2 * cc + 1, 1)
                step(CH - 2, 0, stage=False)
                step(CH - 1, 1, inverse=False, stage=False)

                act.wait_ge(s["ctxT_ps"], b + 1)
                A(ctxT.rearrange("p k c -> p (k c)"), bank[2][:, 0:KC * SK], ACT.Copy).then_inc(s["ctxT_a"], 1)
                act.wait_ge(s["kx_ps"], b + 1)
                for g in range(XG):
                    ins = A(kTx[:, g, :], bank[3][:, SK * g:SK * g + SK], ACT.Identity, bias=xbk[:, g:g + 1])
                ins.then_inc(s["kx_a"], 1)
                act.wait_ge(s["x1T_ps"], b + 1)
                A(x1T.rearrange("p k t -> p (k t)"), bank[0][:], ACT.Copy).then_inc(s["x1T_a"], 1)
                for q in range(2):
                    act.wait_ge(s["qx_ps"], 2 * b + q + 1)
                    for j in range(2):
                        ins = A(qTx[:, 2 * q + j, :], bank[6 + q][:, T * j:T * j + T], ACT.Identity, bias=xbq[:, 2 * q + j:2 * q + j + 1])
                    ins.then_inc(s["qx_a"], 1)
                for q in range(8):
                    act.wait_ge(s["sc_ps"], 8 * b + q + 1)
                    A(qk[:, XG * q:XG * q + XG, :].rearrange("p r k -> p (r k)"), bank[q][:, 0:XG * SK], ACT.Copy).then_inc(s["qk_a"], 1)
                act.wait_ge(s["d_v"], b + 1)
                A(ex, qk, ACT.Exp, scale=DK ** -0.5).then_inc(s["e1_a"], 1)
                act.wait_ge(s["h1_ps"], b + 1)
                A(h1[:], bank[0][0:64, 0:XH], ACT.Gelu, bias=tb1[:]).then_inc(s["h1_a"], 1)
                act.wait_ge(s["h2_ps"], b + 1)
                A(h2[:], bank[1][0:64, 0:XH], ACT.Gelu, bias=tb2[:]).then_inc(s["h2_a"], 1)
                act.wait_ge(s["lt_v"], 2 * b + 2)
                A(inv_t[:], lt[:], ACT.Exp, scale=-1.0).then_inc(s["it_a"], 1)
                act.wait_ge(s["d2_v"], b + 1)
                A(ex, qk, ACT.Exp).then_inc(s["e2_a"], 1)
                act.wait_ge(s["aoT_ps"], b + 1)
                A(aoT.rearrange("p k t -> p (k t)"), bank[1][:], ACT.Copy).then_inc(s["aoT_a"], 1)

                act.wait_ge(s["x2T_ps"], b + 1)
                A(x2T.rearrange("p k t -> p (k t)"), bank[4][:], ACT.Copy).then_inc(s["x2T_a"], 1)
                for q, bk in enumerate((0, 1, 6, 7)):
                    act.wait_ge(s["hid_ps"], 4 * b + q + 5)
                    for j in range(2):
                        f = 2 * q + j
                        ins = A(hid[:, f, :], bank[bk][:, T * j:T * j + T], ACT.Identity, bias=fb1[:, f:f + 1])
                    ins.then_inc(s["hid_a"], 1)
                act.wait_ge(s["rnd_v"], 4 * b + 4)
                A(rnd, arg, ACT.Sin).then_inc(s["sin_a"], 1)
                act.wait_ge(s["x3_v"], 2 * b + 4)
                act.dma_start(out[bass.ds(b, 1)].rearrange("b (t p) d -> (b p) t d", p=P), x3[:]).then_inc(s["stored"], 16)
                act.wait_ge(s["stored"], 16 * b + 16)

        @block.tensor
        def _(pe):
            MM = pe.matmul
            pe.wait_ge(s["const"], ALL_CONST)
            pe.wait_ge(s["setup_p"], 2)
            for q in range(4):
                MM(bank[0][:, 0:P], ident[:], ident[:], start=True, stop=True).then_inc(s["hid_ps"], 1)
            for q in range(2):
                MM(bank[0][:, 0:P], ident[:], ident[:], start=True, stop=True).then_inc(s["x3_ps"], 1)
            with pe.Fori(0, BATCHES) as b:
                pe.wait_ge(s["x3_v"], 2 * b + 2)
                pe.wait_ge(s["x_in"], 16 * b + 16)
                for k in range(KC):
                    for t in range(TT):
                        ins = pe.transpose(bank[0][:, T * k + P * t:T * k + P * t + P], x_tok[:, t, P * k:P * k + P], ident[:])
                ins.then_inc(s["xT_ps"], 1)
                pe.wait_ge(s["xT"], b + 1)
                for c in range(CH):
                    for k in range(KC):
                        ins = MM(bank[7][0:TOK, 4 * H * c:4 * H * (c + 1)], xT[:, k, TOK * c:TOK * c + TOK], w_ab[:, k, :],
                                 start=(k == 0), stop=(k == KC - 1))
                ins.then_inc(s["ab_ps"], 1)

                def project(n, e, wsem_value):
                    pe.wait_ge(s[f"w_in{e}"], wsem_value)
                    for q in range(BANKS):
                        if not isinstance(n, int) or n >= 2:
                            pe.wait_ge(s["raw_a"], PARTS * BANKS * b + BANKS * (n - 2) + q + 1)
                        for j in range(2):
                            o = DH * (2 * q + j)
                            for k in range(KC):
                                ins = MM(bank[BANKS * e + q][:, T * j:T * j + T], w_part[e][:, k, o:o + DH], xT[:, k, :],
                                         start=(k == 0), stop=(k == KC - 1))
                        ins.then_inc(s["proj_ps"], 1)

                project(0, 0, 16 * (STREAM // 2) * b + 16)
                pe.wait_ge(s["ab_used"], b + 1)
                pe.wait_ge(s["eb_a"], 3 * b + 1)
                project(1, 1, 16 * (STREAM // 2) * b + 16)
                with pe.Fori(0, (PARTS - 2) // 2) as pp:
                    for e in range(2):
                        project(2 * pp + 2 + e, e, 16 * (STREAM // 2) * b + 16 * pp + 32)

                pe.wait_ge(s["raw_a"], PARTS * BANKS * b + PARTS * BANKS)
                pe.wait_ge(s["gate_v"], b + 1)
                pe.wait_ge(s["beta_v"], 2 * b + 2)
                gflat = gdec[:].rearrange("m c h -> m (c h)")
                NCH = CH * H
                MM(bank[0][:, 0:NCH], cst["upto"][:], gflat, start=True, stop=True)
                MM(bank[0][:, NCH:2 * NCH], ones[0:TOK, :], gflat, start=True, stop=True)
                MM(bank[0][0:L, 2 * NCH:3 * NCH], cst["after"][:], gflat, start=True, stop=True).then_inc(s["gsum_ps"], 1)
                for i in range(NHH):
                    ins = MM(bank[5][0:L, 0:NCH], cst["spread"][:, L * i:L * i + L], beta[:, :, i, :], start=(i == 0), stop=(i == NHH - 1))
                ins.then_inc(s["norm_ps"], 1)
                pe.wait_ge(s["gtab_p"], b + 1)
                for q in range(4):
                    MM(bank[1 + q][0:L, :], cst["after"][:], gtab[:, 16 * q:16 * q + 16, :], start=True, stop=True).then_inc(s["eseg_ps"], 1)

                def norms_k(m):
                    pe.wait_ge(s["sq_p"], CH * b + m + 1)
                    for h in range(H):
                        MM(bank[5][:, 2 * P + h:2 * P + h + 1], SQ[:, h, :], ones[:, 0:1], start=True, stop=True)

                def norms_q(m):
                    for h in range(H):
                        o, col = TOK * (h % G), 2 * P + H + h // G
                        ins = MM(bank[5][o:o + TOK, col:col + 1], SQ[:, h, L:P], ones[:, 0:1], start=True, stop=True)
                    ins.then_inc(s["norm_ps"], 1)

                def dots(m, par, g):
                    pe.wait_ge(s["silu_a"], 4 * (CH * b + m) + 4)
                    for j in range(G):
                        h = G * g + j
                        ins = MM(bank[2 * g][0:L, P * j:P * j + P], KQ[par][:, h, 0:L], KQ[par][:, h, :], start=True, stop=True)
                    ins.then_inc(s["p1_ps"], 1)

                def x_rows(m, par, g):
                    pe.wait_ge(s["x_v"], 2 * (CH * b + m) + g + 1)
                    for j in range(G):
                        ins = pe.transpose(bank[2 * g][0:L, L * j:L * j + L], X[par][0:L, G * g + j, 0:L], ident[0:L, 0:L])
                    ins.then_inc(s["xt_ps"], 1)

                def step(c, par, state=True, inverse=True, stage=True):
                    n, m = c + 1, c + 2
                    it, itn = CH * b + c, CH * b + n
                    kqn, x = KQ[1 - par], X[par]

                    def level(lv, g):
                        if not inverse:
                            return
                        cur = lv % 2
                        if lv == 0:
                            pe.wait_ge(s["nh_v"], 2 * itn + g + 1)
                            pe.wait_ge(s["m32_a"], 2 * itn + g + 1)
                        else:
                            pe.wait_ge(s["m_a"], NL * itn + 2 * (lv - 1) + g + 1)
                        if 1 <= lv < LEVELS:
                            pe.wait_ge(s["n_a"], (NL - 2) * itn + 2 * (lv - 1) + g + 1)
                        if lv < LEVELS - 1:
                            for j in range(G):
                                ins = MM(bank[2 * g][0:L, L * j:L * j + L], Mh[cur][:, G * g + j, :], Nh[cur][:, G * g + j, :], start=True, stop=True)
                            ins.then_inc(s["n2_ps"], 1)
                        if lv < LEVELS:
                            for j in range(G):
                                ins = MM(bank[2 * g + 1][0:L, L * j:L * j + L], Nh[cur][:, G * g + j, :], Mh[cur][:, G * g + j, :], start=True, stop=True)
                            ins.then_inc(s["m2_ps"], 1)
                        if lv >= 1:
                            if lv == 1:
                                pe.wait_ge(s["rh_p"], 2 * itn + g + 1)
                            if lv > 1 or g == 1:
                                pe.wait_ge(s["r_v"], NL * itn + 2 * (lv - 1) + g)
                            for j in range(G):
                                ins = MM(bank[4][0:L, L * j:L * j + L], Mh[cur][:, G * g + j, :], Rh[1 - cur][:, G * g + j, :], start=True, stop=True)
                            ins.then_inc(s["rr_ps"], 1)

                    def y(g):
                        pe.wait_ge(s["wn_v"], 2 * it + g + 1)
                        pe.wait_ge(s["rf_v"], 2 * it + g + 1)
                        for j in range(G):
                            h = G * g + j
                            ins = MM(bank[6 + g][:, P * j:P * j + P], R[:, h, :], Wn[:, h, :], start=True, stop=True)
                        ins.then_inc(s["y_ps"], 1)

                    def outer(g):
                        pe.wait_ge(s["y_a"], 2 * it + g + 1)
                        for j in range(G):
                            h = G * g + j
                            ins = MM(bank[6 + g][:, P * j:P * j + P], Ks[:, h, :], Y[0:L, h, :], start=True, stop=True)
                        ins.then_inc(s["su_ps"], 1)

                    def rows(src, g, done):
                        for j in range(G):
                            ins = pe.transpose(bank[6 + g][0:L, P * j:P * j + P], src[:, G * g + j, 0:L], ident[:])
                        ins.then_inc(done, 1)

                    def from_state(g):
                        pe.wait_ge(s["S_v"], (2 * CH + 2) * b + 2 * n + g + 1)
                        pe.wait_ge(s["ks_v"], 2 * itn + g + 1)
                        for j in range(G):
                            h = G * g + j
                            ins = MM(bank[6 + g][:, P * j:P * j + P], kqn[:, h, :], S[:, h, :], start=True, stop=True)
                        ins.then_inc(s["st_ps"], 1)

                    for g in range(2):
                        if state:
                            y(g)
                        level(0, g)
                    for g in range(2):
                        if state:
                            outer(g)
                        level(1, g)
                    if state:
                        pe.wait_ge(s["oT_v"], it + 1)
                        for h in range(H):
                            o = TOK * (h % G)
                            ins = MM(bank[5][o:o + TOK, P * (h // G):P * (h // G) + P], x[:, h, L:P], Y[:, h, :], start=True, stop=True)
                        ins.then_inc(s["o_ps"], 1)
                    level(2, 0)
                    if stage:
                        if state:
                            pe.wait_ge(s["so_a"], 2 * it + 2)
                        norms_k(m)
                    level(2, 1)
                    if stage:
                        norms_q(m)
                    if inverse:
                        pe.wait_ge(s["vsilu_a"], NHH * itn + NHH)
                        for g in range(2):
                            pe.wait_ge(s["S_v"], (2 * CH + 2) * b + 2 * n + g + 1)
                            rows(VT, g, s["vt_ps"])
                            level(3, g)
                        for g in range(2):
                            pe.wait_ge(s["vn_a"], 2 * itn + g + 1)
                            rows(kqn, g, s["kt_ps"])
                            level(4, g)
                        for g in range(2):
                            level(5, g)
                            if stage:
                                dots(m, par, g)
                        for g in range(2):
                            from_state(g)
                            level(6, g)
                    if state:
                        pe.wait_ge(s["on_a"], 2 * it + 2)
                        for j in range(2):
                            ins = pe.transpose(bank[5][:, P * j:P * j + P], On[:, j, :], ident[:])
                        ins.then_inc(s["ot_ps"], 1)
                    if inverse:
                        eye_h = ident_h[0:L, 0:L]
                        for g in range(2):
                            pe.wait_ge(s["r_v"], NL * itn + NL - 2 + g + 1)
                            for j in range(G):
                                o = bank[2 * g + 1][0:L, L * j:L * j + L]
                                MM(o, M32[:, G * g + j, :], R0[:, G * g + j, :], start=True, stop=False)
                                ins = MM(o, eye_h, eye_h, start=False, stop=True)
                            ins.then_inc(s["ar_ps"], 1)
                        for g in range(2):
                            if g == 1:
                                pe.wait_ge(s["rt_a"], 2 * itn + 1)
                            for j in range(G):
                                ins = pe.transpose(bank[4][0:L, L * j:L * j + L], R0[:, G * g + j, :], ident[0:L, 0:L])
                            ins.then_inc(s["rt_ps"], 1)
                            if stage:
                                x_rows(m, par, g)
                        for g in range(2):
                            pe.wait_ge(s["er_v"], 2 * itn + g + 1)
                            pe.wait_ge(s["rt_a"], 2 * itn + g + 1)
                            for j in range(G):
                                ins = MM(bank[2 * g + 1][0:L, L * j:L * j + L], R0T[:, G * g + j, :], Er[:, G * g + j, :], start=True, stop=True)
                            ins.then_inc(s["re_ps"], 1)

                pe.wait_ge(s["beta_s_v"], b + 1)
                pe.wait_ge(s["eseg_a"], 4 * b + 4)
                norms_k(0)
                norms_q(0)
                for g in range(2):
                    dots(0, 0, g)
                for g in range(2):
                    x_rows(0, 0, g)
                step(-1, 1, state=False)
                with pe.Fori(0, CH // 2 - 1) as cc:
                    step(2 * cc, 0)
                    step(2 * cc + 1, 1)
                step(CH - 2, 0, stage=False)
                step(CH - 1, 1, inverse=False, stage=False)

                pe.wait_ge(s["oT_v"], CH * b + CH + 1)
                for t in range(TT):
                    for h in range(H):
                        ins = MM(bank[6 + t][:, 0:D], oT[:, h, P * t:P * t + P], w_o[:, h, :], start=(h == 0), stop=(h == H - 1))
                    ins.then_inc(s["ao_ps"], 1)

                pe.wait_ge(s["ctx_in"], 16 * b + 16)
                for k in range(KC):
                    ins = pe.transpose(bank[2][:, SK * k:SK * k + SK], ctx_sb[:, P * k:P * k + P], ident[0:SK, 0:SK])
                ins.then_inc(s["ctxT_ps"], 1)
                pe.wait_ge(s["ctxT_a"], b + 2)
                for g in range(XG):
                    for k in range(KC):
                        ins = MM(bank[3][:, SK * g:SK * g + SK], xwk[:, k, P * g:P * g + P], ctxT[:, k, :], start=(k == 0), stop=(k == KC - 1))
                ins.then_inc(s["kx_ps"], 1)
                for k in range(KC):
                    ins = MM(bank[5][0:SK, 0:D], ctxT[:, k, :], xwv[:, k, :], start=(k == 0), stop=(k == KC - 1))
                ins.then_inc(s["vx_ps"], 1)
                pe.wait_ge(s["x1_v"], 2 * b + 4)
                for k in range(KC):
                    for t in range(TT):
                        ins = pe.transpose(bank[0][:, T * k + P * t:T * k + P * t + P], x1[:, t, P * k:P * k + P], ident[:])
                ins.then_inc(s["x1T_ps"], 1)
                pe.wait_ge(s["x1T_a"], b + 1)
                for q in range(2):
                    for j in range(2):
                        g = 2 * q + j
                        for k in range(KC):
                            ins = MM(bank[6 + q][:, T * j:T * j + T], xwq[:, k, P * g:P * g + P], x1T[:, k, :], start=(k == 0), stop=(k == KC - 1))
                    ins.then_inc(s["qx_ps"], 1)
                pe.wait_ge(s["kx_a"], b + 1)
                pe.wait_ge(s["vx_v"], b + 1)
                pe.wait_ge(s["qx_a"], 2 * b + 2)
                for t in range(TT):
                    for g in range(XG):
                        for j in range(XG):
                            r = slice(32 * j, 32 * j + 32)
                            ins = MM(bank[XG * t + j][:, SK * g:SK * g + SK], qTx[r, g, P * t:P * t + P], kTx[r, g, :], start=True, stop=True)
                            if g == XG - 1:
                                ins.then_inc(s["sc_ps"], 1)
                pe.wait_ge(s["qk_a"], 8 * b + 8)
                pe.wait_ge(s["var_v"], 3 * b + 3)
                for f in range(3):
                    for t in range(TT):
                        ins = MM(bank[0][0:64, 0:XH], tw1[:, f, :], stat[:, f, XH * t:XH * t + XH], start=(f + t == 0), stop=(f == 2 and t == TT - 1))
                ins.then_inc(s["h1_ps"], 1)
                pe.wait_ge(s["h1_a"], b + 1)
                MM(bank[1][:, 0:XH], tw2[:], h1[:], start=True, stop=True).then_inc(s["h2_ps"], 1)
                pe.wait_ge(s["h2_a"], b + 1)
                MM(bank[2][:, 0:XH], tw3b[:], h2[:], start=True, stop=True).then_inc(s["h3_ps"], 1)
                pe.wait_ge(s["e2_a"], b + 1)
                for q in range(8):
                    for j in range(XG):
                        ins = pe.transpose(bank[q][0:SK, P * j:P * j + P], ex[:, XG * q + j, :], ident[:])
                    ins.then_inc(s["eT_ps"], 1)
                for t in range(TT):
                    pe.wait_ge(s["eT_v"], 8 * b + XG * t + XG)
                    for h in range(XH):
                        ins = MM(bank[XG * t][:, DK * h:DK * h + DK], exT[:, XH * t + h, :], vx[:, DK * h:DK * h + DK], start=True, stop=True)
                    ins.then_inc(s["av_ps"], 1)
                pe.wait_ge(s["ao_v"], 2 * b + 2)
                for k in range(KC):
                    for t in range(TT):
                        ins = pe.transpose(bank[1][:, T * k + P * t:T * k + P * t + P], ao[:, t, P * k:P * k + P], ident[:])
                ins.then_inc(s["aoT_ps"], 1)
                pe.wait_ge(s["aoT_a"], b + 1)
                for t in range(TT):
                    for k in range(KC):
                        ins = MM(bank[2 + t][:, 0:D], aoT[:, k, P * t:P * t + P], xwo[:, k, :], start=(k == 0), stop=(k == KC - 1))
                    ins.then_inc(s["x2_ps"], 1)

                pe.wait_ge(s["x2_v"], 2 * b + 2)
                for k in range(KC):
                    for t in range(TT):
                        ins = pe.transpose(bank[4][:, T * k + P * t:T * k + P * t + P], x2[:, t, P * k:P * k + P], ident[:])
                ins.then_inc(s["x2T_ps"], 1)
                pe.wait_ge(s["x2T_a"], b + 1)
                pe.wait_ge(s["w_in0"], 16 * (STREAM // 2) * (b + 1))
                for q, bk in enumerate((0, 1, 6, 7)):
                    for j in range(2):
                        f = 2 * q + j
                        for k in range(KC):
                            ins = MM(bank[bk][:, T * j:T * j + T], fw1[:, k, P * f:P * f + P], x2T[:, k, :], start=(k == 0), stop=(k == KC - 1))
                    ins.then_inc(s["hid_ps"], 1)
                pe.wait_ge(s["act_v"], b + 1)
                pe.wait_ge(s["w_in1"], 16 * (STREAM // 2) * (b + 1))
                for t in range(TT):
                    for f in range(FT):
                        ins = MM(bank[2 + t][:, 0:D], arg[:, f, P * t:P * t + P], fw2[:, f, :], start=(f == 0), stop=(f == FT - 1))
                    ins.then_inc(s["x3_ps"], 1)

        @block.vector
        def _(v):
            v.memset(x1[:, 0, :], 0.0).then_inc(s["x1_v"], 1)
            v.memset(x1[:, 1, :], 0.0).then_inc(s["x1_v"], 1)
            v.memset(x3[:, 0, :], 0.0).then_inc(s["x3_v"], 1)
            v.memset(x3[:, 1, :], 0.0).then_inc(s["x3_v"], 1)
            v.memset(oT[:, 0, :], 0.0).then_inc(s["oT_v"], 1)
            v.memset(co[:, 0, :], 0.0).then_inc(s["conv_v"], 1)
            v.memset(rs_x[:], 1.0)
            v.wait_ge(s["const"], ALL_CONST)

            def turns_off(x, y, sem_, at, add=0.0):
                v.tensor_scalar(y, x, 1 / TWO_PI, MAGIC, ALU.mult, ALU.add).then_inc(sem_, 1)
                v.wait_ge(sem_, at + 1)
                v.tensor_scalar(y, y, MAGIC, -TWO_PI, ALU.subtract, ALU.mult).then_inc(sem_, 1)
                v.wait_ge(sem_, at + 2)
                v.tensor_tensor(x, x, y, ALU.add).then_inc(sem_, 1)
                v.wait_ge(sem_, at + 3)
                v.tensor_scalar(x, x, PI_BELOW, -PI_BELOW, ALU.min, ALU.max).then_inc(sem_, 1)

            def rsqrt(x, y, tmp, sem_, at, steps=range(RS)):
                xi, yi = x.bitcast(mybir.dt.int32), y.bitcast(mybir.dt.int32)
                for k in steps:
                    if k == 0:
                        v.tensor_scalar(yi, xi, 1, None, ALU.logical_shift_right).then_inc(sem_, 1)
                        continue
                    v.wait_ge(sem_, at + k)
                    if k == 1:
                        v.tensor_scalar(yi, yi, -1.0, float(0x5F3759DF), ALU.mult, ALU.add).then_inc(sem_, 1)
                    elif k % 3 == 2:
                        v.tensor_tensor(tmp, y, y, ALU.mult).then_inc(sem_, 1)
                    elif k % 3 == 0:
                        v.scalar_tensor_tensor(tmp, tmp, -0.5, x, ALU.mult, ALU.mult).then_inc(sem_, 1)
                    else:
                        v.scalar_tensor_tensor(y, tmp, 1.5, y, ALU.add, ALU.mult).then_inc(sem_, 1)
                if steps[-1] == RS - 1:
                    v.wait_ge(sem_, at + RS)

            v.tensor_copy(turn[:, 0:FT], theta[:])
            v.tensor_scalar(turn[:, FT:2 * FT], theta[:], float(np.pi / 2), None, ALU.add).then_inc(s["setup_v"], 1)
            v.wait_ge(s["setup_v"], 1)
            turns_off(turn[:], trig[:], s["setup_v"], 1)
            for f, m in enumerate((DK ** -0.5 / (T * SK), DK ** -0.5 / T, 1.0 / T)):
                v.tensor_scalar(tw1[:, f, :], tw1[:, f, :], m, None, ALU.mult)
            v.tensor_copy(tw3b[:], tw3[:].to_broadcast([64, P]))
            v.wait_ge(s["setup_a"], 2)
            v.tensor_scalar(neg_a[:], neg_a[:], -1.0, None, ALU.mult).then_inc(s["setup_v"], 1)
            v.tensor_tensor(turn[:, 0:FT], trig[:, FT:2 * FT], w_re[:], ALU.mult).then_inc(s["setup_v"], 1)
            v.tensor_tensor(turn[:, FT:2 * FT], trig[:, 0:FT], w_im[:], ALU.mult).then_inc(s["setup_v"], 1)
            v.wait_ge(s["setup_v"], 8)
            v.tensor_tensor(turn[:, 0:FT], turn[:, 0:FT], turn[:, FT:2 * FT], ALU.add).then_inc(s["setup_v"], 1)
            v.wait_ge(s["setup_v"], 9)
            v.scalar_tensor_tensor(coef[:], turn[:, 0:FT], 0.1, w_im[:], ALU.mult, ALU.mult).then_inc(s["setup_v"], 1)
            v.wait_ge(s["setup_v"], 10)
            v.wait_ge(s["setup_p"], 2)
            for x in X:
                v.tensor_copy(x[L:P, :, L:P], ident[L:P, L:P].unsqueeze(1).to_broadcast([TOK, H, TOK]))
            v.tensor_copy(R[L:P, :, L:P], ident[L:P, L:P].unsqueeze(1).to_broadcast([TOK, H, TOK]))

            with v.Fori(0, BATCHES) as b:
                v.wait_ge(s["ab_ps"], b + 1)
                v.wait_ge(s["eb_a"], 3 * b + 1)
                ab = bank[7][0:TOK, 0:CH * 4 * H].rearrange("m (c k) -> m c k", k=4 * H)
                v.tensor_tensor(zdec[:], ab[:, :, 0:H], dt_b[:].unsqueeze(1).to_broadcast([TOK, CH, H]), ALU.add).then_inc(s["zdec_v"], 1)
                v.wait_ge(s["zdec_v"], 2 * b + 1)
                v.scalar_tensor_tensor(zabs[:], zdec[:], -1.0, zdec[:], ALU.mult, ALU.max).then_inc(s["zdec_v"], 1)
                v.tensor_scalar(beta[:], beta[:], 1.0, 0.5, ALU.add, ALU.mult).then_inc(s["ab_used"], 1)
                v.wait_ge(s["ab_used"], b + 1)
                v.reciprocal(beta[:], beta[:]).then_inc(s["beta_v"], 1)
                v.wait_ge(s["eb_a"], 3 * b + 3)
                v.scalar_tensor_tensor(gdec[:], zdec[:], 0.0, zabs[:], ALU.max, ALU.add).then_inc(s["beta_v"], 1)
                v.wait_ge(s["beta_v"], 2 * b + 2)
                v.tensor_tensor(gdec[:], gdec[:], neg_a[:].unsqueeze(1).to_broadcast([TOK, CH, H]), ALU.mult).then_inc(s["gate_v"], 1)

                def conv(n, e):
                    v.wait_ge(s["raw_a"], PARTS * BANKS * b + BANKS * n + BANKS)
                    for i in range(CONV):
                        for j in range(H):
                            tile = (n - 1) * H + j
                            o = co[:, tile, :] if isinstance(tile, int) else co[:, bass.ds(tile, 1), :].rearrange("p o t -> p (o t)")
                            w = conv_w[:, tile, i:i + 1] if isinstance(tile, int) else conv_w[:, bass.ds(tile, 1), i:i + 1].rearrange("p o t -> p (o t)")
                            src = raw[e][:, j, i:i + T]
                            if i == 0:
                                ins = v.tensor_scalar(o, src, w, None, ALU.mult)
                            else:
                                v.wait_ge(s["tap_v"], CONV * H * (PARTS - 1) * b + CONV * H * (n - 1) + H * (i - 1) + j + 1)
                                ins = v.scalar_tensor_tensor(o, src, w, o, ALU.mult, ALU.add)
                            ins.then_inc(s["tap_v"], 1)
                    v.wait_ge(s["tap_v"], CONV * H * (PARTS - 1) * b + CONV * H * n)
                    v.tensor_copy(ms[:, 0:1], ones[:, 0:1]).then_inc(s["conv_v"], 1)

                v.memset(raw_all[:, :, :, 0:CONV - 1].rearrange("p a h t -> p (a h) t"), 0.0).then_inc(s["pad_v"], 1)
                v.wait_ge(s["pad_v"], b + 1)
                conv(1, 1)
                with v.Fori(0, (PARTS - 2) // 2) as pp:
                    for e in range(2):
                        conv(2 * pp + 2 + e, e)
                v.wait_ge(s["norm_ps"], (CH + 1) * b + 1)
                v.tensor_copy(beta_s[:], bank[5][0:L, 0:CH * H]).then_inc(s["beta_s_v"], 1)
                for g in range(2):
                    v.memset(S[:, G * g:G * g + G, :], 0.0).then_inc(s["S_v"], 1)

                def roots_in(m, par):
                    cs = bass.ds(m * H, H)
                    k = 4 * (CH * b + m)
                    at = 2 * P
                    v.wait_ge(s["norm_ps"], (CH + 1) * b + m + 2)
                    v.tensor_scalar(rs_x[0:L, 0:H], bank[5][0:L, at:at + H], 1e-6, None, ALU.add).then_inc(s["norm_v"], 1)
                    v.tensor_scalar(epsq[par][:], bank[5][:, at + H:at + H + 2], DH * LN_EPS, DH * LN_EPS * 1e-6, ALU.mult, ALU.add)
                    v.wait_ge(s["norm_v"], k + 1)
                    v.reciprocal(inv[:], rs_x[0:L, 0:H]).then_inc(s["norm_v"], 1)
                    v.wait_ge(s["norm_v"], k + 2)
                    v.scalar_tensor_tensor(bneg[par][:], inv[:], -1.0, beta_s[:, cs], ALU.mult, ALU.mult).then_inc(s["norm_v"], 1)
                    v.wait_ge(s["norm_v"], k + 3)
                    v.tensor_tensor(kend[par][:], bneg[par][:], e_out[:, cs], ALU.mult).then_inc(s["norm_v"], 1)

                def key_norms(par):
                    v.tensor_tensor(vnorm[par][:], rs_x[0:L, 0:H], rs_y[0:L, 0:H], ALU.mult).then_inc(s["vnorm_v"], 1)

                def n_and_weights(m, par, g):
                    itm = CH * b + m
                    v.wait_ge(s["dd_p"], 2 * itm + 2)
                    v.wait_ge(s["p1_ps"], 2 * itm + g + 1)
                    for j in range(G):
                        h = G * g + j
                        ins = v.scalar_tensor_tensor(X[par][0:L, h, :], bank[2 * g][0:L, P * j:P * j + P], bneg[par][:, h:h + 1], DD[:, h, :],
                                                     ALU.mult, ALU.mult)
                    ins.then_inc(s["x_v"], 1)
                    v.wait_ge(s["x_v"], 2 * itm + g + 1)
                    v.tensor_copy(Nh[0][:, G * g:G * g + G, :], X[par][0:L, G * g:G * g + G, 0:L]).then_inc(s["nh_v"], 1)

                def step(c, par, state=True, inverse=True, stage=True):
                    n, m = c + 1, c + 2
                    it, itn = CH * b + c, CH * b + n
                    at = RS * ((CH + 2) * b + c + 2)
                    roots = rs_x[:], rs_y[:], rs_t[:], s["rs_c_v"], at

                    def wn(g):
                        v.wait_ge(s["st_ps"], 2 * it + g + 1)
                        v.wait_ge(s["vn_a"], 2 * it + g + 1)
                        for j in range(G):
                            h = G * g + j
                            ins = v.scalar_tensor_tensor(Wn[:, h, :], bank[6 + g][:, P * j:P * j + P], e_in[:, 0, bass.ds(c * H + h, 1)], Vn[:, h, :],
                                                         ALU.mult, ALU.subtract)
                        ins.then_inc(s["wn_v"], 1)

                    def new_state(g):
                        v.wait_ge(s["su_ps"], 2 * it + g + 1)
                        for j in range(G):
                            h = G * g + j
                            ins = v.scalar_tensor_tensor(S[:, h, :], S[:, h, :], e_in[:, 1, bass.ds(c * H + h, 1)], bank[6 + g][:, P * j:P * j + P],
                                                         ALU.mult, ALU.add)
                        ins.then_inc(s["S_v"], 1)

                    def level(lv, g):
                        hs = slice(G * g, G * g + G)
                        v.wait_ge(s["rr_ps"], NL * itn + 2 * (lv - 1) + g + 1)
                        dst = Rh[lv % 2] if lv < LEVELS else R0
                        v.tensor_tensor(dst[:, hs, :], bank[4][0:L, 0:G * L].rearrange("r (h s) -> r h s", s=L),
                                        Rh[(lv - 1) % 2][:, hs, :], ALU.add).then_inc(s["r_v"], 1)

                    if state:
                        wn(0)
                        wn(1)
                    for g in range(2):
                        if state:
                            new_state(g)
                        if inverse:
                            level(1, g)
                    if inverse:
                        level(2, 0)
                        level(2, 1)
                    if state:
                        v.wait_ge(s["so_a"], 2 * it + 2)
                        v.scalar_tensor_tensor(rs_x[:, H:H + 2], so[:], 1.0 / DH, epsq[par][:], ALU.mult, ALU.add).then_inc(s["rs_in_v"], 1)
                        v.wait_ge(s["rs_in_v"], it + 1)
                    if stage:
                        roots_in(m, par)
                    rsqrt(*roots, range(0, 3))
                    if inverse:
                        level(3, 0)
                    rsqrt(*roots, range(3, 5))
                    if inverse:
                        level(3, 1)
                    rsqrt(*roots, range(5, 7))
                    if inverse:
                        for g in range(2):
                            hs = slice(G * g, G * g + G)
                            level(4, g)
                            v.wait_ge(s["kt_ps"], 2 * itn + g + 1)
                            v.tensor_tensor(Ks[:, hs, :], bank[6 + g][0:L, :].rearrange("r (h d) -> r h d", d=P),
                                            kend[1 - par][:, hs].unsqueeze(2).to_broadcast([L, G, P]), ALU.mult).then_inc(s["ks_v"], 1)
                    rsqrt(*roots, range(7, RS))
                    if state:
                        v.tensor_copy(rstd[:], rs_y[:, H:H + 2]).then_inc(s["rstd_v"], 1)
                    if stage:
                        key_norms(par)
                    if inverse:
                        for g in range(2):
                            level(5, g)
                            if stage:
                                n_and_weights(m, par, g)
                        for g in range(2):
                            level(6, g)
                        for g in range(2):
                            hs = slice(G * g, G * g + G)
                            v.wait_ge(s["ar_ps"], 2 * itn + g + 1)
                            v.tensor_tensor(Er[:, hs, :], bank[2 * g + 1][0:L, 0:G * L].rearrange("r (h s) -> r h s", s=L), R0[:, hs, :],
                                            ALU.subtract).then_inc(s["er_v"], 1)
                    if state:
                        v.wait_ge(s["ot_ps"], it + 1)
                        tk = bass.ds(c * TOK, TOK)
                        v.scalar_tensor_tensor(oT[:, :, tk], bank[5][:, 0:2 * P].rearrange("p (h t) -> p h t", t=TOK), rms_w[:], gate[:, :, tk],
                                               ALU.mult, ALU.mult).then_inc(s["oT_v"], 1)
                    if inverse:
                        for g in range(2):
                            hs = slice(G * g, G * g + G)
                            v.wait_ge(s["re_ps"], 2 * itn + g + 1)
                            v.tensor_tensor(R[0:L, hs, 0:L], bank[2 * g + 1][0:L, 0:G * L].rearrange("r (h s) -> r h s", s=L), R0[:, hs, :],
                                            ALU.add).then_inc(s["rf_v"], 1)

                v.wait_ge(s["gsum_a"], 2 * b + 2)
                v.wait_ge(s["beta_s_v"], b + 1)
                roots_in(0, 0)
                first = RS * (CH + 2) * b
                rsqrt(rs_x[:], rs_y[:], rs_t[:], s["rs_c_v"], first)
                key_norms(0)
                n_and_weights(0, 0, 0)
                n_and_weights(0, 0, 1)
                step(-1, 1, state=False)
                with v.Fori(0, CH // 2 - 1) as cc:
                    step(2 * cc, 0)
                    step(2 * cc + 1, 1)
                step(CH - 2, 0, stage=False)
                step(CH - 1, 1, inverse=False, stage=False)

                def layer_norm(k, psum, skip, dst, done, ready, skip_ready=None):
                    n = 3 * b + k
                    for t in range(TT):
                        if skip_ready:
                            v.wait_ge(skip_ready, TT * b + t + 1)
                        v.wait_ge(ready[0], ready[1] + t)
                        v.tensor_tensor(yln[:, t, :], psum[t], skip[:, t, :], ALU.add).then_inc(s["yln_v"], 1)
                    for t in range(TT):
                        v.wait_ge(s["yln_v"], TT * n + t + 1)
                        v.bn_stats(bst[:, t, :], yln[:, t, :]).then_inc(s["bst_v"], 1)
                    v.wait_ge(s["bst_v"], TT * n + TT)
                    v.tensor_copy(ms[:], ones[:, 0:2])
                    for t in range(TT):
                        v.bn_aggr(mv[:, t, :], bst[:, t, :]).then_inc(s["mv_v"], 1)
                    v.wait_ge(s["mv_v"], TT * n + TT)
                    v.tensor_scalar(lnr[:], mv[:, :, 1], LN_EPS, None, ALU.add).then_inc(s["ve_v"], 1)
                    v.wait_ge(s["ve_v"], n + 1)
                    rsqrt(lnr[:], rs_y[:, 0:TT], rs_t[:, 0:TT], s["rs_l_v"], RS * n)
                    for t in range(TT):
                        v.tensor_scalar(dst[:, t, :], yln[:, t, :], mv[:, t, 0:1], rs_y[:, t:t + 1], ALU.subtract, ALU.mult).then_inc(done, 1)

                layer_norm(0, [bank[6 + t][:, 0:D] for t in range(TT)], x_tok, x1, s["x1_v"], (s["ao_ps"], 2 * b + 1))

                v.wait_ge(s["vx_ps"], b + 1)
                v.tensor_tensor(vx, bank[5][0:SK, 0:D], xbv[0:SK, :], ALU.add).then_inc(s["vx_v"], 1)
                v.wait_ge(s["qk_a"], 8 * b + 8)
                v.tensor_reduce(stat[:, 0, :], qk, AX.X, ALU.add).then_inc(s["stat_v"], 1)
                v.tensor_reduce(stat[:, 1, :], qk, AX.X, ALU.max).then_inc(s["stat_v"], 1)
                v.wait_ge(s["stat_v"], 2 * b + 2)
                v.tensor_tensor(qk, qk, stat[:, 1, :].unsqueeze(2).to_broadcast([P, ROWS, SK]), ALU.subtract).then_inc(s["d_v"], 1)
                v.wait_ge(s["e1_a"], b + 1)
                v.tensor_reduce(s_1[:], ex, AX.X, ALU.add).then_inc(s["s1_v"], 1)
                v.wait_ge(s["s1_v"], b + 1)
                v.reciprocal(r_1[:], s_1[:]).then_inc(s["r1_v"], 1)
                v.wait_ge(s["esq_p"], b + 1)
                v.tensor_reduce(s_2[:], e_sq, AX.X, ALU.add).then_inc(s["s2_v"], 1)
                v.wait_ge(s["s2_v"], b + 1)
                v.wait_ge(s["r1_v"], b + 1)
                v.tensor_tensor(s_2[:], s_2[:], r_1[:], ALU.mult).then_inc(s["var_v"], 1)
                v.wait_ge(s["var_v"], 3 * b + 1)
                v.tensor_tensor(s_2[:], s_2[:], r_1[:], ALU.mult).then_inc(s["var_v"], 1)
                v.wait_ge(s["var_v"], 3 * b + 2)
                v.tensor_scalar(stat[:, 2, :], s_2[:], 1.0 / SK, 1.0 / (SK - 1), ALU.subtract, ALU.mult).then_inc(s["var_v"], 1)
                v.wait_ge(s["h3_ps"], b + 1)
                v.tensor_scalar(lt[:], bank[2][:, 0:XH], tb3[:], LOG_T_MAX, ALU.add, ALU.min).then_inc(s["lt_v"], 1)
                v.wait_ge(s["lt_v"], 2 * b + 1)
                v.tensor_scalar(lt[:], lt[:], LOG_T_MIN, None, ALU.max).then_inc(s["lt_v"], 1)
                v.wait_ge(s["it_a"], b + 1)
                v.tensor_scalar(inv_t[:], inv_t[:], 0.5, None, ALU.mult).then_inc(s["it_v"], 1)
                v.wait_ge(s["it_v"], b + 1)
                for t in range(TT):
                    rs = slice(XH * t, XH * t + XH)
                    ins = v.tensor_tensor(qk[:, rs, :], qk[:, rs, :], inv_t[:].unsqueeze(2).to_broadcast([P, XH, SK]), ALU.mult)
                ins.then_inc(s["d2_v"], 1)
                v.wait_ge(s["e2_a"], b + 1)
                v.tensor_reduce(s_1[:], ex, AX.X, ALU.add).then_inc(s["se_v"], 1)
                v.wait_ge(s["se_v"], b + 1)
                v.reciprocal(r_1[:], s_1[:]).then_inc(s["rinv_v"], 1)
                v.wait_ge(s["rinv_v"], 2 * b + 1)
                v.tensor_scalar(r_1[:], r_1[:], 0.0, None, ALU.max).then_inc(s["rinv_v"], 1)
                for q in range(8):
                    v.wait_ge(s["eT_ps"], 8 * b + q + 1)
                    v.tensor_scalar(exT[:, XG * q:XG * q + XG, :].rearrange("k r q -> k (r q)"), bank[q][0:SK, :], 0.0, None, ALU.max).then_inc(s["eT_v"], 1)
                v.wait_ge(s["rinv_v"], 2 * b + 2)
                for t in range(TT):
                    v.wait_ge(s["av_ps"], 2 * b + t + 1)
                    v.tensor_tensor(ao[:, t, :].rearrange("p (h d) -> p h d", d=DK), bank[XG * t][:, 0:D].rearrange("p (h d) -> p h d", d=DK),
                                    r_1[:, XH * t:XH * t + XH].unsqueeze(2).to_broadcast([P, XH, DK]), ALU.mult).then_inc(s["ao_v"], 1)
                layer_norm(1, [bank[2 + t][:, 0:D] for t in range(TT)], x1b, x2, s["x2_v"], (s["x2_ps"], 2 * b + 1), s["x1b_p"])

                for q in range(4):
                    v.wait_ge(s["hid_a"], 4 * b + q + 1)
                    for f in (2 * q, 2 * q + 1):
                        v.tensor_scalar(arg[:, f, :], hid[:, f, :], 0.1, theta[:, f:f + 1], ALU.mult, ALU.add).then_inc(s["arg_v"], 1)
                v.wait_ge(s["arg_v"], FT * b + FT)
                turns_off(arg, rnd, s["rnd_v"], 4 * b)
                v.wait_ge(s["sin_a"], b + 1)
                for f in range(FT):
                    v.scalar_tensor_tensor(hid[:, f, :], rnd[:, f, :], coef[:, f:f + 1], hid[:, f, :], ALU.mult, ALU.add).then_inc(s["q_v"], 1)
                v.wait_ge(s["q_v"], FT * b + FT)
                v.tensor_scalar(arg, hid, 0.0, None, ALU.max).then_inc(s["act_v"], 1)
                layer_norm(2, [bank[2 + t][:, 0:D] for t in range(TT)], x2b, x3, s["x3_v"], (s["x3_ps"], 2 * b + 3), s["x2b_p"])


def rows_to_tiles(w):
    return w.reshape(w.shape[0] // P, P, w.shape[1]).transpose(1, 0, 2)


def padded_heads(w):
    o = np.zeros((w.shape[0], XG, XG, 32), np.float32)
    o[..., :DK] = w.reshape(w.shape[0], XG, XG, DK).transpose(0, 2, 1, 3)
    return o.reshape(w.shape[0], XH * 32)


def lay_out(i):
    f = {k: np.asarray(v, np.float32) if np.asarray(v).dtype == np.float32 else np.asarray(v) for k, v in i.items()}
    d, x, n = "L0_attn_", "L0_xattn_", "L0_ffn_"
    k, v = f[d + "Wk"], f[d + "Wv"]
    parts = [f[d + "Wg"], f[d + "Wq"]] + [w[:, H * DH * j:H * DH * (j + 1)] for w in (k, v) for j in range(NHH)]
    taps = np.concatenate([f[d + "conv_q"], f[d + "conv_k"], f[d + "conv_v"]])
    cols = lambda u: u.reshape(-1, P).T
    a = {
        "x": f["x"], "ctx": f["ctx_1024"],
        "w_parts": np.stack([rows_to_tiles(w) for w in parts] + [
            rows_to_tiles(f[n + "W1"]), rows_to_tiles(f[n + "W2"]).reshape(P, KC, H * DH)]),
        "conv_w": taps.reshape(-1, P, CONV).transpose(1, 0, 2),
        "w_ab": rows_to_tiles(np.concatenate([f[d + "Wa"], f[d + "Wb"]], 1)),
        "w_o": rows_to_tiles(f[d + "Wo"]), "rms_w": f[d + "rms_weight"][:, None],
        "A_log": f[d + "A_log"], "dt_bias": f[d + "dt_bias"],
        "xwq": rows_to_tiles(padded_heads(f[x + "Wq"].T)), "xwk": rows_to_tiles(padded_heads(f[x + "Wk"].T)),
        "xbq": cols(padded_heads(f[x + "bq"][None])[0]), "xbk": cols(padded_heads(f[x + "bk"][None])[0]),
        "xwv": rows_to_tiles(f[x + "Wv"].T), "xwo": rows_to_tiles(f[x + "Wo"].T),
        "xbv": f[x + "bv"], "xbo": f[x + "bo"], "fb2": f[n + "b2"],
        "tw1": f[x + "w1"].T, "tb1": f[x + "b1"][:, None], "tw2": np.pad(f[x + "w2"].T, ((0, 0), (0, P - 64))), "tb2": f[x + "b2"][:, None],
        "tw3": f[x + "w3"].T, "tb3": f[x + "b3"],
        "fb1": cols(f[n + "b1"]),
        "theta": cols(f[n + "quantum_phases"]), "w_re": cols(f[n + "quantum_weights_real"]),
        "w_im": cols(f[n + "quantum_weights_imag"]),
    }
    a |= {"c_" + key: w for key, w in shape_constants().items()}
    return {key: np.ascontiguousarray(w) for key, w in a.items()}


def kernel(**inputs):
    import concourse.bacc as bacc
    from concourse.bass_utils import run_bass_kernel_spmd

    nc = bacc.Bacc("TRN2", target_bir_lowering=False, num_devices=1)
    arrays = lay_out(inputs)
    aps = {k: nc.dram_tensor(f"in_{k}", w.shape, mybir.dt.from_np(w.dtype), kind="ExternalInput").ap() for k, w in arrays.items()}
    out = nc.dram_tensor("out_x", (BATCHES, T, D), F32, kind="ExternalOutput").ap()
    build(nc, aps, out)
    r = run_bass_kernel_spmd(nc, [{f"in_{k}": w for k, w in arrays.items()}], core_ids=[0])
    return r.results[0]["out_x"]
```

```python
from contextlib import ExitStack

import numpy as np
import concourse.bass as bass
from concourse import mybir

F32, F16 = mybir.dt.float32, mybir.dt.float16
ALU, ACT, AX = mybir.AluOpType, mybir.ActivationFunctionType, mybir.AxisListType

P = 128
BATCHES, T, D = 16, 256, 256
TT, KC = T // P, D // P
H, DH, NHH = 8, 128, 3
TOK = 32
CH = T // TOK
L = TOK * NHH
G = H // 2
PARTS = 1 + 2 * NHH + 1
STREAM = PARTS + 2
CONV = 4
ADDS = CONV - 1
POOL_TILES = 2
LEVELS = 6
XH, DK, SK = 16, 16, 77
XG = 4
FF = 1024
FT = FF // P
LN_EPS = 1e-5
MAGIC = float(1.5 * 2 ** 23)
RS = 11
TWO_PI = 2 * float(np.pi)
PI_BELOW = 3.1415925
LOG_T_MIN, LOG_T_MAX = float(np.log(0.1)), float(np.log(10.0))


def shape_constants():
    s, m, t = np.arange(L), np.arange(TOK)[:, None], np.arange(TOK)
    tok = s // NHH
    out = {
        "ident": np.eye(P),
        "after": m > tok[None],
        "upto": np.concatenate([m <= tok[None], m <= t[None]], 1),
        "strict": s[:, None] < s[None],
        "causal": tok[:, None] <= t[None],
        "spread": np.concatenate([s[None] == NHH * m + i for i in range(NHH)], 1),
        "ones": np.ones((P, P)),
    }
    return {k: v.astype(np.float32) for k, v in out.items()}


def build(nc, a, out):
    const = shape_constants()
    ctx = ExitStack()
    with ctx:
        def sb(name, shape, dt=F32):
            return ctx.enter_context(nc.sbuf_tensor(name, shape, dt))

        def sem(name):
            return ctx.enter_context(nc.semaphore(name))

        bank = [ctx.enter_context(nc.psum_tensor(f"bank{i}", [P, 512], F32)) for i in range(8)]

        cst = {k: sb(f"c_{k}", list(v.shape)) for k, v in const.items()}
        ident, ones = cst["ident"], cst["ones"]
        ident_h = sb("ident_h", [P, P], F16)
        w_ab = sb("w_ab", [P, KC, 4 * H])
        conv_w = sb("conv_w", [P, (PARTS - 1) * H, CONV])
        w_o = sb("w_o", [P, H, D])
        rms_w = sb("rms_w", [P, 1])
        neg_a = sb("neg_a", [TOK, H])
        dt_b = sb("dt_b", [TOK, H])
        xwq = sb("xwq", [P, KC, XG * P])
        xwk = sb("xwk", [P, KC, XG * P])
        xbq, xbk = sb("xbq", [P, XG]), sb("xbk", [P, XG])
        xwv, xwo = sb("xwv", [P, KC, D]), sb("xwo", [P, KC, D])
        xbv, xbo, fb2 = sb("xbv", [P, D]), sb("xbo", [P, D]), sb("fb2", [P, D])
        tw1, tb1 = sb("tw1", [P, 3, 64]), sb("tb1", [64, 1])
        tw2, tb2 = sb("tw2", [64, P]), sb("tb2", [64, 1])
        tw3, tw3b, tb3 = sb("tw3", [64, 1]), sb("tw3b", [64, P]), sb("tb3", [P, 1])
        fb1 = sb("fb1", [P, FT])
        theta, w_re, w_im = sb("theta", [P, FT]), sb("w_re", [P, FT]), sb("w_im", [P, FT])
        coef, trig, turn = sb("coef", [P, FT]), sb("trig", [P, 2 * FT]), sb("turn", [P, 2 * FT])

        w_part = [sb(f"w_part{i}", [P, KC, H * DH]) for i in range(2)]
        x_tok, xT = sb("x_tok", [P, TT, D]), sb("xT", [P, KC, T])
        fw1, fw2 = w_part[1], w_part[0][:].rearrange("p k (g n) -> p (k g) n", n=D)
        raw_all = sb("raw_all", [P, 2, H, CONV - 1 + T])
        raw = [raw_all[:, i] for i in range(2)]
        co = sb("co", [P, (PARTS - 1) * H, T])
        zdec, zabs, gdec = sb("zdec", [TOK, CH, H]), sb("zabs", [TOK, CH, H]), sb("gdec", [TOK, CH, H])
        beta = sb("beta", [TOK, CH, NHH, H])
        e_in = sb("e_in", [P, 2, CH * H])
        e_out = sb("e_out", [L, CH * H])
        beta_s = sb("beta_s", [L, CH * H])

        space = sb("space", [P, 4 * H * P + 3 * H * L])

        def lay(parts, at, rows=P):
            got = []
            for shape in parts:
                n = int(np.prod(shape))
                u = at[0][0:rows, at[1]:at[1] + n]
                at[1] += n
                got.append(u if len(shape) == 1 else u.rearrange("p (a b) -> p a b", b=shape[1]))
            return got

        at = [space, 0]
        KQ0, KQ1, SQ = lay([(H, P)] * 3, at)
        KQ = [KQ0, KQ1]
        VT, = lay([(H, L)], at)
        DD, = lay([(H, P)], at, L)
        M32, R0 = lay([(H, L)] * 2, at, L)
        HALVES = H * L // 2
        desk = sb("desk", [P, 2 * H * T + 8 * HALVES + CH * H * TOK])
        at = [desk, 0]
        gate, oT = lay([(H, T)] * 2, at)
        halves = []
        for _ in range(8):
            u, = lay([(HALVES,)], at, L)
            halves.append(u.bitcast(F16).rearrange("p (h l) -> p h l", l=L))
        Nh, Mh, Rh = halves[0:2], halves[2:4], halves[4:6]
        R0T, Er = halves[6:8]
        e_seg, = lay([(CH * H, TOK)], at, L)
        r_and_v = sb("r_and_v", [P, 2 * H * P])
        R, Vn = lay([(H, P)] * 2, [r_and_v, 0])
        gtab, = lay([(CH * H, TOK)], [r_and_v, 0], TOK)
        x_both = sb("x_both", [P, 2 * H * P])
        X = lay([(H, P)] * 2, [x_both, 0])
        at = [x_both, 0]
        tap = lay([(POOL_TILES, T)] * (CONV - 1), at)
        x_new, = lay([(TT, D)], at)
        at = [raw_all[:].rearrange("p a h t -> p (a h t)"), 0]
        Wn, Y, S = lay([(H, P)] * 3, at)
        Ks, = lay([(H, P)], at, L)
        inv = sb("inv", [L, H])
        bneg, kend, vnorm = ([sb(f"{n}{i}", [L, H]) for i in range(2)] for n in ("bneg", "kend", "vnorm"))
        epsq, so = [sb(f"epsq{i}", [P, 2]) for i in range(2)], sb("so", [P, 2])
        rs_x, rs_t, rs_y = sb("rs_x", [P, H + 2]), sb("rs_t", [P, H + 2]), sb("rs_y", [P, H + 2])
        rstd, On = sb("rstd", [P, 2]), sb("On", [P, 2, P])
        ms, none = sb("ms", [P, 2]), sb("none", [P, 1])

        at = [space, 0]
        x1, x1b, x2, x2b, yln, ao = lay([(TT, D)] * 6, at)
        x1T, x2T, aoT = lay([(KC, T)] * 3, at)
        qTx, kTx = lay([(XG, T), (XG, SK + 1)], at)
        vx, = lay([(D,)], at, SK)
        ctxT, = lay([(KC, SK)], at)
        x3 = sb("x3", [P, TT, D])
        bst, mv, lnr = sb("bst", [P, TT, 6]), sb("mv", [P, TT, 2]), sb("lnr", [P, TT])
        ctx_sb = sb("ctx_sb", [SK, D])
        ROWS = TT * XH
        qk_sum = desk[:, 0:ROWS * (SK + 1)].rearrange("p (r k) -> p r k", k=SK + 1)
        qk = qk_sum[:, :, 0:SK]

        def half(t):
            return slice(XH * t, XH * t + XH)

        ex = desk[:, 2560:2560 + ROWS * SK].rearrange("p (r k) -> p r k", k=SK)
        exT = desk[0:SK, 5120:5120 + ROWS * P].rearrange("p (r q) -> p r q", q=P)
        e_sq = desk[:, 5120:5120 + ROWS * SK].rearrange("p (r k) -> p r k", k=SK)
        hid = desk[:, 0:FT * T].rearrange("p (f t) -> p f t", t=T)
        arg = desk[:, 2560:2560 + FT * T].rearrange("p (f t) -> p f t", t=T)
        rnd = desk[:, 5120:5120 + FT * T].rearrange("p (f t) -> p f t", t=T)
        stat = sb("stat", [P, 2, ROWS])
        s_1, r_1, s_2 = sb("s_1", [P, ROWS]), sb("r_1", [P, ROWS]), sb("s_2", [P, ROWS])
        h1, h2 = sb("h1", [64, XH]), sb("h2", [64, XH])
        lt, inv_t = sb("lt", [P, XH]), sb("inv_t", [P, XH])

        names = """const pad_v x_in res_in ctx_in w_in0 w_in1 setup_p setup_a setup_v
            xT_ps xT ab_ps zdec_v eb_a ab_used gate_v beta_v gtab_p gsum_ps eseg_ps gsum_a beta_s_v eseg_a
            proj_ps raw_a prod_a tap_v conv_v add_p
            silu_a vsilu_a sq_p norm_ps norm_v vnorm_v p1_ps kt_ps vt_ps dd_p x_v rh_p nh_v xt_ps mh_a m32_a vn_a ks_v
            n2_ps m2_ps rr_ps n_a m_a r_v ar_ps rt_ps rt_a er_v re_ps rf_v
            S_v st_ps wn_v y_ps y_a su_ps o_ps so_a rs_in_v rstd_v on_a ot_ps oT_v
            ao_ps yln_v bst_v mv_v ve_v rs_c_v rs_l_v x1_v x1b_p x1T_ps x1T_a ctxT_ps ctxT_a kx_ps kx_a vx_ps vx_v
            qx_ps qx_a sc_ps qk_a stat_v d_v e1_a esq_a s1_v s2_v r1_v var_v h1_ps h1_a h2_ps h2_a h3_ps
            lt_v it_a it_v d2_v e2_a se_v rinv_v eT_ps eT_v av_ps ao_v aoT_ps aoT_a x2_ps x2_v x2b_p
            x2T_ps x2T_a hid_ps hid_a arg_v rnd_v sin_a q_v act_v x3_ps x3_v stored""".split()
        s = {n: sem(n) for n in names}

        block = ctx.enter_context(nc.Block())

        def ld(eng, dst, src):
            eng.dma_start(dst, src).then_inc(s["const"], 16)

        loads = [(cst[k][:], a["c_" + k]) for k in const] + [
            (w_ab[:], a["w_ab"]), (conv_w[:], a["conv_w"]), (w_o[:], a["w_o"]), (rms_w[:], a["rms_w"]),
            (neg_a[:], a["A_log"].partition_broadcast(TOK)), (dt_b[:], a["dt_bias"].partition_broadcast(TOK)),
            (xwq[:], a["xwq"]), (xwk[:], a["xwk"]), (xbq[:], a["xbq"]), (xbk[:], a["xbk"]),
            (xwv[:], a["xwv"]), (xwo[:], a["xwo"]),
            (xbv[:], a["xbv"].partition_broadcast(P)), (xbo[:], a["xbo"].partition_broadcast(P)),
            (fb2[:], a["fb2"].partition_broadcast(P)), (tw1[:], a["tw1"].partition_broadcast(P)),
            (tb1[:], a["tb1"]), (tw2[:], a["tw2"]), (tb2[:], a["tb2"]), (tw3[:], a["tw3"]),
            (tb3[:], a["tb3"].partition_broadcast(P)), (fb1[:], a["fb1"]),
            (theta[:], a["theta"]), (w_re[:], a["w_re"]), (w_im[:], a["w_im"]),
        ]
        ALL_CONST = 16 * len(loads)
        BANKS = H // 2
        NL = 2 * LEVELS
        EARLY = PARTS - 1
        FIRST, ROUND = 16 * (PARTS // 2), 16 * (STREAM // 2)

        def weights(b, n):
            if n >= PARTS:
                return FIRST + ROUND * b + 16 * ((EARLY + n - PARTS) // 2) + 16
            if isinstance(b, int) and b == 0:
                return 16 * (n // 2) + 16
            return FIRST + ROUND * (b - 1) + 16 * ((n if n < EARLY else n + 2) // 2) + 16

        def first(b):
            return isinstance(b, int) and b == 0

        @block.sync
        def _(sp):
            for dst, src in loads:
                ld(sp, dst, src)
            def load_x(b, dst, done):
                sp.dma_start(dst, a["x"][bass.ds(b, 1)].rearrange("b (t p) d -> (b p) t d", p=P)).then_inc(s[done], 16)

            def load_context(b):
                sp.dma_start(ctx_sb[:], a["ctx"][bass.ds(b, 1)].rearrange("b k d -> (b k) d")).then_inc(s["ctx_in"], 16)

            def load_weights(n):
                e = n % 2 if n < PARTS else (EARLY + n - PARTS) % 2
                sp.dma_start(w_part[e][:], a["w_parts"][n]).then_inc(s[f"w_in{e}"], 16)

            load_x(0, x_new, "x_in")
            load_weights(0)
            load_weights(1)
            load_x(0, x_tok[:], "res_in")
            load_context(0)
            for n in range(2, PARTS):
                sp.wait_ge(s["proj_ps"], BANKS * (n - 1))
                load_weights(n)
            with sp.Fori(0, BATCHES - 1) as b:
                used = PARTS * BANKS * b
                sp.wait_ge(s["proj_ps"], used + BANKS * (PARTS - 1))
                load_weights(0)
                sp.wait_ge(s["proj_ps"], used + BANKS * PARTS)
                load_weights(1)
                sp.wait_ge(s["o_ps"], CH * b + CH)
                load_x(b + 1, x_new, "x_in")
                sp.wait_ge(s["ctxT_a"], b + 1)
                load_context(b + 1)
                for n in range(2, EARLY):
                    sp.wait_ge(s["proj_ps"], used + BANKS * (PARTS + n - 1))
                    load_weights(n)
                for n in (PARTS, PARTS + 1):
                    sp.wait_ge(s["proj_ps"], used + BANKS * (PARTS + EARLY - 1 + n - PARTS))
                    load_weights(n)
                sp.wait_ge(s["hid_ps"], 4 * b + 4)
                load_weights(EARLY)
                sp.wait_ge(s["x3_ps"], 2 * b + 2)
                load_x(b + 1, x_tok[:], "res_in")
            sp.wait_ge(s["proj_ps"], PARTS * BANKS * BATCHES)
            for n in (PARTS, PARTS + 1):
                load_weights(n)

        @block.gpsimd
        def _(pool):
            pool.memset(r_and_v[:], 0.0).then_inc(s["setup_p"], 1)
            pool.wait_ge(s["const"], ALL_CONST)
            pool.wait_ge(s["setup_p"], 1)
            pool.tensor_copy(ident_h[:], ident[:]).then_inc(s["setup_p"], 1)

            eye = ident[0:L, 0:L].unsqueeze(1).to_broadcast([L, G, L])
            def start(b):
                pool.wait_ge(s["gate_v"], b + 1)
                pool.tensor_tensor(gtab, gdec[:].rearrange("m c h -> m (c h)").unsqueeze(2).to_broadcast([TOK, CH * H, TOK]),
                                   cst["upto"][:, L:P].unsqueeze(1).to_broadcast([TOK, CH * H, TOK]), ALU.mult).then_inc(s["gtab_p"], 1)

            def part(b, n):
                at = ADDS * ((PARTS - 1) * b + n)
                pool.wait_ge(s["prod_a"], (PARTS - 1) * b + n + 1)
                o = co[:, bass.ds(n * H + H - POOL_TILES, POOL_TILES), :]
                pool.tensor_tensor(tap[0], tap[0], tap[1], ALU.add).then_inc(s["add_p"], 1)
                pool.tensor_tensor(o, o, tap[2], ALU.add).then_inc(s["add_p"], 1)
                pool.wait_ge(s["add_p"], at + 2)
                pool.tensor_tensor(none[:], ones[:, 0:1], ones[:, 0:1], ALU.subtract)
                pool.tensor_tensor(o, o, tap[0], ALU.add).then_inc(s["add_p"], 1)

            def chunks(b):
                def squares(m, par):
                    pool.wait_ge(s["norm_ps"], (CH + 1) * b + m + 1)
                    pool.wait_ge(s["silu_a"], 4 * (CH * b + m) + 4)
                    pool.tensor_tensor(SQ, KQ[par], KQ[par], ALU.mult).then_inc(s["sq_p"], 1)

                def decays(m):
                    es = e_seg[:, bass.ds(m * H, H), :]
                    pool.tensor_tensor(DD[:, :, 0:L].rearrange("s h (t i) -> s h t i", i=NHH),
                                       es.unsqueeze(3).to_broadcast([L, H, TOK, NHH]),
                                       cst["strict"][:].rearrange("s (t i) -> s t i", i=NHH).unsqueeze(1).to_broadcast([L, H, TOK, NHH]),
                                       ALU.mult).then_inc(s["dd_p"], 1)
                    pool.tensor_tensor(DD[:, :, L:P], es, cst["causal"][:].unsqueeze(1).to_broadcast([L, H, TOK]),
                                       ALU.mult).then_inc(s["dd_p"], 1)

                def stage(m, par):
                    squares(m, par)
                    if not isinstance(m, int) or m > 0:
                        pool.wait_ge(s["x_v"], 2 * (CH * b + m))
                    decays(m)
                    for g in range(2):
                        hs = slice(G * g, G * g + G)
                        pool.wait_ge(s["x_v"], 2 * (CH * b + m) + g + 1)
                        pool.tensor_tensor(Rh[0][:, hs, :], X[par][0:L, hs, 0:L], eye, ALU.add).then_inc(s["rh_p"], 1)

                pool.wait_ge(s["eseg_a"], 4 * b + 4)
                pool.wait_ge(s["x3_v"], 2 * b + 2)
                stage(0, 0)
                stage(1, 1)
                with pool.Fori(0, CH // 2 - 1) as cc:
                    stage(2 * cc + 2, 0)
                    stage(2 * cc + 3, 1)
            def tail_out(b):
                for t in range(TT):
                    pool.wait_ge(s["x1_v"], 2 * b + t + 1)
                    pool.tensor_tensor(x1b[:, t, :], x1[:, t, :], xbo[:], ALU.add).then_inc(s["x1b_p"], 1)

            def tail_norm(b):
                for t in range(TT):
                    pool.wait_ge(s["x2_v"], 2 * b + t + 1)
                    pool.tensor_tensor(x2b[:, t, :], x2[:, t, :], fb2[:], ALU.add).then_inc(s["x2b_p"], 1)

            def between(b, more):
                tail_out(b)
                if more:
                    start(b + 1)
                    for n in range(EARLY - 1):
                        part(b + 1, n)
                tail_norm(b)
                if more:
                    part(b + 1, EARLY - 1)

            start(0)
            for n in range(PARTS - 1):
                part(0, n)
            with pool.Fori(0, BATCHES - 1) as b:
                chunks(b)
                between(b, True)
            chunks(BATCHES - 1)
            between(BATCHES - 1, False)

        @block.scalar
        def _(act):
            A = act.activation
            act.wait_ge(s["const"], ALL_CONST)
            A(neg_a[:], neg_a[:], ACT.Exp).then_inc(s["setup_a"], 1)
            act.wait_ge(s["setup_v"], 5)
            A(trig[:], turn[:], ACT.Sin).then_inc(s["setup_a"], 1)

            def start(b):
                act.wait_ge(s["xT_ps"], b + 1)
                A(xT[:].rearrange("p k t -> p (k t)"), bank[6][:], ACT.Copy).then_inc(s["xT"], 1)
                act.wait_ge(s["ab_ps"], b + 1)
                ab = bank[7][0:TOK, 0:CH * 4 * H].rearrange("m (c k) -> m c k", k=4 * H)
                A(beta[:].rearrange("m c i h -> m c (i h)"), ab[:, :, H:4 * H], ACT.Exp, scale=-1.0).then_inc(s["eb_a"], 1)
                act.wait_ge(s["zdec_v"], 2 * b + 2)
                A(zabs[:], zabs[:], ACT.Exp, scale=-1.0).then_inc(s["eb_a"], 1)
                act.wait_ge(s["eb_a"], 3 * b + 2)
                A(zabs[:], zabs[:], ACT.Ln, bias=1.0).then_inc(s["eb_a"], 1)

            def part(b, n, mid=None, late=None):
                if n == PARTS - 1:
                    if not first(b):
                        act.wait_ge(s["act_v"], 4 * b)
                    for q in range(BANKS):
                        act.wait_ge(s["proj_ps"], PARTS * BANKS * b + BANKS * n + q + 1)
                        A(gate[:, 2 * q:2 * q + 2, :], bank[4 + q][:].rearrange("p (j t) -> p j t", t=T), ACT.Silu).then_inc(s["raw_a"], 1)
                else:
                    e = n % 2
                    if n >= 2:
                        act.wait_ge(s["conv_v"], (PARTS - 1) * b + n)
                    for q in range(BANKS):
                        act.wait_ge(s["proj_ps"], PARTS * BANKS * b + BANKS * n + q + 1)
                        src = bank[4 + q][:].rearrange("p (j t) -> p j t", t=T)
                        for j in range(2):
                            i = n * H + 2 * q + j
                            A(co[:, i, :], src[:, j, :], ACT.Copy, scale=conv_w[:, i, CONV - 1:CONV])
                        A(raw[e][:, 2 * q:2 * q + 2, CONV - 1:], src, ACT.Copy).then_inc(s["raw_a"], 1)
                        if mid and q == 1:
                            mid()
                    if late:
                        late()
                    if n > 0 or not first(b):
                        act.wait_ge(s["add_p"], ADDS * ((PARTS - 1) * b + n))
                    act.wait_ge(s["pad_v"], b + 1)
                    act.wait_ge(s["raw_a"], PARTS * BANKS * b + BANKS * n + BANKS)
                    for j in range(POOL_TILES):
                        i = n * H + H - POOL_TILES + j
                        for k in range(CONV - 1):
                            ins = A(tap[k][:, j, :], raw[e][:, H - POOL_TILES + j, k:k + T], ACT.Copy, scale=conv_w[:, i, k:k + 1])
                    ins.then_inc(s["prod_a"], 1)

            def decays(b):
                act.wait_ge(s["gsum_ps"], b + 1)
                A(e_in[:].rearrange("p a c -> p (a c)"), bank[0][:, 0:2 * CH * H], ACT.Exp).then_inc(s["gsum_a"], 1)
                A(e_out[:], bank[0][0:L, 2 * CH * H:3 * CH * H], ACT.Exp).then_inc(s["gsum_a"], 1)
                for q in range(4):
                    act.wait_ge(s["eseg_ps"], 4 * b + q + 1)
                    A(e_seg[:, 16 * q:16 * q + 16, :].rearrange("s c t -> s (c t)"), bank[4 + q][0:L, :], ACT.Exp).then_inc(s["eseg_a"], 1)

            def stage_kq(b, m, par):
                tk = bass.ds(m * TOK, TOK)
                A(KQ[par][:, :, L:P], co[:, 0:H, tk], ACT.Silu).then_inc(s["silu_a"], 1)
                for i in range(NHH):
                    A(KQ[par][:, :, 0:L].rearrange("p h (t i) -> p h t i", i=NHH)[:, :, :, i], co[:, H + H * i:2 * H + H * i, tk],
                      ACT.Silu).then_inc(s["silu_a"], 1)

            def chunks(b):
                def stage_v(m):
                    tk = bass.ds(m * TOK, TOK)
                    for i in range(NHH):
                        A(VT.rearrange("p h (t i) -> p h t i", i=NHH)[:, :, :, i], co[:, H * (4 + i):H * (5 + i), tk],
                          ACT.Silu).then_inc(s["vsilu_a"], 1)

                def step(c, par, state=True, inverse=True, stage=True, last=False):
                    n, m = c + 1, c + 2
                    it, itn = CH * b + c, CH * b + n

                    def level(lv, g):
                        hs = slice(G * g, G * g + G)
                        if lv < LEVELS - 1:
                            act.wait_ge(s["n2_ps"], (NL - 2) * itn + 2 * lv + g + 1)
                            A(Nh[(lv + 1) % 2][:, hs, :], bank[2 * g][0:L, 0:G * L].rearrange("r (h s) -> r h s", s=L),
                              ACT.Copy).then_inc(s["n_a"], 1)
                        act.wait_ge(s["m2_ps"], NL * itn + 2 * lv + g + 1)
                        A(Mh[(lv + 1) % 2][:, hs, :], bank[2 * g + 1][0:L, 0:G * L].rearrange("r (h s) -> r h s", s=L),
                          ACT.Copy).then_inc(s["m_a"], 1)

                    def y_out(g):
                        act.wait_ge(s["y_ps"], 2 * it + g + 1)
                        A(Y[:, G * g:G * g + G, :].rearrange("p h d -> p (h d)"), bank[6 + g][:], ACT.Copy).then_inc(s["y_a"], 1)

                    def vn_out(g):
                        act.wait_ge(s["vnorm_v"], itn + 1)
                        act.wait_ge(s["vt_ps"], 2 * itn + g + 1)
                        for j in range(G):
                            h = G * g + j
                            ins = A(Vn[0:L, h, :], bank[6 + g][0:L, P * j:P * j + P], ACT.Copy, scale=vnorm[1 - par][:, h:h + 1])
                        ins.then_inc(s["vn_a"], 1)

                    if inverse:
                        for g in range(2):
                            hs = slice(G * g, G * g + G)
                            act.wait_ge(s["xt_ps"], 2 * itn + g + 1)
                            src = bank[2 * g][0:L, 0:G * L].rearrange("r (h s) -> r h s", s=L)
                            A(Mh[0][:, hs, :], src, ACT.Copy).then_inc(s["mh_a"], 1)
                            A(M32[:, hs, :], src, ACT.Copy).then_inc(s["m32_a"], 1)
                    if stage:
                        if state:
                            act.wait_ge(s["st_ps"], 2 * it + 2)
                        stage_kq(b, m, par)
                    for g in range(2):
                        if inverse:
                            level(0, g)
                        if state:
                            y_out(g)
                    if inverse:
                        level(1, 0)
                        level(1, 1)
                    if last:
                        act.wait_ge(s["rf_v"], 2 * CH * (b + 1))
                        act.wait_ge(s["ctxT_ps"], b + 1)
                        A(ctxT.rearrange("p k c -> p (k c)"), bank[2][:, 0:KC * SK], ACT.Copy).then_inc(s["ctxT_a"], 1)
                    if state:
                        act.wait_ge(s["o_ps"], it + 1)
                        for j in range(2):
                            A(On[:, j, :], bank[5][:, P * j:P * j + P], ACT.Square, accum_out=so[:, j:j + 1]).then_inc(s["so_a"], 1)
                    if inverse:
                        level(2, 0)
                        level(2, 1)
                        for g in range(2):
                            vn_out(g)
                            level(3, g)
                        for g in range(2):
                            level(4, g)
                        if stage:
                            stage_v(m)
                        for g in range(2):
                            level(5, g)
                    if last:
                        act.wait_ge(s["kx_ps"], b + 1)
                        for g in range(XG):
                            ins = A(kTx[:, g, 0:SK], bank[3][:, SK * g:SK * g + SK], ACT.Identity, bias=xbk[:, g:g + 1], accum_out=kTx[:, g, SK:SK + 1])
                        ins.then_inc(s["kx_a"], 1)
                    if state:
                        act.wait_ge(s["rstd_v"], it + 1)
                        act.wait_ge(s["so_a"], 2 * it + 2)
                        for j in range(2):
                            A(On[:, j, :], bank[5][:, P * j:P * j + P], ACT.Copy, scale=rstd[:, j:j + 1]).then_inc(s["on_a"], 1)
                    if inverse:
                        for g in range(2):
                            act.wait_ge(s["rt_ps"], 2 * itn + g + 1)
                            A(R0T[:, G * g:G * g + G, :], bank[4][0:L, 0:G * L].rearrange("r (h s) -> r h s", s=L),
                              ACT.Copy).then_inc(s["rt_a"], 1)

                act.wait_ge(s["conv_v"], (PARTS - 1) * b + PARTS)
                act.wait_ge(s["add_p"], ADDS * (PARTS - 1) * (b + 1))
                stage_v(0)
                step(-1, 1, state=False)
                with act.Fori(0, CH // 2 - 1) as cc:
                    step(2 * cc, 0)
                    step(2 * cc + 1, 1)
                step(CH - 2, 0, stage=False)
                step(CH - 1, 1, inverse=False, stage=False, last=True)

            def tail_x1(b):
                act.wait_ge(s["x1T_ps"], b + 1)
                A(x1T.rearrange("p k t -> p (k t)"), bank[0][:], ACT.Copy).then_inc(s["x1T_a"], 1)

            def tail_queries(b):
                for q in range(2):
                    act.wait_ge(s["qx_ps"], 2 * b + q + 1)
                    for j in range(2):
                        ins = A(qTx[:, 2 * q + j, :], bank[2 + q][:, T * j:T * j + T], ACT.Identity, bias=xbq[:, 2 * q + j:2 * q + j + 1])
                    ins.then_inc(s["qx_a"], 1)

            def tail_scores(b):
                for q in range(8):
                    act.wait_ge(s["sc_ps"], 8 * b + q + 1)
                    A(qk_sum[:, XG * q:XG * q + XG, :].rearrange("p r k -> p (r k)"), bank[q % 4][:, 0:XG * (SK + 1)], ACT.Copy).then_inc(s["qk_a"], 1)
                for t in range(TT):
                    act.wait_ge(s["d_v"], 2 * b + t + 1)
                    A(ex[:, half(t), :], qk[:, half(t), :], ACT.Exp, scale=DK ** -0.5).then_inc(s["e1_a"], 1)
                for t in range(TT):
                    act.wait_ge(s["e1_a"], 2 * b + t + 1)
                    A(e_sq[:, half(t), :], ex[:, half(t), :], ACT.Square).then_inc(s["esq_a"], 1)

            def tail_net(b):
                act.wait_ge(s["h1_ps"], b + 1)
                A(h1[:], bank[0][0:64, 0:XH], ACT.Gelu, bias=tb1[:]).then_inc(s["h1_a"], 1)
                act.wait_ge(s["h2_ps"], b + 1)
                A(h2[:], bank[1][0:64, 0:XH], ACT.Gelu, bias=tb2[:]).then_inc(s["h2_a"], 1)
                act.wait_ge(s["lt_v"], 2 * b + 2)
                A(inv_t[:], lt[:], ACT.Exp, scale=-1.0).then_inc(s["it_a"], 1)

            def tail_weights(b):
                for t in range(TT):
                    act.wait_ge(s["d2_v"], 2 * b + t + 1)
                    A(ex[:, half(t), :], qk[:, half(t), :], ACT.Exp).then_inc(s["e2_a"], 1)

            def tail_values(b):
                act.wait_ge(s["aoT_ps"], b + 1)
                A(aoT.rearrange("p k t -> p (k t)"), bank[2][:], ACT.Copy).then_inc(s["aoT_a"], 1)

            def tail_x2(b):
                act.wait_ge(s["x2T_ps"], b + 1)
                A(x2T.rearrange("p k t -> p (k t)"), bank[2][:], ACT.Copy).then_inc(s["x2T_a"], 1)

            def tail_ffn(b):
                for q, bk in enumerate((3, 0, 1, 3)):
                    act.wait_ge(s["hid_ps"], 4 * b + q + 1)
                    for j in range(2):
                        f = 2 * q + j
                        ins = A(hid[:, f, :], bank[bk][:, T * j:T * j + T], ACT.Identity, bias=fb1[:, f:f + 1])
                    ins.then_inc(s["hid_a"], 1)
                for q in range(4):
                    act.wait_ge(s["rnd_v"], 16 * b + 4 * q + 4)
                    A(rnd[:, 2 * q:2 * q + 2, :], arg[:, 2 * q:2 * q + 2, :], ACT.Sin).then_inc(s["sin_a"], 1)

            def store(b):
                act.wait_ge(s["x3_v"], 2 * b + 4)
                act.dma_start(out[bass.ds(b, 1)].rearrange("b (t p) d -> (b p) t d", p=P), x3[:]).then_inc(s["stored"], 16)

            def between(b, more):
                if not more:
                    tail_x1(b)
                    tail_queries(b)
                    tail_scores(b)
                    tail_net(b)
                    tail_weights(b)
                    tail_values(b)
                    tail_x2(b)
                    tail_ffn(b)
                    store(b)
                    return
                start(b + 1)
                part(b + 1, 0, mid=lambda: tail_x1(b))
                tail_queries(b)
                part(b + 1, 1)
                tail_scores(b)
                part(b + 1, 2, late=lambda: tail_net(b))
                tail_weights(b)
                part(b + 1, 3)
                part(b + 1, 4)
                part(b + 1, 5)
                tail_values(b)
                part(b + 1, 6, late=lambda: tail_x2(b))
                decays(b + 1)
                tail_ffn(b)
                stage_kq(b + 1, 0, 0)
                part(b + 1, EARLY)
                store(b)

            start(0)
            for n in range(EARLY):
                part(0, n)
            decays(0)
            stage_kq(0, 0, 0)
            part(0, EARLY)
            with act.Fori(0, BATCHES - 1) as b:
                chunks(b)
                between(b, True)
            chunks(BATCHES - 1)
            between(BATCHES - 1, False)
            act.wait_ge(s["stored"], 16 * BATCHES + 16)

        @block.tensor
        def _(pe):
            MM = pe.matmul
            pe.wait_ge(s["const"], ALL_CONST)
            pe.wait_ge(s["setup_p"], 2)

            def start(b):
                pe.wait_ge(s["x_in"], 16 * b + 16)
                for k in range(KC):
                    for t in range(TT):
                        ins = pe.transpose(bank[6][:, T * k + P * t:T * k + P * t + P], x_new[:, t, P * k:P * k + P], ident[:])
                ins.then_inc(s["xT_ps"], 1)
                pe.wait_ge(s["xT"], b + 1)
                for c in range(CH):
                    for k in range(KC):
                        ins = MM(bank[7][0:TOK, 4 * H * c:4 * H * (c + 1)], xT[:, k, TOK * c:TOK * c + TOK], w_ab[:, k, :],
                                 start=(k == 0), stop=(k == KC - 1))
                ins.then_inc(s["ab_ps"], 1)

            def part(b, n, mid=None):
                e = n % 2
                pe.wait_ge(s[f"w_in{e}"], weights(b, n))
                if n == 0:
                    pe.wait_ge(s["ab_used"], b + 1)
                    pe.wait_ge(s["eb_a"], 3 * b + 1)
                    if not first(b):
                        pe.wait_ge(s["vx_v"], b)
                for q in range(BANKS):
                    if n > 0:
                        pe.wait_ge(s["raw_a"], PARTS * BANKS * b + BANKS * (n - 1) + q + 1)
                    if n == EARLY:
                        pe.wait_ge(s["eseg_a"], 4 * b + q + 1)
                    for j in range(2):
                        o = DH * (2 * q + j)
                        for k in range(KC):
                            ins = MM(bank[4 + q][:, T * j:T * j + T], w_part[e][:, k, o:o + DH], xT[:, k, :],
                                     start=(k == 0), stop=(k == KC - 1))
                    ins.then_inc(s["proj_ps"], 1)
                    if mid and q == 1:
                        mid()

            def finish(b):
                pe.wait_ge(s["x3_v"], 2 * b + 2)
                pe.wait_ge(s["raw_a"], PARTS * BANKS * b + PARTS * BANKS)

            def decays(b):
                pe.wait_ge(s["raw_a"], PARTS * BANKS * b + EARLY * BANKS)
                pe.wait_ge(s["gate_v"], b + 1)
                pe.wait_ge(s["beta_v"], 2 * b + 2)
                gflat = gdec[:].rearrange("m c h -> m (c h)")
                NCH = CH * H
                MM(bank[0][:, 0:NCH], cst["upto"][:], gflat, start=True, stop=True)
                MM(bank[0][:, NCH:2 * NCH], ones[0:TOK, :], gflat, start=True, stop=True)
                MM(bank[0][0:L, 2 * NCH:3 * NCH], cst["after"][:], gflat, start=True, stop=True).then_inc(s["gsum_ps"], 1)
                for i in range(NHH):
                    ins = MM(bank[1][0:L, 0:NCH], cst["spread"][:, L * i:L * i + L], beta[:, :, i, :], start=(i == 0), stop=(i == NHH - 1))
                ins.then_inc(s["norm_ps"], 1)
                pe.wait_ge(s["gtab_p"], b + 1)
                for q in range(4):
                    MM(bank[4 + q][0:L, :], cst["after"][:], gtab[:, 16 * q:16 * q + 16, :], start=True, stop=True).then_inc(s["eseg_ps"], 1)

            def project_out(b, t):
                pe.wait_ge(s["oT_v"], CH * b + CH // TT * (t + 1) + 1)
                for h in range(H):
                    ins = MM(bank[t][:, 0:D], oT[:, h, P * t:P * t + P], w_o[:, h, :], start=(h == 0), stop=(h == H - 1))
                ins.then_inc(s["ao_ps"], 1)

            def chunks(b):
                def context_rows():
                    pe.wait_ge(s["ctx_in"], 16 * b + 16)
                    for k in range(KC):
                        ins = pe.transpose(bank[2][:, SK * k:SK * k + SK], ctx_sb[:, P * k:P * k + P], ident[0:SK, 0:SK])
                    ins.then_inc(s["ctxT_ps"], 1)

                def keys_and_values():
                    pe.wait_ge(s["ctxT_a"], b + 1)
                    for g in range(XG):
                        for k in range(KC):
                            ins = MM(bank[3][:, SK * g:SK * g + SK], xwk[:, k, P * g:P * g + P], ctxT[:, k, :], start=(k == 0), stop=(k == KC - 1))
                    ins.then_inc(s["kx_ps"], 1)
                    for k in range(KC):
                        ins = MM(bank[4][0:SK, 0:D], ctxT[:, k, :], xwv[:, k, :], start=(k == 0), stop=(k == KC - 1))
                    ins.then_inc(s["vx_ps"], 1)

                def norms_k(m):
                    pe.wait_ge(s["sq_p"], CH * b + m + 1)
                    for h in range(H):
                        MM(bank[5][:, 2 * P + h:2 * P + h + 1], SQ[:, h, :], ones[:, 0:1], start=True, stop=True)

                def norms_q(m):
                    for h in range(H):
                        o, col = TOK * (h % G), 2 * P + H + h // G
                        ins = MM(bank[5][o:o + TOK, col:col + 1], SQ[:, h, L:P], ones[:, 0:1], start=True, stop=True)
                    ins.then_inc(s["norm_ps"], 1)

                def dots(m, par, g):
                    pe.wait_ge(s["silu_a"], 4 * (CH * b + m) + 4)
                    for j in range(G):
                        h = G * g + j
                        ins = MM(bank[2 * g][0:L, P * j:P * j + P], KQ[par][:, h, 0:L], KQ[par][:, h, :], start=True, stop=True)
                    ins.then_inc(s["p1_ps"], 1)

                def x_rows(m, par, g):
                    pe.wait_ge(s["x_v"], 2 * (CH * b + m) + g + 1)
                    for j in range(G):
                        ins = pe.transpose(bank[2 * g][0:L, L * j:L * j + L], X[par][0:L, G * g + j, 0:L], ident[0:L, 0:L])
                    ins.then_inc(s["xt_ps"], 1)

                def step(c, par, state=True, inverse=True, stage=True, last=False):
                    n, m = c + 1, c + 2
                    it, itn = CH * b + c, CH * b + n
                    kqn, x = KQ[1 - par], X[par]

                    def level(lv, g):
                        if not inverse:
                            return
                        cur = lv % 2
                        if lv == 0:
                            pe.wait_ge(s["nh_v"], 2 * itn + g + 1)
                            pe.wait_ge(s["m32_a"], 2 * itn + g + 1)
                            if state:
                                pe.wait_ge(s["rf_v"], 2 * it + g + 1)
                        else:
                            pe.wait_ge(s["m_a"], NL * itn + 2 * (lv - 1) + g + 1)
                        if 1 <= lv < LEVELS:
                            pe.wait_ge(s["n_a"], (NL - 2) * itn + 2 * (lv - 1) + g + 1)
                        if lv < LEVELS - 1:
                            for j in range(G):
                                ins = MM(bank[2 * g][0:L, L * j:L * j + L], Mh[cur][:, G * g + j, :], Nh[cur][:, G * g + j, :], start=True, stop=True)
                            ins.then_inc(s["n2_ps"], 1)
                        if lv < LEVELS:
                            for j in range(G):
                                ins = MM(bank[2 * g + 1][0:L, L * j:L * j + L], Nh[cur][:, G * g + j, :], Mh[cur][:, G * g + j, :], start=True, stop=True)
                            ins.then_inc(s["m2_ps"], 1)
                        if lv >= 1:
                            if lv == 1:
                                pe.wait_ge(s["rh_p"], 2 * itn + g + 1)
                            if lv > 1 or g == 1:
                                pe.wait_ge(s["r_v"], NL * itn + 2 * (lv - 1) + g)
                            for j in range(G):
                                ins = MM(bank[4][0:L, L * j:L * j + L], Mh[cur][:, G * g + j, :], Rh[1 - cur][:, G * g + j, :], start=True, stop=True)
                            ins.then_inc(s["rr_ps"], 1)

                    def y(g):
                        pe.wait_ge(s["wn_v"], 2 * it + g + 1)
                        pe.wait_ge(s["rf_v"], 2 * it + g + 1)
                        for j in range(G):
                            h = G * g + j
                            ins = MM(bank[6 + g][:, P * j:P * j + P], R[:, h, :], Wn[:, h, :], start=True, stop=True)
                        ins.then_inc(s["y_ps"], 1)

                    def outer(g):
                        pe.wait_ge(s["y_a"], 2 * it + g + 1)
                        for j in range(G):
                            h = G * g + j
                            ins = MM(bank[6 + g][:, P * j:P * j + P], Ks[:, h, :], Y[0:L, h, :], start=True, stop=True)
                        ins.then_inc(s["su_ps"], 1)

                    def rows(src, g, done):
                        for j in range(G):
                            ins = pe.transpose(bank[6 + g][0:L, P * j:P * j + P], src[:, G * g + j, 0:L], ident[:])
                        ins.then_inc(done, 1)

                    def from_state(g):
                        pe.wait_ge(s["S_v"], 2 * CH * b + 2 * n + g + 1)
                        pe.wait_ge(s["ks_v"], 2 * itn + g + 1)
                        for j in range(G):
                            h = G * g + j
                            ins = MM(bank[6 + g][:, P * j:P * j + P], kqn[:, h, :], S[:, h, :], start=True, stop=True)
                        ins.then_inc(s["st_ps"], 1)

                    level(0, 0)
                    level(0, 1)
                    if state:
                        y(0)
                        y(1)
                    if last:
                        project_out(b, 0)
                        context_rows()
                    for g in range(2):
                        if last:
                            pe.wait_ge(s["y_a"], 2 * it + g + 1)
                        elif state:
                            outer(g)
                        level(1, g)
                    if state:
                        pe.wait_ge(s["oT_v"], it + 1)
                        for h in range(H):
                            o = TOK * (h % G)
                            ins = MM(bank[5][o:o + TOK, P * (h // G):P * (h // G) + P], x[:, h, L:P], Y[:, h, :], start=True, stop=True)
                        ins.then_inc(s["o_ps"], 1)
                    if last:
                        keys_and_values()
                    level(2, 0)
                    if stage:
                        if state:
                            pe.wait_ge(s["so_a"], 2 * it + 2)
                        norms_k(m)
                        norms_q(m)
                    level(2, 1)
                    if inverse:
                        pe.wait_ge(s["vsilu_a"], NHH * itn + NHH)
                        for g in range(2):
                            pe.wait_ge(s["S_v"], 2 * CH * b + 2 * n + g + 1)
                            rows(VT, g, s["vt_ps"])
                            level(3, g)
                        for g in range(2):
                            pe.wait_ge(s["vn_a"], 2 * itn + g + 1)
                            rows(kqn, g, s["kt_ps"])
                            level(4, g)
                        for g in range(2):
                            level(5, g)
                            if stage:
                                dots(m, par, g)
                        for g in range(2):
                            from_state(g)
                            level(6, g)
                    if state:
                        pe.wait_ge(s["on_a"], 2 * it + 2)
                        for j in range(2):
                            ins = pe.transpose(bank[5][:, P * j:P * j + P], On[:, j, :], ident[:])
                        ins.then_inc(s["ot_ps"], 1)
                    if inverse:
                        eye_h = ident_h[0:L, 0:L]
                        for g in range(2):
                            pe.wait_ge(s["r_v"], NL * itn + NL - 2 + g + 1)
                            for j in range(G):
                                o = bank[2 * g + 1][0:L, L * j:L * j + L]
                                MM(o, M32[:, G * g + j, :], R0[:, G * g + j, :], start=True, stop=False)
                                ins = MM(o, eye_h, eye_h, start=False, stop=True)
                            ins.then_inc(s["ar_ps"], 1)
                        for g in range(2):
                            if g == 1:
                                pe.wait_ge(s["rt_a"], 2 * itn + 1)
                            for j in range(G):
                                ins = pe.transpose(bank[4][0:L, L * j:L * j + L], R0[:, G * g + j, :], ident[0:L, 0:L])
                            ins.then_inc(s["rt_ps"], 1)
                        if stage:
                            x_rows(m, par, 0)
                            x_rows(m, par, 1)
                        for g in range(2):
                            pe.wait_ge(s["er_v"], 2 * itn + g + 1)
                            pe.wait_ge(s["rt_a"], 2 * itn + g + 1)
                            for j in range(G):
                                ins = MM(bank[2 * g + 1][0:L, L * j:L * j + L], R0T[:, G * g + j, :], Er[:, G * g + j, :], start=True, stop=True)
                            ins.then_inc(s["re_ps"], 1)

                pe.wait_ge(s["beta_s_v"], b + 1)
                pe.wait_ge(s["eseg_a"], 4 * b + 4)
                pe.wait_ge(s["gsum_a"], 2 * b + 2)
                norms_k(0)
                norms_q(0)
                for g in range(2):
                    dots(0, 0, g)
                for g in range(2):
                    x_rows(0, 0, g)
                step(-1, 1, state=False)
                with pe.Fori(0, CH // 2 - 1) as cc:
                    step(2 * cc, 0)
                    step(2 * cc + 1, 1)
                step(CH - 2, 0, stage=False)
                step(CH - 1, 1, inverse=False, stage=False, last=True)

            def tail_x1(b):
                pe.wait_ge(s["x1_v"], 2 * b + 2)
                for k in range(KC):
                    for t in range(TT):
                        ins = pe.transpose(bank[0][:, T * k + P * t:T * k + P * t + P], x1[:, t, P * k:P * k + P], ident[:])
                ins.then_inc(s["x1T_ps"], 1)

            def tail_queries(b):
                pe.wait_ge(s["x1T_a"], b + 1)
                pe.wait_ge(s["kx_a"], b + 1)
                for q in range(2):
                    for j in range(2):
                        g = 2 * q + j
                        for k in range(KC):
                            ins = MM(bank[2 + q][:, T * j:T * j + T], xwq[:, k, P * g:P * g + P], x1T[:, k, :], start=(k == 0), stop=(k == KC - 1))
                    ins.then_inc(s["qx_ps"], 1)

            def tail_scores(b):
                pe.wait_ge(s["vx_v"], b + 1)
                pe.wait_ge(s["qx_a"], 2 * b + 2)
                for t in range(TT):
                    for g in range(XG):
                        for j in range(XG):
                            if t == 1 and g == 0:
                                pe.wait_ge(s["qk_a"], 8 * b + j + 1)
                            r = slice(32 * j, 32 * j + 32)
                            ins = MM(bank[j][:, (SK + 1) * g:(SK + 1) * (g + 1)], qTx[r, g, P * t:P * t + P], kTx[r, g, :], start=True, stop=True)
                            if g == XG - 1:
                                ins.then_inc(s["sc_ps"], 1)

            def tail_net(b):
                pe.wait_ge(s["qk_a"], 8 * b + 8)
                pe.wait_ge(s["var_v"], 3 * b + 3)
                for f in range(3):
                    for t in range(TT):
                        rhs = stat[:, f - 1, half(t)] if f else qk_sum[:, half(t), SK]
                        ins = MM(bank[0][0:64, 0:XH], tw1[:, f, :], rhs, start=(f + t == 0), stop=(f == 2 and t == TT - 1))
                ins.then_inc(s["h1_ps"], 1)
                pe.wait_ge(s["h1_a"], b + 1)
                MM(bank[1][:, 0:XH], tw2[:], h1[:], start=True, stop=True).then_inc(s["h2_ps"], 1)
                pe.wait_ge(s["h2_a"], b + 1)
                MM(bank[2][:, 0:XH], tw3b[:], h2[:], start=True, stop=True).then_inc(s["h3_ps"], 1)

            def tail_weights(b):
                for q in range(8):
                    if q % XG == 0:
                        pe.wait_ge(s["e2_a"], 2 * b + q // XG + 1)
                    if q >= 4:
                        pe.wait_ge(s["eT_v"], 8 * b + q - 3)
                    for j in range(XG):
                        ins = pe.transpose(bank[q % 4][0:SK, P * j:P * j + P], ex[:, XG * q + j, :], ident[:])
                    ins.then_inc(s["eT_ps"], 1)

            def tail_values(b):
                for t in range(TT):
                    pe.wait_ge(s["eT_v"], 8 * b + (XG + 1 if t == 0 else 8))
                    for h in range(XH):
                        ins = MM(bank[t][:, DK * h:DK * h + DK], exT[:, XH * t + h, :], vx[:, DK * h:DK * h + DK], start=True, stop=True)
                    ins.then_inc(s["av_ps"], 1)

            def tail_ao(b):
                pe.wait_ge(s["ao_v"], 2 * b + 2)
                for k in range(KC):
                    for t in range(TT):
                        ins = pe.transpose(bank[2][:, T * k + P * t:T * k + P * t + P], ao[:, t, P * k:P * k + P], ident[:])
                ins.then_inc(s["aoT_ps"], 1)

            def tail_norm(b):
                pe.wait_ge(s["aoT_a"], b + 1)
                for t in range(TT):
                    for k in range(KC):
                        ins = MM(bank[t][:, 0:D], aoT[:, k, P * t:P * t + P], xwo[:, k, :], start=(k == 0), stop=(k == KC - 1))
                    ins.then_inc(s["x2_ps"], 1)

            def tail_x2(b):
                pe.wait_ge(s["x2_v"], 2 * b + 2)
                for k in range(KC):
                    for t in range(TT):
                        ins = pe.transpose(bank[2][:, T * k + P * t:T * k + P * t + P], x2[:, t, P * k:P * k + P], ident[:])
                ins.then_inc(s["x2T_ps"], 1)

            def tail_ffn(b, more):
                pe.wait_ge(s["x2T_a"], b + 1)
                pe.wait_ge(s["w_in1"], weights(b, PARTS) if more else FIRST + ROUND * b + 16)
                for q, bk in enumerate((3, 0, 1, 3)):
                    if more and q in (1, 2):
                        pe.wait_ge(*((s["gsum_a"], 2 * b + 4) if q == 1 else (s["beta_s_v"], b + 2)))
                    if q == 3:
                        pe.wait_ge(s["hid_a"], 4 * b + 1)
                    for j in range(2):
                        f = 2 * q + j
                        for k in range(KC):
                            ins = MM(bank[bk][:, T * j:T * j + T], fw1[:, k, P * f:P * f + P], x2T[:, k, :], start=(k == 0), stop=(k == KC - 1))
                    ins.then_inc(s["hid_ps"], 1)
                pe.wait_ge(s["w_in0"], weights(b, PARTS + 1) if more else FIRST + ROUND * b + 16)
                pe.wait_ge(s["hid_a"], 4 * b + 2)
                for q in range(4):
                    pe.wait_ge(s["act_v"], 4 * b + q + 1)
                    for t in range(TT):
                        for f in (2 * q, 2 * q + 1):
                            ins = MM(bank[(2, 0)[t]][:, 0:D], arg[:, f, P * t:P * t + P], fw2[:, f, :], start=(f == 0), stop=(f == FT - 1))
                        if q == 3:
                            ins.then_inc(s["x3_ps"], 1)

            def between(b, more):
                if not more:
                    project_out(b, 1)
                    tail_x1(b)
                    tail_queries(b)
                    tail_scores(b)
                    tail_net(b)
                    tail_weights(b)
                    tail_values(b)
                    tail_ao(b)
                    tail_norm(b)
                    tail_x2(b)
                    tail_ffn(b, more)
                    return
                start(b + 1)
                project_out(b, 1)
                part(b + 1, 0, mid=lambda: tail_x1(b))
                tail_queries(b)
                part(b + 1, 1)
                tail_scores(b)
                part(b + 1, 2)
                tail_net(b)
                part(b + 1, 3)
                tail_weights(b)
                part(b + 1, 4)
                part(b + 1, 5)
                tail_values(b)
                tail_ao(b)
                part(b + 1, 6, mid=lambda: tail_norm(b))
                tail_x2(b)
                decays(b + 1)
                tail_ffn(b, more)
                part(b + 1, EARLY)
                finish(b + 1)

            start(0)
            for n in range(EARLY):
                part(0, n)
            decays(0)
            part(0, EARLY)
            finish(0)
            with pe.Fori(0, BATCHES - 1) as b:
                chunks(b)
                between(b, True)
            chunks(BATCHES - 1)
            between(BATCHES - 1, False)

        @block.vector
        def _(v):
            v.memset(x3[:, 0, :], 0.0).then_inc(s["x3_v"], 1)
            v.memset(x3[:, 1, :], 0.0).then_inc(s["x3_v"], 1)
            v.memset(ms[:], 0.0).then_inc(s["stored"], 16)
            v.memset(oT[:, 0, :], 0.0).then_inc(s["oT_v"], 1)
            v.memset(co[:, 0, :], 0.0).then_inc(s["conv_v"], 1)
            v.memset(rs_x[:], 1.0)
            v.wait_ge(s["const"], ALL_CONST)

            def turns_off(x, y, sem_, at, add=0.0):
                v.tensor_scalar(y, x, 1 / TWO_PI, MAGIC, ALU.mult, ALU.add).then_inc(sem_, 1)
                v.wait_ge(sem_, at + 1)
                v.tensor_scalar(y, y, MAGIC, -TWO_PI, ALU.subtract, ALU.mult).then_inc(sem_, 1)
                v.wait_ge(sem_, at + 2)
                v.tensor_tensor(x, x, y, ALU.add).then_inc(sem_, 1)
                v.wait_ge(sem_, at + 3)
                v.tensor_scalar(x, x, PI_BELOW, -PI_BELOW, ALU.min, ALU.max).then_inc(sem_, 1)

            def rsqrt(x, y, tmp, sem_, at, steps=range(RS)):
                xi, yi = x.bitcast(mybir.dt.int32), y.bitcast(mybir.dt.int32)
                for k in steps:
                    if k == 0:
                        v.tensor_scalar(yi, xi, 1, None, ALU.logical_shift_right).then_inc(sem_, 1)
                        continue
                    v.wait_ge(sem_, at + k)
                    if k == 1:
                        v.tensor_scalar(yi, yi, -1.0, float(0x5F3759DF), ALU.mult, ALU.add).then_inc(sem_, 1)
                    elif k % 3 == 2:
                        v.tensor_tensor(tmp, y, y, ALU.mult).then_inc(sem_, 1)
                    elif k % 3 == 0:
                        v.scalar_tensor_tensor(tmp, tmp, -0.5, x, ALU.mult, ALU.mult).then_inc(sem_, 1)
                    else:
                        v.scalar_tensor_tensor(y, tmp, 1.5, y, ALU.add, ALU.mult).then_inc(sem_, 1)
                if steps[-1] == RS - 1:
                    v.wait_ge(sem_, at + RS)

            v.tensor_copy(turn[:, 0:FT], theta[:])
            v.tensor_scalar(turn[:, FT:2 * FT], theta[:], float(np.pi / 2), None, ALU.add).then_inc(s["setup_v"], 1)
            v.wait_ge(s["setup_v"], 1)
            turns_off(turn[:], trig[:], s["setup_v"], 1)
            for f, m in enumerate((DK ** -0.5 / (T * SK), DK ** -0.5 / T, 1.0 / T)):
                v.tensor_scalar(tw1[:, f, :], tw1[:, f, :], m, None, ALU.mult)
            v.tensor_copy(tw3b[:], tw3[:].to_broadcast([64, P]))
            v.wait_ge(s["setup_a"], 2)
            v.tensor_scalar(neg_a[:], neg_a[:], -1.0, None, ALU.mult).then_inc(s["setup_v"], 1)
            v.tensor_tensor(turn[:, 0:FT], trig[:, FT:2 * FT], w_re[:], ALU.mult).then_inc(s["setup_v"], 1)
            v.tensor_tensor(turn[:, FT:2 * FT], trig[:, 0:FT], w_im[:], ALU.mult).then_inc(s["setup_v"], 1)
            v.wait_ge(s["setup_v"], 8)
            v.tensor_tensor(turn[:, 0:FT], turn[:, 0:FT], turn[:, FT:2 * FT], ALU.add).then_inc(s["setup_v"], 1)
            v.wait_ge(s["setup_v"], 9)
            v.scalar_tensor_tensor(coef[:], turn[:, 0:FT], 0.1, w_im[:], ALU.mult, ALU.mult).then_inc(s["setup_v"], 1)
            v.wait_ge(s["setup_v"], 10)
            v.wait_ge(s["setup_p"], 2)
            v.tensor_copy(R[L:P, :, L:P], ident[L:P, L:P].unsqueeze(1).to_broadcast([TOK, H, TOK]))

            def start(b):
                v.wait_ge(s["ab_ps"], b + 1)
                v.wait_ge(s["eb_a"], 3 * b + 1)
                ab = bank[7][0:TOK, 0:CH * 4 * H].rearrange("m (c k) -> m c k", k=4 * H)
                v.tensor_tensor(zdec[:], ab[:, :, 0:H], dt_b[:].unsqueeze(1).to_broadcast([TOK, CH, H]), ALU.add).then_inc(s["zdec_v"], 1)
                v.wait_ge(s["zdec_v"], 2 * b + 1)
                v.scalar_tensor_tensor(zabs[:], zdec[:], -1.0, zdec[:], ALU.mult, ALU.max).then_inc(s["zdec_v"], 1)
                v.tensor_scalar(beta[:], beta[:], 1.0, 0.5, ALU.add, ALU.mult).then_inc(s["ab_used"], 1)
                v.wait_ge(s["ab_used"], b + 1)
                v.reciprocal(beta[:], beta[:]).then_inc(s["beta_v"], 1)

            def decay_in(b):
                v.wait_ge(s["eb_a"], 3 * b + 3)
                v.scalar_tensor_tensor(gdec[:], zdec[:], 0.0, zabs[:], ALU.max, ALU.add).then_inc(s["beta_v"], 1)
                v.wait_ge(s["beta_v"], 2 * b + 2)
                v.tensor_tensor(gdec[:], gdec[:], neg_a[:].unsqueeze(1).to_broadcast([TOK, CH, H]), ALU.mult).then_inc(s["gate_v"], 1)

                v.memset(raw_all[:, :, :, 0:CONV - 1].rearrange("p a h t -> p (a h) t"), 0.0).then_inc(s["pad_v"], 1)

            def part(b, n, mid=None):
                v.wait_ge(s["raw_a"], PARTS * BANKS * b + BANKS * n + BANKS)
                v.wait_ge(s["pad_v"], b + 1)
                e, mine, taps = n % 2, H - POOL_TILES, CONV - 1
                for i in range(taps):
                    for j in range(mine):
                        tile = n * H + j
                        o, w = co[:, tile, :], conv_w[:, tile, i:i + 1]
                        if i > 0:
                            v.wait_ge(s["tap_v"], taps * mine * ((PARTS - 1) * b + n) + mine * (i - 1) + j + 1)
                        v.scalar_tensor_tensor(o, raw[e][:, j, i:i + T], w, o, ALU.mult, ALU.add).then_inc(s["tap_v"], 1)
                    if mid and i == 0:
                        mid()
                v.wait_ge(s["tap_v"], taps * mine * ((PARTS - 1) * b + n + 1))
                v.tensor_copy(ms[:, 0:1], ones[:, 0:1]).then_inc(s["conv_v"], 1)

            def decays(b):
                v.wait_ge(s["norm_ps"], (CH + 1) * b + 1)
                v.tensor_copy(beta_s[:], bank[1][0:L, 0:CH * H]).then_inc(s["beta_s_v"], 1)

            def finish(b):
                v.wait_ge(s["add_p"], ADDS * (PARTS - 1) * (b + 1))
                for x in X:
                    v.tensor_copy(x[L:P, :, L:P], ident[L:P, L:P].unsqueeze(1).to_broadcast([TOK, H, TOK]))
                for g in range(2):
                    v.memset(S[:, G * g:G * g + G, :], 0.0).then_inc(s["S_v"], 1)

                v.wait_ge(s["eseg_ps"], 4 * b + 4)
                v.tensor_copy(R[0:TOK, :, L:P], ident[0:TOK, L:P].unsqueeze(1).to_broadcast([TOK, H, TOK]))

            def chunks(b):
                def roots_in(m, par):
                    cs = bass.ds(m * H, H)
                    k = 4 * (CH * b + m)
                    at = 2 * P
                    v.wait_ge(s["norm_ps"], (CH + 1) * b + m + 2)
                    v.tensor_scalar(rs_x[0:L, 0:H], bank[5][0:L, at:at + H], 1e-6, None, ALU.add).then_inc(s["norm_v"], 1)
                    v.tensor_scalar(epsq[par][:], bank[5][:, at + H:at + H + 2], DH * LN_EPS, DH * LN_EPS * 1e-6, ALU.mult, ALU.add)
                    v.wait_ge(s["norm_v"], k + 1)
                    v.reciprocal(inv[:], rs_x[0:L, 0:H]).then_inc(s["norm_v"], 1)
                    v.wait_ge(s["norm_v"], k + 2)
                    v.scalar_tensor_tensor(bneg[par][:], inv[:], -1.0, beta_s[:, cs], ALU.mult, ALU.mult).then_inc(s["norm_v"], 1)
                    v.wait_ge(s["norm_v"], k + 3)
                    v.tensor_tensor(kend[par][:], bneg[par][:], e_out[:, cs], ALU.mult).then_inc(s["norm_v"], 1)

                def key_norms(par):
                    v.tensor_tensor(vnorm[par][:], rs_x[0:L, 0:H], rs_y[0:L, 0:H], ALU.mult).then_inc(s["vnorm_v"], 1)

                def n_and_weights(m, par, g):
                    itm = CH * b + m
                    v.wait_ge(s["dd_p"], 2 * itm + 2)
                    v.wait_ge(s["p1_ps"], 2 * itm + g + 1)
                    for j in range(G):
                        h = G * g + j
                        ins = v.scalar_tensor_tensor(X[par][0:L, h, :], bank[2 * g][0:L, P * j:P * j + P], bneg[par][:, h:h + 1], DD[:, h, :],
                                                     ALU.mult, ALU.mult)
                    ins.then_inc(s["x_v"], 1)
                    v.wait_ge(s["x_v"], 2 * itm + g + 1)
                    v.tensor_copy(Nh[0][:, G * g:G * g + G, :], X[par][0:L, G * g:G * g + G, 0:L]).then_inc(s["nh_v"], 1)

                def step(c, par, state=True, inverse=True, stage=True, last=False):
                    n, m = c + 1, c + 2
                    it, itn = CH * b + c, CH * b + n
                    at = RS * ((CH + 2) * b + c + 2)
                    roots = rs_x[:], rs_y[:], rs_t[:], s["rs_c_v"], at

                    def wn(g):
                        v.wait_ge(s["st_ps"], 2 * it + g + 1)
                        v.wait_ge(s["vn_a"], 2 * it + g + 1)
                        for j in range(G):
                            h = G * g + j
                            ins = v.scalar_tensor_tensor(Wn[:, h, :], bank[6 + g][:, P * j:P * j + P], e_in[:, 0, bass.ds(c * H + h, 1)], Vn[:, h, :],
                                                         ALU.mult, ALU.subtract)
                        ins.then_inc(s["wn_v"], 1)

                    def new_state(g):
                        v.wait_ge(s["su_ps"], 2 * ((CH - 1) * b + c) + g + 1)
                        for j in range(G):
                            h = G * g + j
                            ins = v.scalar_tensor_tensor(S[:, h, :], S[:, h, :], e_in[:, 1, bass.ds(c * H + h, 1)], bank[6 + g][:, P * j:P * j + P],
                                                         ALU.mult, ALU.add)
                        ins.then_inc(s["S_v"], 1)

                    def level(lv, g):
                        hs = slice(G * g, G * g + G)
                        v.wait_ge(s["rr_ps"], NL * itn + 2 * (lv - 1) + g + 1)
                        dst = Rh[lv % 2] if lv < LEVELS else R0
                        v.tensor_tensor(dst[:, hs, :], bank[4][0:L, 0:G * L].rearrange("r (h s) -> r h s", s=L),
                                        Rh[(lv - 1) % 2][:, hs, :], ALU.add).then_inc(s["r_v"], 1)

                    if state:
                        wn(0)
                        wn(1)
                    if inverse:
                        level(1, 0)
                        level(1, 1)
                    for g in range(2):
                        if state and not last:
                            new_state(g)
                        if inverse:
                            level(2, g)
                    if state:
                        v.wait_ge(s["so_a"], 2 * it + 2)
                        v.scalar_tensor_tensor(rs_x[:, H:H + 2], so[:], 1.0 / DH, epsq[par][:], ALU.mult, ALU.add).then_inc(s["rs_in_v"], 1)
                        v.wait_ge(s["rs_in_v"], it + 1)
                    if last:
                        v.wait_ge(s["vx_ps"], b + 1)
                        v.tensor_tensor(vx, bank[4][0:SK, 0:D], xbv[0:SK, :], ALU.add).then_inc(s["vx_v"], 1)
                    if stage:
                        roots_in(m, par)
                    rsqrt(*roots, range(0, 3))
                    if inverse:
                        level(3, 0)
                    rsqrt(*roots, range(3, 6))
                    if inverse:
                        level(3, 1)
                    rsqrt(*roots, range(6, 9))
                    if inverse:
                        for g in range(2):
                            hs = slice(G * g, G * g + G)
                            level(4, g)
                            v.wait_ge(s["kt_ps"], 2 * itn + g + 1)
                            v.tensor_tensor(Ks[:, hs, :], bank[6 + g][0:L, :].rearrange("r (h d) -> r h d", d=P),
                                            kend[1 - par][:, hs].unsqueeze(2).to_broadcast([L, G, P]), ALU.mult).then_inc(s["ks_v"], 1)
                    rsqrt(*roots, range(9, RS))
                    if state:
                        v.tensor_copy(rstd[:], rs_y[:, H:H + 2]).then_inc(s["rstd_v"], 1)
                    if stage:
                        key_norms(par)
                    if inverse:
                        level(5, 0)
                        level(5, 1)
                        if stage:
                            n_and_weights(m, par, 0)
                        level(6, 0)
                        level(6, 1)
                        if stage:
                            n_and_weights(m, par, 1)
                        for g in range(2):
                            hs = slice(G * g, G * g + G)
                            v.wait_ge(s["ar_ps"], 2 * itn + g + 1)
                            v.tensor_tensor(Er[:, hs, :], bank[2 * g + 1][0:L, 0:G * L].rearrange("r (h s) -> r h s", s=L), R0[:, hs, :],
                                            ALU.subtract).then_inc(s["er_v"], 1)
                    if state:
                        v.wait_ge(s["ot_ps"], it + 1)
                        tk = bass.ds(c * TOK, TOK)
                        v.scalar_tensor_tensor(oT[:, :, tk], bank[5][:, 0:2 * P].rearrange("p (h t) -> p h t", t=TOK), rms_w[:], gate[:, :, tk],
                                               ALU.mult, ALU.mult).then_inc(s["oT_v"], 1)
                    if inverse:
                        for g in range(2):
                            hs = slice(G * g, G * g + G)
                            v.wait_ge(s["re_ps"], 2 * itn + g + 1)
                            v.tensor_tensor(R[0:L, hs, 0:L], bank[2 * g + 1][0:L, 0:G * L].rearrange("r (h s) -> r h s", s=L), R0[:, hs, :],
                                            ALU.add).then_inc(s["rf_v"], 1)

                v.wait_ge(s["gsum_a"], 2 * b + 2)
                v.wait_ge(s["beta_s_v"], b + 1)
                roots_in(0, 0)
                rsqrt(rs_x[:], rs_y[:], rs_t[:], s["rs_c_v"], RS * (CH + 2) * b)
                key_norms(0)
                n_and_weights(0, 0, 0)
                n_and_weights(0, 0, 1)
                step(-1, 1, state=False)
                with v.Fori(0, CH // 2 - 1) as cc:
                    step(2 * cc, 0)
                    step(2 * cc + 1, 1)
                step(CH - 2, 0, stage=False)
                step(CH - 1, 1, inverse=False, stage=False, last=True)

            def layer_norm(b, k, psum, skip, dst, done, ready, skip_ready=None):
                n = 3 * b + k
                for t in range(TT):
                    if skip_ready:
                        v.wait_ge(skip_ready, TT * b + t + 1)
                    v.wait_ge(ready[0], ready[1] + t)
                    v.tensor_tensor(yln[:, t, :], psum[t], skip[:, t, :], ALU.add).then_inc(s["yln_v"], 1)
                for t in range(TT):
                    v.wait_ge(s["yln_v"], TT * n + t + 1)
                    v.bn_stats(bst[:, t, :], yln[:, t, :]).then_inc(s["bst_v"], 1)
                v.wait_ge(s["bst_v"], TT * n + TT)
                v.tensor_copy(ms[:], ones[:, 0:2])
                for t in range(TT):
                    v.bn_aggr(mv[:, t, :], bst[:, t, :]).then_inc(s["mv_v"], 1)
                v.wait_ge(s["mv_v"], TT * n + TT)
                v.tensor_scalar(lnr[:], mv[:, :, 1], LN_EPS, None, ALU.add).then_inc(s["ve_v"], 1)
                v.wait_ge(s["ve_v"], n + 1)
                rsqrt(lnr[:], rs_y[:, 0:TT], rs_t[:, 0:TT], s["rs_l_v"], RS * n)
                for t in range(TT):
                    v.tensor_scalar(dst[:, t, :], yln[:, t, :], mv[:, t, 0:1], rs_y[:, t:t + 1], ALU.subtract, ALU.mult).then_inc(done, 1)

            def tail_out(b):
                v.wait_ge(s["res_in"], 16 * b + 16)
                layer_norm(b, 0, [bank[t][:, 0:D] for t in range(TT)], x_tok, x1, s["x1_v"], (s["ao_ps"], 2 * b + 1))

            def tail_scores(b):
                for t in range(TT):
                    v.wait_ge(s["qk_a"], 8 * b + XG * (t + 1))
                    v.tensor_reduce(stat[:, 0, half(t)], qk[:, half(t), :], AX.X, ALU.max).then_inc(s["stat_v"], 1)
                    v.wait_ge(s["stat_v"], 2 * b + t + 1)
                    v.tensor_tensor(qk[:, half(t), :], qk[:, half(t), :], stat[:, 0, half(t)].unsqueeze(2).to_broadcast([P, XH, SK]),
                                    ALU.subtract).then_inc(s["d_v"], 1)
                for t in range(TT):
                    v.wait_ge(s["e1_a"], 2 * b + t + 1)
                    v.tensor_reduce(s_1[:, half(t)], ex[:, half(t), :], AX.X, ALU.add).then_inc(s["s1_v"], 1)
                v.wait_ge(s["s1_v"], 2 * b + 2)
                v.reciprocal(r_1[:], s_1[:]).then_inc(s["r1_v"], 1)
                for t in range(TT):
                    v.wait_ge(s["esq_a"], 2 * b + t + 1)
                    v.tensor_reduce(s_2[:, half(t)], e_sq[:, half(t), :], AX.X, ALU.add).then_inc(s["s2_v"], 1)
                v.wait_ge(s["s2_v"], 2 * b + 2)
                v.wait_ge(s["r1_v"], b + 1)
                v.tensor_tensor(s_2[:], s_2[:], r_1[:], ALU.mult).then_inc(s["var_v"], 1)
                v.wait_ge(s["var_v"], 3 * b + 1)
                v.tensor_tensor(s_2[:], s_2[:], r_1[:], ALU.mult).then_inc(s["var_v"], 1)
                v.wait_ge(s["var_v"], 3 * b + 2)
                v.tensor_scalar(stat[:, 1, :], s_2[:], 1.0 / SK, 1.0 / (SK - 1), ALU.subtract, ALU.mult).then_inc(s["var_v"], 1)

            def tail_net(b):
                v.wait_ge(s["h3_ps"], b + 1)
                v.tensor_scalar(lt[:], bank[2][:, 0:XH], tb3[:], LOG_T_MAX, ALU.add, ALU.min).then_inc(s["lt_v"], 1)
                v.wait_ge(s["lt_v"], 2 * b + 1)
                v.tensor_scalar(lt[:], lt[:], LOG_T_MIN, None, ALU.max).then_inc(s["lt_v"], 1)

            def tail_weights(b):
                v.wait_ge(s["it_a"], b + 1)
                v.tensor_scalar(inv_t[:], inv_t[:], 0.5, None, ALU.mult).then_inc(s["it_v"], 1)
                v.wait_ge(s["it_v"], b + 1)
                for t in range(TT):
                    v.tensor_tensor(qk[:, half(t), :], qk[:, half(t), :], inv_t[:].unsqueeze(2).to_broadcast([P, XH, SK]), ALU.mult).then_inc(s["d2_v"], 1)
                for t in range(TT):
                    v.wait_ge(s["e2_a"], 2 * b + t + 1)
                    v.tensor_reduce(s_1[:, half(t)], ex[:, half(t), :], AX.X, ALU.add).then_inc(s["se_v"], 1)
                v.wait_ge(s["se_v"], 2 * b + 2)
                v.reciprocal(r_1[:], s_1[:]).then_inc(s["rinv_v"], 1)
                v.wait_ge(s["rinv_v"], 2 * b + 1)
                v.tensor_scalar(r_1[:], r_1[:], 0.0, None, ALU.max).then_inc(s["rinv_v"], 1)
                for q in range(8):
                    v.wait_ge(s["eT_ps"], 8 * b + q + 1)
                    v.tensor_scalar(exT[:, XG * q:XG * q + XG, :].rearrange("k r q -> k (r q)"), bank[q % 4][0:SK, :], 0.0, None, ALU.max).then_inc(s["eT_v"], 1)

            def tail_values(b):
                v.wait_ge(s["rinv_v"], 2 * b + 2)
                for t in range(TT):
                    v.wait_ge(s["av_ps"], 2 * b + t + 1)
                    v.tensor_tensor(ao[:, t, :].rearrange("p (h d) -> p h d", d=DK), bank[t][:, 0:D].rearrange("p (h d) -> p h d", d=DK),
                                    r_1[:, XH * t:XH * t + XH].unsqueeze(2).to_broadcast([P, XH, DK]), ALU.mult).then_inc(s["ao_v"], 1)

            def tail_norm(b):
                layer_norm(b, 1, [bank[t][:, 0:D] for t in range(TT)], x1b, x2, s["x2_v"], (s["x2_ps"], 2 * b + 1), s["x1b_p"])

            def tail_ffn(b):
                def activate(q):
                    v.wait_ge(s["sin_a"], 4 * b + q + 1)
                    for f in (2 * q, 2 * q + 1):
                        v.scalar_tensor_tensor(hid[:, f, :], rnd[:, f, :], coef[:, f:f + 1], hid[:, f, :], ALU.mult, ALU.add).then_inc(s["q_v"], 1)
                    v.wait_ge(s["q_v"], FT * b + 2 * q + 2)
                    v.tensor_scalar(arg[:, 2 * q:2 * q + 2, :], hid[:, 2 * q:2 * q + 2, :], 0.0, None, ALU.max).then_inc(s["act_v"], 1)

                for q in range(4):
                    v.wait_ge(s["hid_a"], 4 * b + q + 1)
                    for f in (2 * q, 2 * q + 1):
                        v.tensor_scalar(arg[:, f, :], hid[:, f, :], 0.1, theta[:, f:f + 1], ALU.mult, ALU.add).then_inc(s["arg_v"], 1)
                    v.wait_ge(s["arg_v"], FT * b + 2 * q + 2)
                    turns_off(arg[:, 2 * q:2 * q + 2, :], rnd[:, 2 * q:2 * q + 2, :], s["rnd_v"], 16 * b + 4 * q)
                    if q > 0:
                        activate(q - 1)
                activate(3)
                v.wait_ge(s["stored"], 16 * b + 16)
                layer_norm(b, 2, [bank[k][:, 0:D] for k in (2, 0)], x2b, x3, s["x3_v"], (s["x3_ps"], 2 * b + 1), s["x2b_p"])

            def between(b, more):
                if not more:
                    tail_out(b)
                    tail_scores(b)
                    tail_net(b)
                    tail_weights(b)
                    tail_values(b)
                    tail_norm(b)
                    tail_ffn(b)
                    return
                start(b + 1)
                tail_out(b)
                decay_in(b + 1)
                part(b + 1, 0)
                part(b + 1, 1)
                tail_scores(b)
                part(b + 1, 2, mid=lambda: tail_net(b))
                tail_weights(b)
                part(b + 1, 3)
                part(b + 1, 4)
                part(b + 1, 5)
                tail_values(b)
                tail_norm(b)
                part(b + 1, 6)
                decays(b + 1)
                finish(b + 1)
                tail_ffn(b)

            start(0)
            decay_in(0)
            for n in range(EARLY):
                part(0, n)
            decays(0)
            finish(0)
            with v.Fori(0, BATCHES - 1) as b:
                chunks(b)
                between(b, True)
            chunks(BATCHES - 1)
            between(BATCHES - 1, False)


def rows_to_tiles(w):
    return w.reshape(w.shape[0] // P, P, w.shape[1]).transpose(1, 0, 2)


def padded_heads(w):
    o = np.zeros((w.shape[0], XG, XG, 32), np.float32)
    o[..., :DK] = w.reshape(w.shape[0], XG, XG, DK).transpose(0, 2, 1, 3)
    return o.reshape(w.shape[0], XH * 32)


def lay_out(i):
    f = {k: np.asarray(v, np.float32) if np.asarray(v).dtype == np.float32 else np.asarray(v) for k, v in i.items()}
    d, x, n = "L0_attn_", "L0_xattn_", "L0_ffn_"
    k, v = f[d + "Wk"], f[d + "Wv"]
    parts = [f[d + "Wq"]] + [w[:, H * DH * j:H * DH * (j + 1)] for w in (k, v) for j in range(NHH)] + [f[d + "Wg"]]
    taps = np.concatenate([f[d + "conv_q"], f[d + "conv_k"], f[d + "conv_v"]])
    cols = lambda u: u.reshape(-1, P).T
    a = {
        "x": f["x"], "ctx": f["ctx_1024"],
        "w_parts": np.stack([rows_to_tiles(w) for w in parts] + [
            rows_to_tiles(f[n + "W1"]), rows_to_tiles(f[n + "W2"]).reshape(P, KC, H * DH)]),
        "conv_w": taps.reshape(-1, P, CONV).transpose(1, 0, 2),
        "w_ab": rows_to_tiles(np.concatenate([f[d + "Wa"], f[d + "Wb"]], 1)),
        "w_o": rows_to_tiles(f[d + "Wo"]), "rms_w": f[d + "rms_weight"][:, None],
        "A_log": f[d + "A_log"], "dt_bias": f[d + "dt_bias"],
        "xwq": rows_to_tiles(padded_heads(f[x + "Wq"].T)), "xwk": rows_to_tiles(padded_heads(f[x + "Wk"].T)),
        "xbq": cols(padded_heads(f[x + "bq"][None])[0]), "xbk": cols(padded_heads(f[x + "bk"][None])[0]),
        "xwv": rows_to_tiles(f[x + "Wv"].T), "xwo": rows_to_tiles(f[x + "Wo"].T),
        "xbv": f[x + "bv"], "xbo": f[x + "bo"], "fb2": f[n + "b2"],
        "tw1": f[x + "w1"].T, "tb1": f[x + "b1"][:, None], "tw2": np.pad(f[x + "w2"].T, ((0, 0), (0, P - 64))), "tb2": f[x + "b2"][:, None],
        "tw3": f[x + "w3"].T, "tb3": f[x + "b3"],
        "fb1": cols(f[n + "b1"]),
        "theta": cols(f[n + "quantum_phases"]), "w_re": cols(f[n + "quantum_weights_real"]),
        "w_im": cols(f[n + "quantum_weights_imag"]),
    }
    a |= {"c_" + key: w for key, w in shape_constants().items()}
    return {key: np.ascontiguousarray(w) for key, w in a.items()}


def kernel(**inputs):
    import concourse.bacc as bacc
    from concourse.bass_utils import run_bass_kernel_spmd

    nc = bacc.Bacc("TRN2", target_bir_lowering=False, num_devices=1)
    arrays = lay_out(inputs)
    aps = {k: nc.dram_tensor(f"in_{k}", w.shape, mybir.dt.from_np(w.dtype), kind="ExternalInput").ap() for k, w in arrays.items()}
    out = nc.dram_tensor("out_x", (BATCHES, T, D), F32, kind="ExternalOutput").ap()
    build(nc, aps, out)
    r = run_bass_kernel_spmd(nc, [{f"in_{k}": w for k, w in arrays.items()}], core_ids=[0])
    return r.results[0]["out_x"]
```
